# Optimizing a Trainium2 kernel written in Bass

```python
import numpy as np
import jax
import jax.numpy as jnp

def _softmax(x, axis=-1):
    return jax.nn.softmax(x, axis=axis)

def _gelu(x):
    return jax.nn.gelu(x, approximate=True)

def _silu(x):
    return jax.nn.silu(x)

def _sigmoid(x):
    return jax.nn.sigmoid(x)

def _layernorm(x, axis=-1, eps=1e-05):
    m = jnp.mean(x, axis=axis, keepdims=True)
    v = jnp.var(x, axis=axis, keepdims=True)
    return (x - m) / jnp.sqrt(v + eps)

def _scatter_add(tgt, idx, src, axis=0):
    return tgt.at[idx].add(src)

def _segment_sum(src, seg, n):
    return jax.ops.segment_sum(src, seg, n)
kernel_name = 'mk_gps_d1_gnn_r8_819f4f'

def setup_inputs(seed: int=0):
    np.random.seed(seed)
    _w = jnp.asarray

    def _rec_inputs():
        import jax
        import jax.numpy as jnp
        _gk = jax.random.key(seed)
        x = -0.0003713 + 1 * jax.random.normal(jax.random.fold_in(_gk, 1), (6250, 256), jnp.float32)
        src = jax.random.randint(jax.random.fold_in(_gk, 2), (100000,), 0, 6250, jnp.int32)
        dst = jnp.minimum((6250 * jax.random.uniform(jax.random.fold_in(_gk, 3), (100000,)) ** 2.0).astype(jnp.int32), 49999)
        _o = jnp.argsort(dst, stable=True)
        src = src[_o]
        dst = dst[_o]
        return (x, src, dst)
    x, src, dst = _rec_inputs()

    def _L0_gnn_setup():
        import jax, jax.numpy as jnp
        import numpy as np
        EMBED = 256
        HEADS = 8
        DK = 32
        DV = 32
        N_NODES = 6250
        N_EDGES = 100000
        LN_EPS = 1e-05
        key = jax.random.key(seed)
        ks = jax.random.split(key, 9)
        h = jax.random.normal(ks[0], (N_NODES, EMBED), dtype=jnp.float32)
        edge_src = jax.random.randint(ks[1], (N_EDGES,), 0, N_NODES)
        edge_dst = jax.random.randint(ks[2], (N_EDGES,), 0, N_NODES)
        s = 1.0 / np.sqrt(EMBED)
        Wq = jax.random.normal(ks[3], (EMBED, HEADS * DK), dtype=jnp.float32) * s
        Wk = jax.random.normal(ks[4], (EMBED, HEADS * DK), dtype=jnp.float32) * s
        Wv = jax.random.normal(ks[5], (EMBED, HEADS * DV), dtype=jnp.float32) * s
        Wo = jax.random.normal(ks[6], (HEADS * DV, EMBED), dtype=jnp.float32) * (1.0 / np.sqrt(HEADS * DV))
        gamma = jnp.ones((EMBED,), dtype=jnp.float32)
        beta = jnp.zeros((EMBED,), dtype=jnp.float32)
        return {'h': h, 'Wq': Wq, 'Wk': Wk, 'Wv': Wv, 'Wo': Wo, 'gamma': gamma, 'beta': beta, 'edge_src': edge_src, 'edge_dst': edge_dst}
    _L0_gnn_all = _L0_gnn_setup()
    _L0_gnn_in = {k: v for k, v in _L0_gnn_all.items() if k in ('Wq', 'Wk', 'Wv', 'Wo', 'gamma', 'beta')}
    del _L0_gnn_all

    def _L0_mix_setup():
        import jax, jax.numpy as jnp
        import numpy as np
        HEADS = 8
        DIM_HEAD = 32
        SCALE = DIM_HEAD ** (-0.5)
        EPS = 1e-05

        def _layernorm_gamma(x, gamma):
            mu = jnp.mean(x, axis=-1, keepdims=True)
            var = jnp.var(x, axis=-1, keepdims=True)
            return (x - mu) * jax.lax.rsqrt(var + EPS) * gamma
        key = jax.random.key(seed)
        k1, k2, k3 = jax.random.split(key, 3)
        B, N, D = (8, 2048, 256)
        hidden = HEADS * DIM_HEAD
        x = jax.random.normal(k1, (B, N, D), dtype=jnp.float32)
        Wqkv = jax.random.normal(k2, (D, 3 * hidden), dtype=jnp.float32) * D ** (-0.5)
        Wout = jax.random.normal(k3, (hidden, D), dtype=jnp.float32) * hidden ** (-0.5)
        gamma = jnp.ones((D,), dtype=jnp.float32)
        return {'x': x, 'Wqkv': Wqkv, 'Wout': Wout, 'gamma': gamma}
    _L0_mix_all = _L0_mix_setup()
    _L0_mix_in = {k: v for k, v in _L0_mix_all.items() if k in ('Wqkv', 'Wout', 'gamma')}
    del _L0_mix_all

    def _L0_ffn_setup():
        import jax, jax.numpy as jnp
        import numpy as np
        B, S, D = (8, 512, 256)
        H = 4 * D
        CAPACITY = 0.5
        key = jax.random.key(seed)
        ks = jax.random.split(key, 6)
        x = jax.random.normal(ks[0], (B, S, D), dtype=jnp.float32)
        attention_mask = jnp.zeros((B, 1, 1, S), dtype=jnp.float32)
        wr = jax.random.normal(ks[1], (D, 1), dtype=jnp.float32) * 0.02
        br = jnp.zeros((1,), dtype=jnp.float32)
        w1 = jax.random.normal(ks[2], (D, H), dtype=jnp.float32) * 0.02
        b1 = jnp.zeros((H,), dtype=jnp.float32)
        w2 = jax.random.normal(ks[3], (H, D), dtype=jnp.float32) * 0.02
        b2 = jnp.zeros((D,), dtype=jnp.float32)
        return {'x': x, 'attention_mask': attention_mask, 'wr': wr, 'br': br, 'w1': w1, 'b1': b1, 'w2': w2, 'b2': b2}
    _L0_ffn_all = _L0_ffn_setup()
    _L0_ffn_in = {k: v for k, v in _L0_ffn_all.items() if k in ('attention_mask', 'wr', 'br', 'w1', 'b1', 'w2', 'b2')}
    del _L0_ffn_all
    return {'x': x, 'src': src, 'dst': dst, 'L0_gnn_Wq': _L0_gnn_in['Wq'], 'L0_gnn_Wk': _L0_gnn_in['Wk'], 'L0_gnn_Wv': _L0_gnn_in['Wv'], 'L0_gnn_Wo': _L0_gnn_in['Wo'], 'L0_gnn_gamma': _L0_gnn_in['gamma'], 'L0_gnn_beta': _L0_gnn_in['beta'], 'L0_mix_Wqkv': _L0_mix_in['Wqkv'], 'L0_mix_Wout': _L0_mix_in['Wout'], 'L0_mix_gamma': _L0_mix_in['gamma'], 'L0_ffn_attention_mask': _L0_ffn_in['attention_mask'], 'L0_ffn_wr': _L0_ffn_in['wr'], 'L0_ffn_br': _L0_ffn_in['br'], 'L0_ffn_w1': _L0_ffn_in['w1'], 'L0_ffn_b1': _L0_ffn_in['b1'], 'L0_ffn_w2': _L0_ffn_in['w2'], 'L0_ffn_b2': _L0_ffn_in['b2']}

def reference(x, src, dst, L0_gnn_Wq, L0_gnn_Wk, L0_gnn_Wv, L0_gnn_Wo, L0_gnn_gamma, L0_gnn_beta, L0_mix_Wqkv, L0_mix_Wout, L0_mix_gamma, L0_ffn_attention_mask, L0_ffn_wr, L0_ffn_br, L0_ffn_w1, L0_ffn_b1, L0_ffn_w2, L0_ffn_b2):
    import jax
    import jax.numpy as jnp

    def _L0_gnn_ref(h, Wq, Wk, Wv, Wo, gamma, beta, edge_src, edge_dst):
        import jax, jax.numpy as jnp
        import numpy as np
        EMBED = 256
        HEADS = 8
        DK = 32
        DV = 32
        N_NODES = 6250
        N_EDGES = 100000
        LN_EPS = 1e-05
        N = h.shape[0]
        q = (h @ Wq).reshape(N, HEADS, DK)
        k = (h @ Wk).reshape(N, HEADS, DK)
        v = (h @ Wv).reshape(N, HEADS, DV)
        scores = jnp.einsum('ehd,ehd->eh', q[edge_dst], k[edge_src]) / jnp.sqrt(jnp.float32(DK))
        m = jax.ops.segment_max(scores, edge_dst, num_segments=N)
        ex = jnp.exp(scores - m[edge_dst])
        denom = jax.ops.segment_sum(ex, edge_dst, num_segments=N)
        agg = jax.ops.segment_sum(ex[:, :, None] * v[edge_src], edge_dst, num_segments=N)
        attn_out = agg / (denom[:, :, None] + 1e-09)
        o = attn_out.reshape(N, HEADS * DV) @ Wo
        y = o + h
        mu = jnp.mean(y, axis=-1, keepdims=True)
        var = jnp.mean(jnp.square(y - mu), axis=-1, keepdims=True)
        return (y - mu) * jax.lax.rsqrt(var + LN_EPS) * gamma + beta

    def _L0_mix_ref(x, Wqkv, Wout, gamma):
        import jax, jax.numpy as jnp
        import numpy as np
        HEADS = 8
        DIM_HEAD = 32
        SCALE = DIM_HEAD ** (-0.5)
        EPS = 1e-05

        def _layernorm_gamma(x, gamma):
            mu = jnp.mean(x, axis=-1, keepdims=True)
            var = jnp.var(x, axis=-1, keepdims=True)
            return (x - mu) * jax.lax.rsqrt(var + EPS) * gamma
        B, N, D = x.shape
        qkv = x @ Wqkv
        q, k, v = jnp.split(qkv, 3, axis=-1)

        def to_heads(t):
            return t.reshape(B, N, HEADS, DIM_HEAD).transpose(0, 2, 1, 3)
        q, k, v = map(to_heads, (q, k, v))
        q = jax.nn.softmax(q, axis=-1) * SCALE
        k = jax.nn.softmax(k, axis=2)
        context = jnp.einsum('bhnd,bhne->bhde', k, v)
        out = jnp.einsum('bhde,bhnd->bhne', context, q)
        out = out.transpose(0, 2, 1, 3).reshape(B, N, HEADS * DIM_HEAD)
        out = out @ Wout
        return _layernorm_gamma(out, gamma)

    def _L0_ffn_ref(x, attention_mask, wr, br, w1, b1, w2, b2):
        import jax, jax.numpy as jnp
        import numpy as np
        B, S, D = (8, 512, 256)
        H = 4 * D
        CAPACITY = 0.5
        b, s, d = x.shape
        weights = (jnp.einsum('bsd,do->bso', x, wr) + br)[..., 0]
        k = max(1, int(CAPACITY * s))
        kk = k - 1 if k > 1 else 1
        _, idx = jax.lax.top_k(weights, k)
        sel_idx = idx[:, :kk]
        sel = jnp.take_along_axis(x, sel_idx[:, :, None], axis=1)
        h = jax.nn.gelu(jnp.einsum('bkd,dh->bkh', sel, w1) + b1)
        y = jnp.einsum('bkh,hd->bkd', h, w2) + b2
        w_sel = jnp.take_along_axis(weights, sel_idx, axis=1)
        y = y * w_sel[..., None]
        batch_idx = jnp.arange(b)[:, None]
        processed = jnp.zeros_like(x).at[batch_idx, sel_idx].set(y)
        return processed + x
    xn = _layernorm(x, axis=-1)
    x = x + _L0_gnn_ref(xn, L0_gnn_Wq, L0_gnn_Wk, L0_gnn_Wv, L0_gnn_Wo, L0_gnn_gamma, L0_gnn_beta, src, dst) + _L0_mix_ref(xn[None], L0_mix_Wqkv, L0_mix_Wout, L0_mix_gamma)[0]
    x = x + _L0_ffn_ref(_layernorm(x, axis=-1)[None], L0_ffn_attention_mask, L0_ffn_wr, L0_ffn_br, L0_ffn_w1, L0_ffn_b1, L0_ffn_w2, L0_ffn_b2)[0]
    return x

_drawn_inputs = setup_inputs


def setup_inputs(seed=0):
    import zlib

    import numpy as np

    out = dict(_drawn_inputs(seed))
    spreads = {'L0_gnn_gamma': (1.0, 0.2),
     'L0_gnn_beta': (0.0, 0.1),
     'L0_mix_gamma': (1.0, 0.2),
     'L0_ffn_b1': (0.0, 0.8),
     'L0_ffn_b2': (0.0, 0.8)}
    factors = {'L0_ffn_wr': 6.621, 'L0_ffn_w1': 7.162, 'L0_ffn_w2': 6.847}
    for name, (base, spread) in spreads.items():
        noise = np.random.default_rng([zlib.crc32(name.encode()), seed]).standard_normal(out[name].shape)
        drawn = base * np.exp(spread * noise) if base else spread * noise
        out[name] = jnp.asarray(drawn.astype(out[name].dtype))
    for name, factor in factors.items():
        out[name] = (out[name] * factor).astype(out[name].dtype)
    return out
```

```python
from contextlib import ExitStack

import numpy as np
import concourse.bass as bass
from concourse import mybir

F32 = mybir.dt.float32
I32 = mybir.dt.int32
ALU = mybir.AluOpType
ACT = mybir.ActivationFunctionType
AX = mybir.AxisListType.X

P = 128
N, D = 6250, 256
E = 100000
HEADS, DH = 8, 32
FF = 4 * D
NB = -(-N // P)
NLAST = N - (NB - 1) * P
TILES = -(-E // P)
ELAST = E - (TILES - 1) * P
GROUP = 16
STEPS = -(-(TILES + NB - 1) // GROUP) * GROUP
TURNS = STEPS // GROUP
SROWS = -(-STEPS // P)
CHUNKS = P // HEADS
CLEN = STEPS * P // CHUNKS
SCALE = float(DH) ** -0.5
KEEP = max(1, N // 2) - 1
EPS = 1e-5
BIG = 1e30
VW = D + 2
AW = D + HEADS


class Tally:

    def __init__(self, eng, sem):
        self.eng, self.sem, self.base, self.n, self.turn, self.per = eng, sem, 0, 0, None, 0

    def now(self):
        v = self.base + self.n
        return v if self.turn is None else self.turn * self.per + v

    def inc(self, ins):
        ins.then_inc(self.sem, 1)
        self.n += 1

    def wait(self):
        self.eng.wait_ge(self.sem, self.now())

    def link(self, ins):
        self.inc(ins)
        self.wait()

    def enter(self, turn, per):
        self.base, self.n, self.turn, self.per = self.base + self.n, 0, turn, per

    def leave(self, turns):
        assert self.n == self.per, (self.n, self.per)
        self.base, self.n, self.turn = self.base + turns * self.per, 0, None


class Mem:
    pass


def ds(start, size):
    return bass.ds(start, size)


def half_rows(d, i, h):
    return d[:, :].rearrange("h (s e) -> s h e", e=P)[ds((i * 2 + h) * (GROUP // 2), GROUP // 2), :, :]


def setup_phase(nc, m, a):
    X = m.R1[:, 0:NB * D].rearrange("p (b c) -> p b c", b=NB)
    DSTE = m.R2[:, 0:TILES]
    JUNK = m.R2[:, 1024:1024 + TILES]
    CUT = m.R2[:, 2048:2048 + NB]
    CUTI = m.R2[:, 2112:2112 + NB].bitcast(I32)
    CUTF = m.R2[:, 2176:2176 + NB]
    SID = m.R2[:, 2240:2240 + SROWS]
    BF = m.R2[:, 2256:2256 + SROWS]
    TF = m.R2[:, 2272:2272 + SROWS]
    TI = m.R2[:, 2288:2288 + SROWS].bitcast(I32)
    OFF = m.R2[:, 2304:2304 + SROWS]
    BI = m.R2[:, 2320:2320 + SROWS].bitcast(I32)
    DROW = m.R2[:, 2560:2560 + SROWS * P].rearrange("p (r e) -> p r e", r=SROWS)
    SROW = m.R2[:, 3584:3584 + SROWS * P].rearrange("p (r e) -> p r e", r=SROWS)
    KEY = m.R2[:, 4608:4608 + SROWS * P].rearrange("p (r e) -> p r e", r=SROWS)
    RAW = m.R2[:, 5632:5632 + 2 * TILES].bitcast(I32).rearrange("p (s t) -> p s t", s=2)
    DINT = m.R2[:, 7680:7680 + SROWS * P].bitcast(I32).rearrange("p (r e) -> p r e", r=SROWS)
    SINT = m.R2[:, 8704:8704 + SROWS * P].bitcast(I32).rearrange("p (r e) -> p r e", r=SROWS)
    MASK = m.R2[:, 9728:9728 + SROWS * P].rearrange("p (r e) -> p r e", r=SROWS)
    MASK2 = m.R2[:, 10752:10752 + SROWS * P].rearrange("p (r e) -> p r e", r=SROWS)
    PADI = m.R2[:, 11776:11776 + P].bitcast(I32)
    with ExitStack() as ctx:
        sem = lambda n: m.sem(n)
        PT = ctx.enter_context(nc.psum_tensor("PT", [P, 4, 512], F32))
        PC = ctx.enter_context(nc.psum_tensor("PC", [P, 512], F32))
        w_in, x_in, pad_in, e_in, e_raw, rows_in = (sem(n) for n in (
            "w_in", "x_in", "pad_in", "e_in", "e_raw", "rows_in"))
        made, chain, counted, stat_var, stat_std = (sem(n) for n in (
            "const_made", "setup_chain", "counts_summed", "stat_var", "stat_std"))
        tiles_known, table_known, turned, table_out = (sem(n) for n in (
            "tiles_known", "table_known", "table_turned", "table_out"))
        pad_made, x_zeroed = sem("pad_made"), sem("x_zeroed")
        block = ctx.enter_context(nc.Block())

        @block.sync
        def _(sp):
            full = (TILES - 1) * P
            sp.dma_start(m.dst_rows[0:TILES - 1, :], a.dst[0:full].rearrange("(t p) -> t p", p=P)).then_inc(e_in, 16)
            sp.dma_start(m.src_rows[0:TILES - 1, :], a.src[0:full].rearrange("(t p) -> t p", p=P)).then_inc(e_in, 16)
            sp.dma_start(m.dst_rows[TILES - 1, 0:ELAST].rearrange("(o p) -> o p", o=1),
                         a.dst[full:E].rearrange("(o p) -> o p", o=1)).then_inc(e_in, 16)
            sp.dma_start(m.src_rows[TILES - 1, 0:ELAST].rearrange("(o p) -> o p", o=1),
                         a.src[full:E].rearrange("(o p) -> o p", o=1)).then_inc(e_in, 16)
            sp.wait_ge(pad_made, 2)
            sp.dma_start(m.dst_rows[TILES - 1, ELAST:P].rearrange("(o p) -> o p", o=1), PADI[0:1, 0:P - ELAST]).then_inc(e_in, 16)
            sp.dma_start(m.src_rows[TILES - 1, ELAST:P].rearrange("(o p) -> o p", o=1), PADI[1:2, 0:P - ELAST]).then_inc(e_in, 16)
            sp.wait_ge(e_in, 96)
            sp.dma_start(RAW[:, 0, :], m.dst_rows[:, :].rearrange("t p -> (t p)").rearrange("(p t) -> p t", p=P)).then_inc(e_raw, 16)
            h = NB // 2
            sp.dma_start(X[:, 0:h, :], a.x[0:h * P, :].rearrange("(b p) c -> p b c", p=P)).then_inc(x_in, 16)
            sp.dma_start(X[:, h:NB - 1, :], a.x[h * P:(NB - 1) * P, :].rearrange("(b p) c -> p b c", p=P)).then_inc(x_in, 16)
            sp.wait_ge(x_zeroed, 1)
            sp.dma_start(X[0:NLAST, NB - 1, :], a.x[(NB - 1) * P:N, :]).then_inc(x_in, 16)
            sp.wait_ge(table_known, 1)
            for r in range(SROWS):
                n = min(P, STEPS - r * P)
                sp.dma_start(m.rel_rows[r * P:r * P + n, :], DROW[0:n, r, :]).then_inc(table_out, 16)
                sp.dma_start(m.key_rows[r * P:r * P + n, :], KEY[0:n, r, :]).then_inc(table_out, 16)
                sp.dma_start(m.step_block[r * P:r * P + n].rearrange("(p o) -> p o", o=1),
                             BI[0:n, r:r + 1]).then_inc(table_out, 16)
            sp.wait_ge(table_out, 48 * SROWS)
            sp.dma_start(m.BT[:, :], m.step_block[:].rearrange("(o s) -> o s", o=1)).then_inc(table_out, 16)
            sp.wait_ge(table_out, 48 * SROWS + 16)

        @block.gpsimd
        def _(pool):
            nc.gpsimd.memset(PADI[0:2, :], 0).then_inc(pad_made, 1)
            pool.wait_ge(pad_made, 1)
            nc.gpsimd.memset(PADI[0:1, :], NB * P).then_inc(pad_made, 1)
            nc.gpsimd.memset(m.ident[:, :], 0.0).then_inc(made, 1)
            nc.gpsimd.memset(m.ones[:, :], 1.0).then_inc(made, 1)
            nc.gpsimd.memset(m.upper[:, :], 1.0).then_inc(made, 1)
            nc.gpsimd.iota(m.iota_row[:, :], pattern=[[1, P]], base=0, channel_multiplier=0,
                           allow_small_or_imprecise_dtypes=True).then_inc(made, 1)
            nc.gpsimd.iota(m.iota_col[:, :], pattern=[[0, 1]], base=0, channel_multiplier=1,
                           allow_small_or_imprecise_dtypes=True).then_inc(made, 1)
            nc.gpsimd.iota(SID, pattern=[[P, SROWS]], base=0, channel_multiplier=1,
                           allow_small_or_imprecise_dtypes=True).then_inc(made, 1)
            nc.gpsimd.iota(CUTF, pattern=[[1, NB]], base=0, channel_multiplier=0,
                           allow_small_or_imprecise_dtypes=True).then_inc(made, 1)
            pool.wait_ge(made, 7)
            nc.gpsimd.affine_select(out=m.ident[:, :], in_=m.ident[:, :], compare_op=ALU.not_equal, fill=1.0,
                                    base=0, pattern=[[-1, P]], channel_multiplier=1).then_inc(made, 1)
            nc.gpsimd.affine_select(out=m.upper[:, :], in_=m.upper[:, :], compare_op=ALU.is_ge, fill=0.0,
                                    base=0, pattern=[[1, P]], channel_multiplier=-1).then_inc(made, 1)
            pool.wait_ge(tiles_known, 1)
            for r in range(SROWS):
                for k, (out, rows) in enumerate(((DINT, m.dst_rows), (SINT, m.src_rows))):
                    nc.gpsimd.indirect_dma_start(
                        out=out[:, r, :], out_offset=None, in_=rows[:, :],
                        in_offset=bass.IndirectOffsetOnAxis(ap=TI[:, r:r + 1], axis=0)).then_inc(rows_in, 16)

        @block.scalar
        def _(act):
            full = lambda v: v.rearrange("(o c) -> o c", o=1).broadcast_to([P, D])
            for out, src in (
                (m.WP[:, :, 0:256], a.L0_gnn_Wq.rearrange("(k p) n -> p k n", p=P)),
                (m.WP[:, :, 256:512], a.L0_gnn_Wk.rearrange("(k p) n -> p k n", p=P)),
                (m.WP[:, :, 512:768], a.L0_gnn_Wv.rearrange("(k p) n -> p k n", p=P)),
                (m.WP[:, :, 768:1536], a.L0_mix_Wqkv.rearrange("(k p) n -> p k n", p=P)),
                (m.Wo[:, :, :], a.L0_gnn_Wo.rearrange("(k p) n -> p k n", p=P)),
                (m.Wout[:, :, :], a.L0_mix_Wout.rearrange("(k p) n -> p k n", p=P)),
                (m.rows[:, 0, :], full(a.L0_gnn_gamma)), (m.rows[:, 1, :], full(a.L0_gnn_beta)),
                (m.rows[:, 2, :], full(a.L0_mix_gamma)), (m.rows[:, 3, :], full(a.L0_ffn_b2)),
                (m.rows[:, 4, :], a.L0_ffn_wr.rearrange("c o -> o c").broadcast_to([P, D])),
                (m.brc[:, :], a.L0_ffn_br.rearrange("(o c) -> o c", o=1).broadcast_to([P, 1])),
                (m.b1c[:, :], a.L0_ffn_b1.rearrange("(k p) -> p k", p=P)),
            ):
                act.dma_start(out, src, allow_slow_non_contiguous=True).then_inc(w_in, 16)
            act.wait_ge(stat_var, NB + 1)
            nc.scalar.activation(m.rstd[:, :], m.stat[:, :, 1], ACT.Sqrt, bias=m.eps[:, :]).then_inc(stat_std, 1)
            act.wait_ge(w_in, 16 * 13)

        @block.tensor
        def _(pe):
            pe.wait_ge(counted, 1)
            pe.wait_ge(made, 9)
            nc.tensor.matmul(PC[:, 0:NB], m.ones[:, :], CUT, start=True, stop=True).then_inc(counted, 1)
            pe.wait_ge(table_known, 1)
            for q, rows in enumerate((DROW, SROW)):
                for r in range(SROWS):
                    n = min(P, STEPS - r * P)
                    nc.tensor.transpose(PT[:, 2 * q + r // 4, (r % 4) * P:(r % 4) * P + n], rows[0:n, r, :],
                                        m.ident[0:n, 0:n]).then_inc(turned, 1)

        @block.vector
        def _(dve):
            t = Tally(dve, chain)
            nc.vector.memset(m.eps[:, :], EPS).then_inc(stat_var, 1)
            nc.vector.memset(X[:, NB - 1, :], 0.0).then_inc(x_zeroed, 1)
            dve.wait_ge(e_raw, 16)
            t.link(nc.vector.tensor_copy(DSTE, RAW[:, 0, :]))
            for b in range(NB):
                t.link(nc.vector.tensor_scalar(JUNK, DSTE, float(b * P), None, ALU.is_lt, ALU.add,
                                               accum_out=CUT[:, b:b + 1]))
            dve.sem_inc(counted, 1)
            dve.wait_ge(counted, 2)
            dve.wait_ge(made, 9)
            t.link(nc.vector.tensor_copy(CUTI, PC[:, 0:NB]))
            t.link(nc.vector.tensor_scalar(CUTI, CUTI, 7, None, ALU.arith_shift_right))
            t.link(nc.vector.tensor_copy(CUT, CUTI))
            t.link(nc.vector.tensor_tensor(CUT, CUT, CUTF, ALU.add))
            for r in range(SROWS):
                t.link(nc.vector.tensor_scalar(JUNK[:, 0:NB - 1], CUT[:, 1:NB], SID[:, r:r + 1], None, ALU.is_le, ALU.add,
                                               accum_out=BF[:, r:r + 1]))
            t.link(nc.vector.tensor_tensor(TF, SID, BF, ALU.subtract))
            t.link(nc.vector.tensor_scalar(OFF, TF, float(TILES - 1), 4.0 * NB * P, ALU.is_gt, ALU.mult))
            t.link(nc.vector.tensor_scalar(TF, TF, float(TILES - 1), None, ALU.min))
            t.link(nc.vector.tensor_copy(BI, BF))
            t.link(nc.vector.scalar_tensor_tensor(out=OFF, in0=BF, scalar=float(-P), in1=OFF, op0=ALU.mult, op1=ALU.add))
            nc.vector.tensor_copy(TI, TF).then_inc(tiles_known, 1)
            dve.wait_ge(x_in, 48)
            for b in range(NB):
                t.inc(nc.vector.bn_stats(m.bnst[:, b, :], X[:, b, :]))
            t.wait()
            for b in range(NB):
                nc.vector.bn_aggr(m.stat[:, b, :], m.bnst[:, b, :]).then_inc(stat_var, 1)
            dve.wait_ge(rows_in, 32 * SROWS)
            t.inc(nc.vector.tensor_copy(SROW, SINT))
            t.link(nc.vector.tensor_copy(KEY, DINT))
            t.link(nc.vector.tensor_tensor(DROW, KEY, OFF.rearrange("p (r o) -> p r o", o=1).broadcast_to([P, SROWS, P]),
                                           ALU.add))
            t.inc(nc.vector.tensor_scalar(MASK, DROW, 0.0, None, ALU.is_ge))
            t.link(nc.vector.tensor_scalar(MASK2, DROW, float(P), None, ALU.is_lt))
            t.link(nc.vector.tensor_tensor(MASK, MASK, MASK2, ALU.mult))
            t.link(nc.vector.scalar_tensor_tensor(out=KEY, in0=KEY, scalar=1.0, in1=MASK, op0=ALU.add, op1=ALU.mult))
            nc.vector.tensor_scalar(KEY, KEY, -1.0, None, ALU.add).then_inc(table_known, 1)
            dve.wait_ge(turned, 2 * SROWS)
            for q, out in enumerate((m.REL, m.SRC)):
                t.inc(nc.vector.tensor_copy(out[:, 0:512], PT[:, 2 * q, :]))
                t.inc(nc.vector.tensor_copy(out[:, 512:STEPS], PT[:, 2 * q + 1, 0:STEPS - 512]))
            dve.wait_ge(stat_std, 1)
            t.link(nc.vector.reciprocal(m.rstd[:, :], m.rstd[:, :]))


def projection_phase(nc, m, a):
    KM = m.R1[:, 0:NB * D]
    VM = m.R2[:, 0:NB * VW]
    XS = m.slots[:, 0:2 * D].rearrange("p (u c) -> p u c", u=2)
    XN = m.slots[:, 512:512 + 2 * D].rearrange("p (u c) -> p u c", u=2)
    XT = m.slots[:, 1024:1024 + 2 * D].rearrange("p (u k t) -> p u k t", u=2, k=2)
    QKV = m.slots[:, 1536:1536 + 8 * D].rearrange("p (u c) -> p u c", u=2)
    QM = m.slots[:, 3584:3584 + 2 * D].rearrange("p (u c) -> p u c", u=2)
    QR = m.EX[:, 0:32].rearrange("p (u s h) -> p u s h", u=2, s=2)
    with ExitStack() as ctx:
        sem = lambda n: [m.sem(f"{n}{u}") for u in range(2)]
        PX = ctx.enter_context(nc.psum_tensor("PX", [P, 2, 512], F32))
        PP = ctx.enter_context(nc.psum_tensor("PP", [P, 2, 3, 512], F32))
        x_in, xn_made, xn_stored, xn_free = (sem(n) for n in ("px_in", "pxn_made", "pxn_stored", "pxn_free"))
        turned, xt_made, done, act_free = (sem(n) for n in ("p_turned", "p_xt", "p_done", "p_afree"))
        qkv_made, stored, out_free, q_sub, q_exp, q_made = (sem(n) for n in ("p_qkv", "p_st", "p_ofree", "p_qsub", "p_qexp", "p_qmade"))
        zero, chain = m.sem("p_zero"), m.sem("p_chain")
        block = ctx.enter_context(nc.Block())
        last = NB // 2

        def rows(i, u):
            return ds((i * 2 + u) * P, P)

        @block.sync
        def _(sp):
            def load(i, u):
                sp.dma_start(XS[:, u, :], a.x[rows(i, u), :]).then_inc(x_in[u], 16)

            def store(i, u, then=None):
                sp.wait_ge(xn_made[u], i + 1)
                sp.dma_start(m.xn_d[rows(i, u), :], XN[:, u, :]).then_inc(xn_stored[u], 16)
                if then:
                    then()
                sp.wait_ge(xn_stored[u], (i + 1) * 16)
                sp.sem_inc(xn_free[u], 1)
                sp.wait_ge(qkv_made[u], (i + 1) * 2)
                for k, d in enumerate((m.q_d, m.k_d, m.v_d)):
                    sp.dma_start(d[rows(i, u), :], QKV[:, u, k * D:(k + 1) * D]).then_inc(stored[u], 16)
                sp.wait_ge(q_made[u], i + 1)
                sp.dma_start(m.qs_d[rows(i, u), :], QM[:, u, :]).then_inc(stored[u], 16)

            def free(i, u):
                sp.wait_ge(stored[u], (i + 1) * 64)
                sp.sem_inc(out_free[u], 1)
            for u in range(2):
                sp.sem_inc(out_free[u], 1)
                sp.sem_inc(xn_free[u], 1)
            load(0, 0)
            load(0, 1)
            store(0, 0, lambda: load(1, 0))
            store(0, 1, lambda: load(1, 1))
            free(0, 0)
            with sp.Fori(1, last - 1) as i:
                store(i, 0, lambda: load(i + 1, 0))
                free(i - 1, 1)
                store(i, 1, lambda: load(i + 1, 1))
                free(i, 0)
            store(last - 1, 0, lambda: sp.dma_start(XS[0:NLAST, 0, :], a.x[(NB - 1) * P:N, :]).then_inc(x_in[0], 16))
            free(last - 2, 1)
            store(last - 1, 1)
            free(last - 1, 0)
            store(last, 0)
            for u, n in ((0, last + 1), (1, last)):
                sp.wait_ge(stored[u], 64 * n)

        @block.scalar
        def _(act):
            def copy_x(i, u):
                act.wait_ge(turned[u], i + 1)
                nc.scalar.activation(XT[:, u, :, :], PX[:, u, 0:D].rearrange("p (k t) -> p k t", k=2), ACT.Copy).then_inc(xt_made[u], 1)

            def copies(i, u):
                act.wait_ge(done[u], i + 1)
                act.wait_ge(out_free[u], i + 1)
                nc.scalar.activation(QKV[:, u, 0:512], PP[:, u, 0, :], ACT.Copy).then_inc(qkv_made[u], 1)
                nc.scalar.activation(QKV[:, u, 512:1024], PP[:, u, 1, :], ACT.Copy).then_inc(qkv_made[u], 1)
                nc.scalar.activation(KM[:, ds((i * 2 + u) * D, D)], PP[:, u, 2, 0:D], ACT.Copy)
                for k in range(2):
                    ins = nc.scalar.activation(VM[:, ds((i * 2 + u) * VW + k * (P + 1), P)],
                                               PP[:, u, 2, D + k * P:D + k * P + P], ACT.Copy)
                ins.then_inc(act_free[u], 1)
                act.wait_ge(q_sub[u], i + 1)
                nc.scalar.activation(QM[:, u, :], QM[:, u, :], ACT.Exp).then_inc(q_exp[u], 1)

            for u in range(2):
                act.sem_inc(act_free[u], 1)
            copy_x(0, 0)
            with act.Fori(0, last) as i:
                copy_x(i, 1)
                copies(i, 0)
                copy_x(i + 1, 0)
                copies(i, 1)
            copies(last, 0)

        @block.tensor
        def _(pe):
            def turn(i, u):
                pe.wait_ge(xn_made[u], i + 1)
                for k in range(2):
                    ins = nc.tensor.transpose(PX[:, u, k * P:(k + 1) * P], XN[:, u, k * P:(k + 1) * P], m.ident[:, :])
                ins.then_inc(turned[u], 1)

            def project(i, u):
                pe.wait_ge(xt_made[u], i + 1)
                pe.wait_ge(act_free[u], i + 1)
                for c in range(3):
                    for k in range(2):
                        ins = nc.tensor.matmul(PP[:, u, c, :], XT[:, u, k, :], m.WP[:, k, c * 512:(c + 1) * 512],
                                               start=(k == 0), stop=(k == 1))
                ins.then_inc(done[u], 1)

            turn(0, 0)
            with pe.Fori(0, last) as i:
                turn(i, 1)
                project(i, 0)
                turn(i + 1, 0)
                project(i, 1)
            project(last, 0)

        @block.vector
        def _(dve):
            t = Tally(dve, chain)
            head = lambda x: x.rearrange("p (h d) -> p h d", h=HEADS)

            def normalise(i, u, first=False):
                dve.wait_ge(x_in[u], (i + 1) * 16)
                dve.wait_ge(xn_free[u], i + 1)
                if not first:
                    dve.wait_ge(turned[u], i + 0)
                b = i * 2 + u
                nc.vector.tensor_scalar(XN[:, u, :], XS[:, u, :], m.stat[:, ds(b, 1), 0], m.rstd[:, ds(b, 1)],
                                        ALU.subtract, ALU.mult).then_inc(xn_made[u], 1)

            def soft(i, u):
                dve.wait_ge(qkv_made[u], i * 2 + 2)
                q = QKV[:, u, 3 * D:4 * D]
                over = lambda x: x.rearrange("p (h o) -> p h o", o=1).broadcast_to([P, HEADS, DH])
                t.link(nc.vector.tensor_reduce(QR[:, u, 0, :], head(q), AX, ALU.max))
                nc.vector.tensor_tensor(head(QM[:, u, :]), head(q), over(QR[:, u, 0, :]), ALU.subtract).then_inc(q_sub[u], 1)
                dve.wait_ge(q_exp[u], i + 1)
                t.link(nc.vector.tensor_reduce(QR[:, u, 1, :], head(QM[:, u, :]), AX, ALU.add))
                t.link(nc.vector.reciprocal(QR[:, u, 1, :], QR[:, u, 1, :]))
                nc.vector.scalar_tensor_tensor(out=head(QM[:, u, :]), in0=head(QM[:, u, :]), scalar=SCALE,
                                               in1=over(QR[:, u, 1, :]), op0=ALU.mult, op1=ALU.mult).then_inc(q_made[u], 1)

            t.link(nc.vector.memset(VM.rearrange("p (n w) -> p n w", w=P + 1)[:, :, P], 1.0))
            normalise(0, 0, True)
            normalise(0, 1, True)
            with dve.Fori(0, last - 1) as i:
                t.enter(i, 6)
                for u in range(2):
                    normalise(i + 1, u)
                    soft(i, u)
                t.leave(last - 1)
            normalise(last, 0)
            soft(last - 1, 0)
            soft(last - 1, 1)
            soft(last, 0)


def context_phase(nc, m, a):
    KM = m.R1[:, 0:NB * D].rearrange("p (b c) -> p b c", b=NB)
    VM = m.R2[:, 0:NB * VW]
    KX = m.slots[:, 0:2 * D].rearrange("p (u c) -> p u c", u=2)
    TOP = m.slots[:, 512:768]
    TOPT = m.slots[:, 768:776]
    DIAG = m.slots[:, 1024:1280].rearrange("p (k c) -> p k c", k=2)
    TOPB = m.slots[:, 1280:1536]
    CTX = m.slots[:, 1536:1536 + 2 * P].rearrange("p (k c) -> p k c", k=2)
    CTXT = m.slots[:, 1792:1792 + 2 * P].rearrange("p (k c) -> p k c", k=2)
    RDEN = m.slots[:, 2048:2050]
    SAME = m.slots[:, 2176:2176 + P]
    with ExitStack() as ctx:
        sem = lambda n: m.sem(n)
        PA = ctx.enter_context(nc.psum_tensor("PCA", [P, 512], F32))
        PB = ctx.enter_context(nc.psum_tensor("PCB", [P, 512], F32))
        PC0 = ctx.enter_context(nc.psum_tensor("PC0", [P, 512], F32))
        PC1 = ctx.enter_context(nc.psum_tensor("PC1", [P, 512], F32))
        PCC = (PC0, PC1)
        PM = ctx.enter_context(nc.psum_tensor("PCM", [P, 512], F32))
        chain, top_made, top_turned, diag_made, top_spread = (sem(n) for n in ("c_chain", "c_top", "c_topt", "c_diag", "c_topb"))
        ctx_made, ctx_turned, ctxt_made, m_made = (sem(n) for n in ("c_ctx", "c_ctxt", "c_ctxs", "c_m"))
        same = sem("c_same")
        sub = [sem(f"c_sub{u}") for u in range(2)]
        exp = [sem(f"c_exp{u}") for u in range(2)]
        used = [sem(f"c_used{u}") for u in range(2)]
        block = ctx.enter_context(nc.Block())
        last = NB // 2

        @block.gpsimd
        def _(pool):
            nc.gpsimd.memset(SAME, 0.0).then_inc(same, 1)
            for g in range(P // DH):
                pool.wait_ge(same, g + 1)
                nc.gpsimd.memset(SAME[g * DH:(g + 1) * DH, g * DH:(g + 1) * DH], 1.0).then_inc(same, 1)

        @block.scalar
        def _(act):
            def exps(i, u, n=P):
                act.wait_ge(sub[u], i + 1)
                nc.scalar.activation(KX[0:n, u, :], KX[0:n, u, :], ACT.Exp).then_inc(exp[u], 1)
            with act.Fori(0, last) as i:
                exps(i, 0)
                exps(i, 1)
            exps(last, 0, NLAST)

        @block.tensor
        def _(pe):
            pe.wait_ge(top_made, 1)
            for k in range(2):
                ins = nc.tensor.transpose(PA[:, k * P:(k + 1) * P], TOP[:, k * P:(k + 1) * P], m.ident[:, :])
            ins.then_inc(top_turned, 1)
            pe.wait_ge(diag_made, 2)
            for k in range(2):
                ins = nc.tensor.matmul(PB[:, k * P:(k + 1) * P], m.ones[:, :], DIAG[:, k, :], start=True, stop=True)
            ins.then_inc(top_spread, 1)

            def add(i, u, rows, start, stop):
                pe.wait_ge(exp[u], i + 1)
                for k in range(2):
                    ins = nc.tensor.matmul(PCC[k][:, 0:P + 1], KX[0:rows, u, k * P:(k + 1) * P],
                                           VM[0:rows, ds((i * 2 + u) * VW + k * (P + 1), P + 1)], start=start, stop=stop)
                ins.then_inc(used[u], 1)
            add(0, 0, P, True, False)
            add(0, 1, P, False, False)
            with pe.Fori(1, last) as i:
                add(i, 0, P, False, False)
                add(i, 1, P, False, False)
            add(last, 0, NLAST, False, True)
            pe.wait_ge(ctx_made, 2)
            for k in range(2):
                ins = nc.tensor.transpose(PA[:, k * P:(k + 1) * P], CTX[:, k, :], m.ident[:, :])
            ins.then_inc(ctx_turned, 1)
            pe.wait_ge(ctxt_made, 1)
            for k in range(2):
                ins = nc.tensor.matmul(PM[:, k * D:(k + 1) * D], CTXT[:, k, :], m.Wout[:, k, :], start=True, stop=True)
            ins.then_inc(m_made, 1)

        @block.vector
        def _(dve):
            t = Tally(dve, chain)
            t.link(nc.vector.tensor_reduce(TOP, KM[:, 0:NB - 1, :].rearrange("p b c -> p c b"), AX, ALU.max))
            nc.vector.tensor_tensor(TOP[0:NLAST, :], TOP[0:NLAST, :], KM[0:NLAST, NB - 1, :], ALU.max).then_inc(top_made, 1)
            dve.wait_ge(top_turned, 1)
            t.link(nc.vector.tensor_reduce(TOPT[:, 0:2], PA[:, 0:D].rearrange("p (k t) -> p k t", k=2), AX, ALU.max))
            for k in range(2):
                nc.vector.tensor_scalar(DIAG[:, k, :], m.ident[:, :], TOPT[:, k:k + 1], None, ALU.mult).then_inc(diag_made, 1)
            dve.wait_ge(top_spread, 1)
            t.link(nc.vector.tensor_copy(TOPB, PB[:, 0:D]))

            def subtract(i, u):
                nc.vector.tensor_tensor(KX[:, u, :], m.R1[:, ds((i * 2 + u) * D, D)], TOPB, ALU.subtract).then_inc(sub[u], 1)
            subtract(0, 0)
            subtract(0, 1)
            with dve.Fori(1, last) as i:
                for u in range(2):
                    dve.wait_ge(used[u], i + 0)
                    subtract(i, u)
            dve.wait_ge(used[0], last)
            subtract(last, 0)
            dve.wait_ge(used[0], last + 1)
            for k in range(2):
                t.inc(nc.vector.reciprocal(RDEN[:, k:k + 1], PCC[k][:, P:P + 1]))
            t.wait()
            dve.wait_ge(same, P // DH + 1)
            for k in range(2):
                nc.vector.scalar_tensor_tensor(out=CTX[:, k, :], in0=PCC[k][:, 0:P], scalar=RDEN[:, k:k + 1], in1=SAME,
                                               op0=ALU.mult, op1=ALU.mult).then_inc(ctx_made, 1)
            dve.wait_ge(ctx_turned, 1)
            nc.vector.tensor_copy(CTXT, PA[:, 0:D].rearrange("p (k t) -> p k t", k=2)).then_inc(ctxt_made, 1)
            dve.wait_ge(m_made, 1)
            t.link(nc.vector.tensor_copy(m.Wmix[:, :, :], PM[:, :].rearrange("p (k c) -> p k c", k=2)))


def score_phase(nc, m, a):
    QB = m.R2[:, 0:NB * D]
    KG = m.slots.rearrange("p (j c) -> p j c", j=GROUP)
    OH = m.R1[:, 0:16 * P].rearrange("p (h j e) -> p h j e", h=2, j=8)
    PR = m.R1[:, 2048:2048 + 1024].rearrange("p (g c) -> p g c", g=2)
    SC = m.R1[:, 3072:3072 + P].rearrange("p (h n) -> p h n", h=2)
    ST = m.R1[0:P // 2, 3200:3200 + 2 * P].rearrange("p (h e) -> p h e", h=2)
    with ExitStack() as ctx:
        sem = lambda n: m.sem(n)
        PQ = ctx.enter_context(nc.psum_tensor("PQ", [P, 4, 512], F32))
        PT = ctx.enter_context(nc.psum_tensor("PTS", [P, 2, 512], F32))
        turned = [sem(f"s_turned{h}") for h in range(2)]
        copied = [sem(f"s_copied{h}") for h in range(2)]
        stored = [sem(f"s_stored{h}") for h in range(2)]
        passed = sem("s_passed")
        q_in, mulled, scored = sem("s_qin"), sem("s_mulled"), sem("s_scored")
        idx_made = [sem(f"s_idx{h}") for h in range(2)]
        k_in = [sem(f"s_k{j}") for j in range(GROUP)]
        rel_in = [sem(f"s_rel{h}") for h in range(2)]
        hot = [sem(f"s_hot{h}") for h in range(2)]
        q_out = [sem(f"s_q{b}") for b in range(4)]
        block = ctx.enter_context(nc.Block())

        @block.sync
        def _(sp):
            h = NB // 2
            sp.dma_start(QB[:, 0:h * D].rearrange("p (b c) -> p b c", b=h),
                         m.q_d[0:h * P, :].rearrange("(b p) c -> p b c", p=P)).then_inc(q_in, 16)
            sp.dma_start(QB[:, h * D:NB * D].rearrange("p (b c) -> p b c", b=NB - h),
                         m.q_d[h * P:NB * P, :].rearrange("(b p) c -> p b c", p=P)).then_inc(q_in, 16)

            def load(i, h):
                sp.dma_start(OH[:, h, :, :], m.rel_rows[ds((i * 2 + h) * 8, 8), :].rearrange("(o s) e -> o s e", o=1)
                             .broadcast_to([P, 8, P])).then_inc(rel_in[h], 16)
            load(0, 0)
            load(0, 1)
            with sp.Fori(0, TURNS - 1) as i:
                for h in range(2):
                    sp.wait_ge(q_out[3], i * 2 + h + 1)
                    load(i + 1, h)

        @block.gpsimd
        def _(pool):
            def gather(i, first):
                for h in range(2):
                    pool.wait_ge(idx_made[h], i + 1)
                    for j in range(8 * h, 8 * h + 8):
                        if j % 2 == 0 and not first:
                            pool.wait_ge(mulled, i * 8 + j // 2 - 7)
                        if j % 2 == 0:
                            pool.sem_inc(passed, 1)
                        nc.gpsimd.indirect_dma_start(
                            out=KG[:, j, :], out_offset=None, in_=m.k_d[:, :],
                            in_offset=bass.IndirectOffsetOnAxis(ap=m.IDX[:, j:j + 1], axis=0)).then_inc(k_in[j], 16)
            gather(0, True)
            with pool.Fori(1, TURNS) as i:
                gather(i, False)

        @block.scalar
        def _(act):
            def store(i, h, first):
                act.wait_ge(turned[h], i + 1)
                if not first:
                    act.wait_ge(stored[h], i * 16)
                nc.scalar.activation(ST[:, h, :], PT[0:P // 2, h, 0:P], ACT.Copy).then_inc(copied[h], 1)
                act.wait_ge(copied[h], i + 1)
                act.dma_start(half_rows(m.score_d, i, h), ST[:, h, :]).then_inc(stored[h], 16)
            store(0, 0, True)
            store(0, 1, True)
            with act.Fori(1, TURNS) as i:
                store(i, 0, False)
                store(i, 1, False)
            for h in range(2):
                act.wait_ge(stored[h], 16 * TURNS)

        @block.tensor
        def _(pe):
            def turn(i, h, first):
                pe.wait_ge(scored, i * 8 + 4 * h + 4)
                if not first:
                    pe.wait_ge(copied[h], i + 0)
                pe.sem_inc(passed, 1)
                nc.tensor.transpose(PT[0:P // 2, h, 0:P], SC[:, h, :], m.ident[:, :]).then_inc(turned[h], 1)

            def expand(i, first):
                for j in range(GROUP):
                    g = j // 2
                    if j % 8 == 0:
                        pe.wait_ge(hot[j // 8], i + 1)
                    if j == 8 and not first:
                        turn(i - 1, 1, isinstance(i, int) and i == 1)
                    if j % 2 == 0 and (g >= 4 or not first):
                        pe.wait_ge(mulled, i * 8 + g - 3)
                    b = pe.value_load(m.BT[0:1, ds(i * GROUP + j, 1)], min_val=0, max_val=NB - 1)
                    ins = nc.tensor.matmul(PQ[:, g % 4, (j % 2) * D:(j % 2 + 1) * D], OH[:, j // 8, j % 8, :],
                                           QB[:, ds(b * D, D)], start=True, stop=True)
                    if j % 2:
                        ins.then_inc(q_out[g % 4], 1)
                turn(i, 0, first)
            pe.wait_ge(q_in, 32)
            expand(0, True)
            expand(1, False)
            with pe.Fori(2, TURNS) as i:
                expand(i, False)
            turn(TURNS - 1, 1, False)

        @block.vector
        def _(dve):
            def hots(i, h):
                dve.wait_ge(rel_in[h], (i + 1) * 16)
                nc.vector.tensor_scalar(OH[:, h, :, :], OH[:, h, :, :], m.iota_col[:, 0:1], None, ALU.is_equal).then_inc(hot[h], 1)

            def index(i, h):
                nc.vector.tensor_copy(m.IDX[:, 8 * h:8 * h + 8], m.SRC[:, ds(i * GROUP + 8 * h, 8)]).then_inc(idx_made[h], 1)

            def multiply(i, g, first):
                dve.wait_ge(q_out[g % 4], i * 2 + g // 4 + 1)
                dve.wait_ge(k_in[2 * g], (i + 1) * 16)
                dve.wait_ge(k_in[2 * g + 1], (i + 1) * 16)
                if g >= 2 or not first:
                    dve.wait_ge(scored, i * 8 + g - 1)
                nc.vector.tensor_tensor(PR[:, g % 2, :], PQ[:, g % 4, :], KG[:, 2 * g:2 * g + 2, :].rearrange("p j c -> p (j c)"),
                                        ALU.mult).then_inc(mulled, 1)

            def add_up(i, g, first):
                dve.wait_ge(mulled, i * 8 + g + 1)
                if g % 4 == 0 and not first:
                    dve.wait_ge(turned[g // 4], i + 0)
                nc.vector.tensor_reduce(SC[:, g // 4, (g % 4) * 2 * HEADS:(g % 4 + 1) * 2 * HEADS],
                                        PR[:, g % 2, :].rearrange("p (n d) -> p n d", d=DH), AX, ALU.add).then_inc(scored, 1)

            def turn(i, first, last):
                for g in range(8):
                    multiply(i, g, first)
                    if g == 1:
                        hots(i, 1)
                    if g:
                        add_up(i, g - 1, first)
                    if g == 4 and not last:
                        index(i + 1, 0)
                    if g == 5 and not last:
                        hots(i + 1, 0)
                add_up(i, 7, first)
                if not last:
                    index(i + 1, 1)
            index(0, 0)
            index(0, 1)
            hots(0, 0)
            turn(0, True, False)
            with dve.Fori(1, TURNS - 1) as i:
                turn(i, False, False)
            turn(TURNS - 1, False, True)


def softmax_phase(nc, m, a):
    S, KEY = m.R1[:, 0:CLEN], m.R1[:, CLEN:2 * CLEN]
    CUT, M = m.R2[:, 0:CLEN + 1], m.R2[:, CLEN + 1:2 * CLEN + 1]
    END = m.slots[:, 1024:1028]
    ENDS = m.slots[:, 1088:1088 + 4 * CHUNKS]
    MSK = m.slots[:, 1280:1280 + 2 * CHUNKS]
    TOP = m.slots[:, 1344:1346]
    with ExitStack() as ctx:
        sem = lambda n: m.sem(n)
        s_in, key_in, end_made, end_out, ends_in = (sem(n) for n in ("m_sin", "m_kin", "m_end", "m_eout", "m_ein"))
        chain, diff, exped, ex_out = (sem(n) for n in ("m_chain", "m_diff", "m_exp", "m_xout"))
        block = ctx.enter_context(nc.Block())

        @block.sync
        def _(sp):
            for h in range(HEADS):
                sp.dma_start(KEY[h * CHUNKS:(h + 1) * CHUNKS, :],
                             m.key_rows[:, :].rearrange("s e -> (s e)").rearrange("(c l) -> c l", c=CHUNKS)).then_inc(key_in, 16)
            sp.dma_start(S, m.score_d[:, :].rearrange("h (c l) -> (h c) l", c=CHUNKS)).then_inc(s_in, 16)
            sp.wait_ge(end_made, 2)
            sp.dma_start(m.end_d[:, :], END).then_inc(end_out, 16)
            sp.wait_ge(end_out, 16)
            for h in range(HEADS):
                sp.dma_start(ENDS[h * CHUNKS:(h + 1) * CHUNKS, :],
                             m.end_d[h * CHUNKS:(h + 1) * CHUNKS, :].rearrange("c k -> (c k)").rearrange("(o n) -> o n", o=1)
                             .broadcast_to([CHUNKS, 4 * CHUNKS])).then_inc(ends_in, 16)
            sp.wait_ge(exped, 1)
            sp.dma_start(m.ex_d[:, :].rearrange("h (c l) -> (h c) l", c=CHUNKS), S).then_inc(ex_out, 16)
            sp.wait_ge(ex_out, 16)

        @block.scalar
        def _(act):
            act.wait_ge(diff, 1)
            nc.scalar.activation(S, S, ACT.Exp, scale=SCALE).then_inc(exped, 1)

        @block.vector
        def _(dve):
            t = Tally(dve, chain)
            dve.wait_ge(key_in, 16 * HEADS)
            t.inc(nc.vector.memset(CUT[:, 0:1], -BIG))
            t.inc(nc.vector.memset(CUT[:, CLEN:CLEN + 1], -BIG))
            t.link(nc.vector.tensor_tensor(CUT[:, 1:CLEN], KEY[:, 1:CLEN], KEY[:, 0:CLEN - 1], ALU.not_equal))
            t.link(nc.vector.tensor_scalar(CUT[:, 1:CLEN], CUT[:, 1:CLEN], -BIG, None, ALU.mult))
            dve.wait_ge(s_in, 16)
            t.link(nc.vector.tensor_tensor_scan(M, CUT[:, 0:CLEN], S, -BIG, ALU.add, ALU.max))
            t.link(nc.vector.tensor_tensor_scan(M[:, ::-1], CUT[:, 1:CLEN + 1][:, ::-1], M[:, ::-1], -BIG, ALU.add, ALU.max))
            nc.vector.tensor_copy(END[:, 0:2], M[:, 0:CLEN:CLEN - 1]).then_inc(end_made, 1)
            nc.vector.tensor_copy(END[:, 2:4], KEY[:, 0:CLEN:CLEN - 1]).then_inc(end_made, 1)
            dve.wait_ge(ends_in, 16 * HEADS)
            ends = ENDS.rearrange("p (c v k) -> p c v k", v=2, k=2)
            msk = MSK.rearrange("p (c k) -> p c k", k=2)
            for e in range(2):
                t.link(nc.vector.tensor_scalar(msk, ends[:, :, 1, :], END[:, 2 + e:3 + e], -BIG, ALU.not_equal, ALU.mult))
                t.link(nc.vector.tensor_tensor(msk, msk, ends[:, :, 0, :], ALU.add))
                t.link(nc.vector.tensor_reduce(TOP[:, e:e + 1], MSK, AX, ALU.max))
            for e in range(2):
                t.link(nc.vector.tensor_scalar(CUT[:, 0:CLEN], KEY, END[:, 2 + e:3 + e], -BIG, ALU.not_equal, ALU.mult))
                t.link(nc.vector.scalar_tensor_tensor(out=M, in0=CUT[:, 0:CLEN], scalar=TOP[:, e:e + 1], in1=M,
                                                      op0=ALU.add, op1=ALU.max))
            nc.vector.tensor_tensor(S, S, M, ALU.subtract).then_inc(diff, 1)


def aggregate_phase(nc, m, a):
    ACC = m.R1
    VG = m.slots.rearrange("p (j c) -> p j c", j=GROUP)
    OH = m.R2[:, 0:16 * P].rearrange("p (h j e) -> p h j e", h=2, j=8)
    WV = m.R2[:, 2048:2048 + GROUP * AW].rearrange("p (j c) -> p j c", j=GROUP)
    XT = m.R2[0:P // 2, 6400:6400 + 2 * P].rearrange("p (h e) -> p h e", h=2)
    EX = m.R2[:, 6656:6656 + P].rearrange("p (h n) -> p h n", h=2)
    with ExitStack() as ctx:
        sem = lambda n: m.sem(n)
        PA = ctx.enter_context(nc.psum_tensor("PACC", [P, 4, 512], F32))
        PT = ctx.enter_context(nc.psum_tensor("PTG", [P, 2, 512], F32))
        passed = sem("g_passed")
        x_in = [sem(f"g_xin{h}") for h in range(2)]
        turned = [sem(f"g_turned{h}") for h in range(2)]
        zeroed, mulled, hot, summed, added = (sem(n) for n in ("g_zero", "g_mulled", "g_hot", "g_summed", "g_added"))
        idx_made = [sem(f"g_idx{h}") for h in range(2)]
        v_in = [sem(f"g_v{j}") for j in range(GROUP)]
        w_made = [sem(f"g_w{h}") for h in range(2)]
        block = ctx.enter_context(nc.Block())

        @block.gpsimd
        def _(pool):
            def gather(i, first):
                for h in range(2):
                    pool.wait_ge(idx_made[h], i + 1)
                    for j in range(8 * h, 8 * h + 8):
                        if j % 2 == 0 and not first:
                            pool.wait_ge(mulled, i * 8 + j // 2 - 7)
                        if j % 2 == 0:
                            pool.sem_inc(passed, 1)
                        nc.gpsimd.indirect_dma_start(
                            out=VG[:, j, :], out_offset=None, in_=m.v_d[:, :],
                            in_offset=bass.IndirectOffsetOnAxis(ap=m.IDX[:, j:j + 1], axis=0)).then_inc(v_in[j], 16)
            gather(0, True)
            with pool.Fori(1, TURNS) as i:
                gather(i, False)

        @block.sync
        def _(sp):
            def load(i, h):
                sp.dma_start(XT[:, h, :], half_rows(m.ex_d, i, h)).then_inc(x_in[h], 16)
            load(0, 0)
            load(0, 1)
            with sp.Fori(0, TURNS - 1) as i:
                for h in range(2):
                    sp.wait_ge(turned[h], i + 1)
                    load(i + 1, h)

        @block.scalar
        def _(act):
            def weights(i, h, first):
                act.wait_ge(turned[h], i + 1)
                if not first:
                    act.wait_ge(mulled, i * 8 + 4 * h - 4)
                    act.wait_ge(summed, i * GROUP + 8 * h - 8)
                nc.scalar.activation(EX[:, h, :], PT[:, h, 0:P // 2], ACT.Copy).then_inc(w_made[h], 1)
                nc.scalar.activation(WV[:, 8 * h:8 * h + 8, D:AW], PT[:, h, 0:P // 2].rearrange("p (j h) -> p j h", j=8),
                                     ACT.Copy).then_inc(w_made[h], 1)
            weights(0, 0, True)
            weights(0, 1, True)
            with act.Fori(1, TURNS) as i:
                weights(i, 0, False)
                weights(i, 1, False)

        @block.tensor
        def _(pe):
            def turn(i, h, first):
                pe.wait_ge(x_in[h], (i + 1) * 16)
                if not first:
                    pe.wait_ge(w_made[h], i * 2)
                pe.sem_inc(passed, 1)
                nc.tensor.transpose(PT[:, h, 0:P // 2], XT[:, h, :], m.ident[0:P // 2, 0:P // 2]).then_inc(turned[h], 1)

            def sums(i, first, last):
                for j in range(GROUP):
                    if j % 8 == 0:
                        pe.wait_ge(hot, i * 2 + j // 8 + 1)
                        pe.wait_ge(w_made[j // 8], i * 2 + 2)
                    if j == 8 and not last:
                        turn(i + 1, 0, False)
                    if j % 2 == 0:
                        pe.wait_ge(mulled, i * 8 + j // 2 + 1)
                    if j >= 4 or not first:
                        pe.wait_ge(added, i * GROUP + j - 3)
                    nc.tensor.matmul(PA[:, j % 4, 0:AW], OH[:, j // 8, j % 8, :], WV[:, j, :],
                                     start=True, stop=True).then_inc(summed, 1)
                if not last:
                    turn(i + 1, 1, False)
            turn(0, 0, True)
            turn(0, 1, True)
            sums(0, True, False)
            with pe.Fori(1, TURNS - 1) as i:
                sums(i, False, False)
            sums(TURNS - 1, False, True)

        @block.vector
        def _(dve):
            def index(i, h):
                nc.vector.tensor_copy(m.IDX[:, 8 * h:8 * h + 8], m.SRC[:, ds(i * GROUP + 8 * h, 8)]).then_inc(idx_made[h], 1)

            def hots(i, h):
                nc.vector.tensor_tensor(OH[:, h, :, :], m.iota_row[:, :].rearrange("p (o n) -> p o n", o=1).broadcast_to([P, 8, P]),
                                        m.REL[:, ds(i * GROUP + 8 * h, 8)].rearrange("p (j o) -> p j o", o=1).broadcast_to([P, 8, P]),
                                        ALU.is_equal).then_inc(hot, 1)

            def multiply(i, g):
                dve.wait_ge(v_in[2 * g], (i + 1) * 16)
                dve.wait_ge(v_in[2 * g + 1], (i + 1) * 16)
                if g % 4 == 0:
                    dve.wait_ge(w_made[g // 4], i * 2 + 2)
                nc.vector.tensor_tensor(
                    WV[:, 2 * g:2 * g + 2, 0:D].rearrange("p j (h d) -> p j h d", d=DH),
                    VG[:, 2 * g:2 * g + 2, :].rearrange("p j (h d) -> p j h d", d=DH),
                    EX[:, g // 4, (g % 4) * 2 * HEADS:(g % 4 + 1) * 2 * HEADS].rearrange("p (j h o) -> p j h o", j=2, o=1)
                    .broadcast_to([P, 2, HEADS, DH]), ALU.mult).then_inc(mulled, 1)

            def add(i, j, first):
                b = dve.value_load(m.BT[0:1, ds(i * GROUP + j, 1)], min_val=0, max_val=NB - 1)
                dve.wait_ge(summed, i * GROUP + j + 1)
                if j or not first:
                    dve.wait_ge(added, i * GROUP + j)
                nc.vector.tensor_tensor(ACC[:, ds(b * AW, AW)], ACC[:, ds(b * AW, AW)], PA[:, j % 4, 0:AW],
                                        ALU.add).then_inc(added, 1)

            def turn(i, first, last):
                for g in range(8):
                    if g == 0:
                        hots(i, 1)
                    multiply(i, g)
                    if g:
                        add(i, 2 * g - 2, first)
                        add(i, 2 * g - 1, first)
                    if g == 4 and not last:
                        index(i + 1, 0)
                        hots(i + 1, 0)
                if not last:
                    index(i + 1, 1)
                add(i, GROUP - 2, False)
                add(i, GROUP - 1, False)
            nc.vector.memset(ACC[:, 0:NB * AW], 0.0).then_inc(zeroed, 1)
            dve.wait_ge(zeroed, 1)
            index(0, 0)
            index(0, 1)
            hots(0, 0)
            turn(0, True, False)
            with dve.Fori(1, TURNS - 1) as i:
                turn(i, False, False)
            turn(TURNS - 1, False, True)


def output_phase(nc, m, a):
    ACC = m.R1
    XT = m.R2[:, 0:2 * NB * P].rearrange("p (k t) -> p k t", k=2)
    SL = m.slots
    XI = SL[:, 0:2 * D].rearrange("p (u c) -> p u c", u=2)
    NI = SL[:, 512:512 + 2 * D].rearrange("p (u c) -> p u c", u=2)
    AI = SL[:, 1024:1024 + 4 * D].rearrange("p (u c) -> p u c", u=2)
    AT = SL[:, 2048:2048 + 4 * D].rearrange("p (u k t) -> p u k t", u=2, k=4)
    Y = m.EX[:, 0:2 * D].rearrange("p (u c) -> p u c", u=2)
    G = m.EX[:, 512:512 + 2 * D].rearrange("p (u c) -> p u c", u=2)
    H = m.EX[:, 1024:1024 + 2 * D].rearrange("p (u c) -> p u c", u=2)
    X1 = m.EX[:, 1536:1536 + 2 * D].rearrange("p (u c) -> p u c", u=2)
    X2 = m.EX[:, 2048:2048 + 2 * D].rearrange("p (u c) -> p u c", u=2)
    JUNK = m.EX[:, 2560:2560 + D]
    DEN = m.EX[:, 2816:2816 + 2 * HEADS].rearrange("p (u h) -> p u h", u=2)
    BST = m.EX[:, 2880:2880 + 36].rearrange("p (u k c) -> p u k c", u=2, k=3)
    ST = m.EX[:, 2944:2944 + 12].rearrange("p (u k c) -> p u k c", u=2, k=3)
    SD = m.EX[:, 2976:2976 + 8].rearrange("p (u k) -> p u k", u=2)
    with ExitStack() as ctx:
        sem = lambda n: [m.sem(f"{n}{u}") for u in range(2)]
        PT = ctx.enter_context(nc.psum_tensor("POT", [P, 2, 512], F32))
        PO = ctx.enter_context(nc.psum_tensor("POO", [P, 2, 512], F32))
        PX = ctx.enter_context(nc.psum_tensor("POX", [P, 2, 512], F32))
        x_in, at_made, turned, at_copied, o_made = (sem(n) for n in ("o_xin", "o_at", "o_turned", "o_copied", "o_made"))
        n_in, q_in = sem("o_nin"), sem("o_qin")
        var1, std1, var2, std2 = (sem(n) for n in ("o_var1", "o_std1", "o_var2", "o_std2"))
        x2_made, x2_turned, x2_copied = (sem(n) for n in ("o_x2", "o_x2t", "o_x2c"))
        chain, passed = m.sem("o_chain"), m.sem("o_passed")
        block = ctx.enter_context(nc.Block())
        last = NB // 2
        rows = lambda i, u: ds((i * 2 + u) * P, P)

        @block.sync
        def _(sp):
            def load(i, u, n):
                sp.dma_start(NI[:, u, :], m.xn_d[rows(i, u), :]).then_inc(n_in[u], 16)
                sp.dma_start(AI[:, u, D:2 * D], m.qs_d[rows(i, u), :]).then_inc(q_in[u], 16)
                sp.dma_start(XI[0:n, u, :], a.x[ds((i * 2 + u) * P, n), :]).then_inc(x_in[u], 16)
            load(0, 0, P)
            load(0, 1, P)
            with sp.Fori(0, last - 1) as i:
                for u in range(2):
                    sp.wait_ge(x2_made[u], i + 1)
                    load(i + 1, u, P)
            sp.wait_ge(x2_made[0], last)
            load(last, 0, NLAST)

        @block.scalar
        def _(act):
            def copy_a(i, u):
                act.wait_ge(turned[u], i + 1)
                nc.scalar.activation(AT[:, u, :, :], PT[:, u, :].rearrange("p (k t) -> p k t", k=4), ACT.Copy).then_inc(at_copied[u], 1)

            def root(i, u):
                act.wait_ge(var1[u], i + 1)
                nc.scalar.activation(SD[:, u, 0:2], ST[:, u, 0:2, 1], ACT.Sqrt, bias=m.eps[:, :]).then_inc(std1[u], 1)

            def root2(i, u):
                act.wait_ge(var2[u], i + 1)
                nc.scalar.activation(SD[:, u, 2:3], ST[:, u, 2, 1:2], ACT.Sqrt, bias=m.eps[:, :]).then_inc(std2[u], 1)

            def copy_x(i, u):
                act.wait_ge(x2_turned[u], i + 1)
                nc.scalar.activation(XT[:, :, ds((i * 2 + u) * P, P)], PX[:, u, 0:D].rearrange("p (k t) -> p k t", k=2),
                                     ACT.Copy).then_inc(x2_copied[u], 1)
            copy_a(0, 0)
            with act.Fori(0, last) as i:
                root(i, 0)
                copy_a(i, 1)
                root2(i, 0)
                copy_x(i, 0)
                root(i, 1)
                copy_a(i + 1, 0)
                root2(i, 1)
                copy_x(i, 1)
            root(last, 0)
            root2(last, 0)
            copy_x(last, 0)

        @block.tensor
        def _(pe):
            def attend(i, u, first):
                pe.wait_ge(at_made[u], i + 1)
                pe.wait_ge(q_in[u], (i + 1) * 16)
                for k in range(4):
                    ins = nc.tensor.transpose(PT[:, u, k * P:(k + 1) * P], AI[:, u, k * P:(k + 1) * P], m.ident[:, :])
                ins.then_inc(turned[u], 1)
                pe.wait_ge(at_copied[u], i + 1)
                for w, c in ((m.Wo, 0), (m.Wmix, 1)):
                    for k in range(2):
                        ins = nc.tensor.matmul(PO[:, u, c * D:(c + 1) * D], AT[:, u, 2 * c + k, :], w[:, k, :],
                                               start=(k == 0), stop=(k == 1))
                ins.then_inc(o_made[u], 1)

            def turn_x(i, u, first):
                pe.wait_ge(x2_made[u], i + 1)
                if not first:
                    pe.wait_ge(x2_copied[u], i + 0)
                for k in range(2):
                    ins = nc.tensor.transpose(PX[:, u, k * P:(k + 1) * P], X2[:, u, k * P:(k + 1) * P], m.ident[:, :])
                ins.then_inc(x2_turned[u], 1)
            attend(0, 0, True)
            attend(0, 1, True)
            turn_x(0, 0, True)
            attend(1, 0, False)
            turn_x(0, 1, True)
            with pe.Fori(1, last) as i:
                attend(i, 1, False)
                turn_x(i, 0, False)
                attend(i + 1, 0, False)
                turn_x(i, 1, False)
            turn_x(last, 0, False)

        @block.vector
        def _(dve):
            t = Tally(dve, chain)

            def attention(i, u):
                b = i * 2 + u
                if not isinstance(i, int) or i:
                    dve.wait_ge(turned[u], i + 0)
                t.link(nc.vector.tensor_scalar(DEN[:, u, :], ACC[:, ds(b * AW + D, HEADS)], 1e-9, None, ALU.add))
                t.link(nc.vector.reciprocal(DEN[:, u, :], DEN[:, u, :]))
                nc.vector.tensor_tensor(AI[:, u, 0:D].rearrange("p (h d) -> p h d", d=DH),
                                        ACC[:, ds(b * AW, D)].rearrange("p (h d) -> p h d", d=DH),
                                        DEN[:, u, :].rearrange("p (h o) -> p h o", o=1).broadcast_to([P, HEADS, DH]),
                                        ALU.mult).then_inc(at_made[u], 1)

            def norms(i, u):
                dve.wait_ge(o_made[u], i + 1)
                dve.wait_ge(n_in[u], (i + 1) * 16)
                dve.wait_ge(x_in[u], (i + 1) * 16)
                mix = PO[:, u, D:2 * D]
                t.inc(nc.vector.tensor_tensor(Y[:, u, :], PO[:, u, 0:D], NI[:, u, :], ALU.add))
                t.link(nc.vector.bn_stats(BST[:, u, 1, :], mix))
                t.link(nc.vector.bn_stats(BST[:, u, 0, :], Y[:, u, :]))
                t.inc(nc.vector.tensor_tensor(X1[:, u, :], XI[:, u, :], m.rows[:, 1, :], ALU.add))
                t.inc(nc.vector.bn_aggr(ST[:, u, 0, :], BST[:, u, 0, :]))
                nc.vector.bn_aggr(ST[:, u, 1, :], BST[:, u, 1, :]).then_inc(var1[u], 1)
                t.wait()
                dve.wait_ge(var1[u], i + 1)
                t.inc(nc.vector.scalar_tensor_tensor(out=G[:, u, :], in0=Y[:, u, :], scalar=ST[:, u, 0, 0:1], in1=m.rows[:, 0, :],
                                                     op0=ALU.subtract, op1=ALU.mult))
                t.inc(nc.vector.scalar_tensor_tensor(out=H[:, u, :], in0=mix, scalar=ST[:, u, 1, 0:1], in1=m.rows[:, 2, :],
                                                     op0=ALU.subtract, op1=ALU.mult))
                dve.wait_ge(std1[u], i + 1)
                t.link(nc.vector.reciprocal(SD[:, u, 0:2], SD[:, u, 0:2]))
                t.link(nc.vector.scalar_tensor_tensor(out=G[:, u, :], in0=G[:, u, :], scalar=SD[:, u, 0:1], in1=X1[:, u, :],
                                                      op0=ALU.mult, op1=ALU.add))
                t.link(nc.vector.scalar_tensor_tensor(out=X1[:, u, :], in0=H[:, u, :], scalar=SD[:, u, 1:2], in1=G[:, u, :],
                                                      op0=ALU.mult, op1=ALU.add))
                t.link(nc.vector.bn_stats(BST[:, u, 2, :], X1[:, u, :]))
                dve.sem_inc(passed, 1)
                nc.vector.bn_aggr(ST[:, u, 2, :], BST[:, u, 2, :]).then_inc(var2[u], 1)

            def router(i, u):
                b = i * 2 + u
                dve.wait_ge(std2[u], i + 1)
                dve.wait_ge(var2[u], i + 1)
                if not isinstance(i, int) or i:
                    dve.wait_ge(x2_turned[u], i + 0)
                t.link(nc.vector.reciprocal(SD[:, u, 2:3], SD[:, u, 2:3]))
                nc.vector.tensor_scalar(X2[:, u, :], X1[:, u, :], ST[:, u, 2, 0:1], SD[:, u, 2:3],
                                        ALU.subtract, ALU.mult).then_inc(x2_made[u], 1)
                dve.wait_ge(x2_made[u], i + 1)
                t.inc(nc.vector.tensor_tensor(ACC[:, ds(b * AW, D)], X1[:, u, :], X2[:, u, :], ALU.add))
                t.link(nc.vector.tensor_tensor_reduce(out=JUNK, in0=X2[:, u, :], in1=m.rows[:, 4, :], scale=1.0, scalar=0.0,
                                                      op0=ALU.mult, op1=ALU.add, accum_out=SD[:, u, 3:4]))
                t.link(nc.vector.tensor_copy(m.weight[:, ds(b, 1)], SD[:, u, 3:4]))
            each = 2 + 11 + 4
            attention(0, 0)
            attention(0, 1)
            norms(0, 0)
            router(0, 0)
            attention(1, 0)
            norms(0, 1)
            router(0, 1)
            with dve.Fori(1, last) as i:
                t.enter(i - 1, 2 * each)
                attention(i, 1)
                norms(i, 0)
                router(i, 0)
                attention(i + 1, 0)
                norms(i, 1)
                router(i, 1)
                t.leave(last - 1)
            norms(last, 0)
            router(last, 0)
            t.link(nc.vector.tensor_scalar(m.weight[:, :], m.weight[:, :], m.brc[:, 0:1], None, ALU.add))


def feed_forward_phase(nc, m, a):
    BASE = m.R1
    XT = m.R2[:, 0:2 * NB * P].rearrange("p (k t) -> p k t", k=2)
    W1 = m.slots[:, 0:2 * FF].rearrange("p (k n) -> p k n", k=2)
    W2 = m.slots[:, 2 * FF:4 * FF].rearrange("p (c n) -> p c n", c=8)
    HT = m.EX[:, 0:8 * 512].rearrange("p (c t) -> p c t", c=8)
    TMP = m.EX[:, 4096:4096 + 4 * D].rearrange("p (u c) -> p u c", u=4)
    S = [m.EX[:, 5120 + 64 * k:5120 + 64 * k + NB] for k in range(10)]
    HI, LO, NEG, SGN, KEY, T1, T2, SEL, TIE, COEF = S
    C = m.EX[:, 5824:5856]
    U32 = mybir.dt.uint32
    groups = NB // 4
    with ExitStack() as ctx:
        sem = lambda n: m.sem(n)
        PH = ctx.enter_context(nc.psum_tensor("PFH", [P, 3, 512], F32))
        PY = ctx.enter_context(nc.psum_tensor("PFY", [P, 4, 512], F32))
        PS = ctx.enter_context(nc.psum_tensor("PFS", [P, 512], F32))
        w_in, chain, counted, total, ties, ranked = (sem(n) for n in ("f_win", "f_chain", "f_cnt", "f_tot", "f_ties", "f_rank"))
        h_made, h_act, y_made, y_out, stored, tmp_made = (sem(n) for n in ("f_h", "f_act", "f_y", "f_yo", "f_st", "f_tmp"))
        block = ctx.enter_context(nc.Block())

        @block.sync
        def _(sp):
            sp.dma_start(W1, a.L0_ffn_w1.rearrange("(k p) n -> p k n", p=P)).then_inc(w_in, 16)
            sp.dma_start(W2, a.L0_ffn_w2.rearrange("(c p) n -> p c n", p=P)).then_inc(w_in, 16)
            with sp.Fori(0, NB - 1) as b:
                sp.wait_ge(y_out, b + 1)
                sp.dma_start(a.out[ds(b * P, P), :], BASE[:, ds(b * AW, D)]).then_inc(stored, 16)
            sp.wait_ge(y_out, NB)
            sp.dma_start(a.out[(NB - 1) * P:N, :], BASE[0:NLAST, (NB - 1) * AW:(NB - 1) * AW + D]).then_inc(stored, 16)
            sp.wait_ge(stored, 16 * NB)

        @block.scalar
        def _(act):
            def group(i):
                for c in range(8):
                    act.wait_ge(h_made, i * 8 + c + 1)
                    nc.scalar.activation(HT[:, c, :], PH[:, c % 3, :], ACT.Gelu_apprx_tanh, bias=m.b1c[:, c:c + 1]).then_inc(h_act, 1)
            with act.Fori(0, groups) as i:
                group(i)
            for c in range(8):
                act.wait_ge(h_made, groups * 8 + c + 1)
                nc.scalar.activation(HT[:, c, 0:P], PH[:, c % 3, 0:P], ACT.Gelu_apprx_tanh, bias=m.b1c[:, c:c + 1]).then_inc(h_act, 1)

        @block.tensor
        def _(pe):
            with pe.Fori(0, 32) as r:
                pe.wait_ge(counted, r + 1)
                nc.tensor.matmul(PS[:, 0:1], m.ones[:, :], C[:, 3:4], start=True, stop=True).then_inc(total, 1)
            pe.wait_ge(ties, 1)
            nc.tensor.matmul(PS[:, 64:64 + NB], m.ones[:, :], SEL, start=True, stop=True)
            nc.tensor.matmul(PS[:, 128:128 + NB], m.upper[:, :], TIE, start=True, stop=True)
            nc.tensor.matmul(PS[:, 192:192 + NB], m.ones[:, :], TIE, start=True, stop=True).then_inc(ranked, 1)
            pe.wait_ge(w_in, 32)

            def group(i, blocks, first):
                n = blocks * P
                for c in range(8):
                    if c >= 3 or not first:
                        pe.wait_ge(h_act, i * 8 + c - 2)
                    for k in range(2):
                        ins = nc.tensor.matmul(PH[:, c % 3, 0:n], W1[:, k, c * P:(c + 1) * P], XT[:, k, ds(i * 4 * P, n)],
                                               start=(k == 0), stop=(k == 1))
                    ins.then_inc(h_made, 1)
                pe.wait_ge(h_act, i * 8 + 8)
                for b in range(blocks):
                    if not first:
                        pe.wait_ge(tmp_made, i * 4 + b - 3)
                    for c in range(8):
                        ins = nc.tensor.matmul(PY[:, b, 0:D], HT[:, c, b * P:(b + 1) * P], W2[:, c, :],
                                               start=(c == 0), stop=(c == 7))
                    ins.then_inc(y_made, 1)
            group(0, 4, True)
            with pe.Fori(1, groups) as i:
                group(i, 4, False)
            group(groups, NB - 4 * groups, False)

        @block.vector
        def _(dve):
            t = Tally(dve, chain)
            bits = m.weight[:, :].bitcast(U32)
            t.link(nc.vector.tensor_scalar(m.weight[:, :], m.weight[:, :], 0.0, None, ALU.add))
            t.link(nc.vector.tensor_scalar(T1.bitcast(U32), bits, 16, None, ALU.logical_shift_right))
            t.link(nc.vector.tensor_copy(HI, T1.bitcast(U32)))
            t.link(nc.vector.tensor_scalar(T2.bitcast(U32), bits, 65535, None, ALU.bitwise_and))
            t.link(nc.vector.tensor_copy(LO, T2.bitcast(U32)))
            t.link(nc.vector.tensor_scalar(NEG, m.weight[:, :], 0.0, None, ALU.is_lt))
            t.link(nc.vector.tensor_scalar(SGN, NEG, -2.0, 1.0, ALU.mult, ALU.add))
            t.link(nc.vector.tensor_tensor(LO, LO, SGN, ALU.mult))
            t.link(nc.vector.scalar_tensor_tensor(out=LO, in0=NEG, scalar=65535.0, in1=LO, op0=ALU.mult, op1=ALU.add))
            t.link(nc.vector.tensor_tensor(HI, HI, SGN, ALU.mult))
            t.link(nc.vector.scalar_tensor_tensor(out=HI, in0=NEG, scalar=65535.0 - 32768.0, in1=HI, op0=ALU.mult, op1=ALU.add))
            t.link(nc.vector.tensor_scalar(HI, HI, 32768.0, None, ALU.add))
            t.link(nc.vector.tensor_scalar(T1[:, 0:1], m.iota_col[:, 0:1], float(NLAST), None, ALU.is_lt))
            t.link(nc.vector.scalar_tensor_tensor(out=HI[:, NB - 1:NB], in0=HI[:, NB - 1:NB], scalar=1.0, in1=T1[:, 0:1],
                                                  op0=ALU.add, op1=ALU.mult))
            t.link(nc.vector.tensor_scalar(HI[:, NB - 1:NB], HI[:, NB - 1:NB], -1.0, None, ALU.add))

            def search(key, base):
                t.link(nc.vector.memset(C[:, 0:1], 0.0))
                t.link(nc.vector.memset(C[:, 1:2], 32768.0))
                with dve.Fori(0, 16) as r:
                    t.enter(r, 4)
                    t.link(nc.vector.tensor_tensor(C[:, 2:3], C[:, 0:1], C[:, 1:2], ALU.add))
                    nc.vector.tensor_scalar(T2, key, C[:, 2:3], None, ALU.is_ge, ALU.add, accum_out=C[:, 3:4]).then_inc(counted, 1)
                    dve.wait_ge(total, r + (base + 1))
                    t.link(nc.vector.scalar_tensor_tensor(out=C[:, 4:5], in0=PS[:, 0:1], scalar=float(KEEP), in1=C[:, 1:2],
                                                          op0=ALU.is_ge, op1=ALU.mult))
                    t.link(nc.vector.tensor_tensor(C[:, 0:1], C[:, 0:1], C[:, 4:5], ALU.add))
                    t.link(nc.vector.tensor_scalar(C[:, 1:2], C[:, 1:2], 0.5, None, ALU.mult))
                    t.leave(16)
            search(HI, 0)
            t.link(nc.vector.tensor_scalar(T1, HI, C[:, 0:1], 65537.0, ALU.is_gt, ALU.mult))
            t.link(nc.vector.tensor_scalar(SEL, HI, C[:, 0:1], None, ALU.is_equal))
            t.link(nc.vector.scalar_tensor_tensor(out=KEY, in0=LO, scalar=1.0, in1=SEL, op0=ALU.add, op1=ALU.mult))
            t.link(nc.vector.tensor_tensor(KEY, KEY, T1, ALU.add))
            t.link(nc.vector.tensor_scalar(KEY, KEY, -1.0, None, ALU.add))
            search(KEY, 16)
            t.link(nc.vector.tensor_scalar(SEL, KEY, C[:, 0:1], None, ALU.is_gt))
            nc.vector.tensor_scalar(TIE, KEY, C[:, 0:1], None, ALU.is_equal).then_inc(ties, 1)
            dve.wait_ge(ranked, 1)
            t.link(nc.vector.tensor_reduce(C[:, 5:6], PS[:, 64:64 + NB], AX, ALU.add))
            t.link(nc.vector.tensor_scalar(C[:, 5:6], C[:, 5:6], -1.0, float(KEEP), ALU.mult, ALU.add))
            t.link(nc.vector.tensor_copy(T1, PS[:, 192:192 + NB]))
            t.link(nc.vector.memset(NEG, 0.0))
            t.link(nc.vector.tensor_tensor_scan(T2, NEG, T1, 0.0, ALU.add, ALU.add))
            t.link(nc.vector.tensor_tensor(T2, T2, T1, ALU.subtract))
            t.link(nc.vector.tensor_tensor(T2, T2, PS[:, 128:128 + NB], ALU.add))
            t.link(nc.vector.tensor_scalar(T2, T2, C[:, 5:6], None, ALU.is_le))
            t.link(nc.vector.tensor_tensor(T2, T2, TIE, ALU.mult))
            t.link(nc.vector.tensor_tensor(SEL, SEL, T2, ALU.add))
            t.link(nc.vector.tensor_tensor(COEF, SEL, m.weight[:, :], ALU.mult))

            def finish(i, b):
                k = i * 4 + b
                dve.wait_ge(y_made, k + 1)
                if not isinstance(i, int):
                    dve.wait_ge(y_out, k - 3)
                nc.vector.tensor_tensor(TMP[:, b, :], PY[:, b, 0:D], m.rows[:, 3, :], ALU.add).then_inc(tmp_made, 1)
                dve.wait_ge(tmp_made, k + 1)
                nc.vector.scalar_tensor_tensor(out=BASE[:, ds(k * AW, D)], in0=TMP[:, b, :], scalar=COEF[:, ds(k, 1)],
                                               in1=BASE[:, ds(k * AW, D)], op0=ALU.mult, op1=ALU.add).then_inc(y_out, 1)
            for b in range(4):
                finish(0, b)
            with dve.Fori(1, groups) as i:
                for b in range(4):
                    finish(i, b)
            for b in range(NB - 4 * groups):
                dve.wait_ge(y_out, 4 * groups + b - 3)
                finish(groups, b)


def build_program(nc, a):
    m = Mem()
    with ExitStack() as ctx:
        sb = lambda n, shape, dt=F32: ctx.enter_context(nc.sbuf_tensor(n, shape, dt))
        region = 2 * CLEN + 8
        m.R1 = sb("region1", [P, region])
        m.R2 = sb("region2", [P, region])
        m.EX = sb("edge_values", [P, STEPS * HEADS])
        m.slots = sb("slots", [P, GROUP * D])
        m.WP = sb("w_project", [P, 2, 6 * D])
        m.Wo, m.Wout, m.Wmix = sb("w_o", [P, 2, D]), sb("w_out", [P, 2, D]), sb("w_mix", [P, 2, D])
        m.rows = sb("row_vectors", [P, 5, D])
        m.REL, m.SRC = sb("relative", [P, STEPS]), sb("source", [P, STEPS], I32)
        m.IDX = sb("index", [P, GROUP], I32)
        m.BT = sb("block_table", [1, STEPS], I32)
        m.ident, m.ones, m.upper = sb("ident", [P, P]), sb("ones", [P, P]), sb("upper", [P, P])
        m.iota_row, m.iota_col = sb("iota_row", [P, P]), sb("iota_col", [P, 1])
        m.bnst, m.stat, m.rstd = sb("bn", [P, NB, 6]), sb("stat", [P, NB, 2]), sb("rstd", [P, NB])
        m.eps, m.brc, m.b1c = sb("eps", [P, 1]), sb("brc", [P, 1]), sb("b1c", [P, 8])
        m.weight = sb("weight", [P, NB])
        dram = lambda n, shape, dt=F32: nc.dram_tensor(n, shape, dt, kind="Internal").ap()
        m.dst_rows, m.src_rows = dram("dst_rows", [TILES, P], I32), dram("src_rows", [TILES, P], I32)
        m.rel_rows, m.key_rows = dram("rel_rows", [STEPS, P]), dram("key_rows", [STEPS, P])
        m.step_block = dram("step_block", [STEPS], I32)
        m.q_d, m.k_d, m.v_d = (dram(n, [NB * P, D]) for n in ("q_rows", "k_rows", "v_rows"))
        m.xn_d, m.qs_d = dram("xn_rows", [NB * P, D]), dram("mix_q_rows", [NB * P, D])
        m.score_d, m.ex_d = dram("scores", [HEADS, STEPS * P]), dram("weights", [HEADS, STEPS * P])
        m.end_d = dram("piece_ends", [P, 4])
        for phase in (setup_phase, projection_phase, context_phase, score_phase, softmax_phase,
                      aggregate_phase, output_phase, feed_forward_phase)[:PHASES]:
            used = []
            m.sem = lambda name: used.append(nc.alloc_semaphore(name)) or used[-1]
            phase(nc, m, a)
            nc.clear_and_free_semaphores(used)
            nc.all_engine_barrier()


PHASES = 99
_INS = ["x", "src", "dst", "L0_gnn_Wq", "L0_gnn_Wk", "L0_gnn_Wv", "L0_gnn_Wo", "L0_gnn_gamma", "L0_gnn_beta",
        "L0_mix_Wqkv", "L0_mix_Wout", "L0_mix_gamma", "L0_ffn_attention_mask", "L0_ffn_wr", "L0_ffn_br",
        "L0_ffn_w1", "L0_ffn_b1", "L0_ffn_w2", "L0_ffn_b2"]


def kernel(**inputs):
    import concourse.bacc as bacc
    from concourse.bass_utils import run_bass_kernel_spmd

    nc = bacc.Bacc("TRN2", target_bir_lowering=False, num_devices=1)
    arrays, a = {}, Mem()
    for name in _INS:
        v = np.ascontiguousarray(inputs[name])
        arrays[f"in_{name}"] = v
        a.__dict__[name] = nc.dram_tensor(f"in_{name}", v.shape, mybir.dt.from_np(v.dtype), kind="ExternalInput").ap()
    a.out = nc.dram_tensor("out", (N, D), F32, kind="ExternalOutput").ap()
    build_program(nc, a)
    r = run_bass_kernel_spmd(nc, [arrays], core_ids=[0])
    return r.results[0]["out"]
```

```python
from contextlib import ExitStack

import numpy as np
import concourse.bass as bass
from concourse import mybir

F32 = mybir.dt.float32
I32 = mybir.dt.int32
ALU = mybir.AluOpType
ACT = mybir.ActivationFunctionType
AX = mybir.AxisListType.X

P = 128
N, D = 6250, 256
E = 100000
HEADS, DH = 8, 32
FF = 4 * D
NB = -(-N // P)
NLAST = N - (NB - 1) * P
TILES = -(-E // P)
ELAST = E - (TILES - 1) * P
GROUP = 16
STEPS = -(-(TILES + NB - 1) // GROUP) * GROUP
TURNS = STEPS // GROUP
SROWS = -(-STEPS // P)
CHUNKS = P // HEADS
CLEN = STEPS * P // CHUNKS
SCALE = float(DH) ** -0.5
KEEP = max(1, N // 2) - 1
EPS = 1e-5
BIG = 1e30
VW = D + 2
AW = D + HEADS


class Tally:

    def __init__(self, eng, sem):
        self.eng, self.sem, self.base, self.n, self.turn, self.per = eng, sem, 0, 0, None, 0

    def now(self):
        v = self.base + self.n
        return v if self.turn is None else self.turn * self.per + v

    def inc(self, ins):
        ins.then_inc(self.sem, 1)
        self.n += 1

    def wait(self):
        self.eng.wait_ge(self.sem, self.now())

    def link(self, ins):
        self.inc(ins)
        self.wait()

    def enter(self, turn, per):
        self.base, self.n, self.turn, self.per = self.base + self.n, 0, turn, per

    def leave(self, turns):
        assert self.n == self.per, (self.n, self.per)
        self.base, self.n, self.turn = self.base + turns * self.per, 0, None


class Mem:
    pass


def ds(start, size):
    return bass.ds(start, size)


def blocks_of(nc, m, engine, i, h):
    return nc.values_load_multi_w_load_instructions(
        m.BT[0:1, ds(i * GROUP + 8 * h, 8)], engines=bass.OrderedEngineSet([engine]), min_val=0, max_val=NB - 1,
        skip_runtime_bounds_check_because="a block is a sum of NB - 1 comparisons")[1]


def half_rows(d, i, h):
    return d[:, :].rearrange("h (s e) -> s h e", e=P)[ds((i * 2 + h) * (GROUP // 2), GROUP // 2), :, :]


def setup_phase(nc, m, a):
    X = m.R1[:, 0:NB * D].rearrange("p (b c) -> p b c", b=NB)
    at = [0]

    def take(n, dt=F32):
        at[0] += n
        v = m.R2[:, at[0] - n:at[0]]
        return v if dt is F32 else v.bitcast(dt)
    ENDI, ENDF = take(SROWS, I32), take(SROWS)
    BELOW = take(SROWS * NB).rearrange("p (r b) -> p r b", r=SROWS)
    CUT, BLK, START = take(NB), take(NB), take(NB)
    SID, BF, TF, OFF = (take(SROWS) for _ in range(4))
    TI, BI = take(SROWS, I32), take(SROWS, I32)
    PADI = take(P, I32)
    PASSED = take(SROWS * NB).rearrange("p (r b) -> p r b", r=SROWS)
    DROW, SROW, KEY, MASK, MASK2 = (take(SROWS * P).rearrange("p (r e) -> p r e", r=SROWS) for _ in range(5))
    DINT, SINT = (take(SROWS * P, I32).rearrange("p (r e) -> p r e", r=SROWS) for _ in range(2))
    last1 = lambda v: v.rearrange("p (r o) -> p r o", o=1)
    FULL = TILES - 1
    PARTS = 7
    each = NB // PARTS
    with ExitStack() as ctx:
        sem = lambda n: m.sem(n)
        PT = ctx.enter_context(nc.psum_tensor("PT", [P, 4, 512], F32))
        PC = ctx.enter_context(nc.psum_tensor("PC", [P, 512], F32))
        w_in, e_in, rows_in, end_set, end_in = (sem(n) for n in ("w_in", "e_in", "rows_in", "end_set", "end_in"))
        x_in = [sem(f"x_in{k}") for k in range(PARTS)]
        made, chain, counted, stat_var, stat_std = (sem(n) for n in (
            "const_made", "setup_chain", "counts_summed", "stat_var", "stat_std"))
        tiles_known, table_known, turned, table_out = (sem(n) for n in (
            "tiles_known", "table_known", "table_turned", "table_out"))
        pad_made, x_zeroed = sem("pad_made"), sem("x_zeroed")
        block = ctx.enter_context(nc.Block())

        @block.sync
        def _(sp):
            sp.wait_ge(end_set, 1)
            ends = a.dst[0:FULL * P].rearrange("(t e) -> t e", e=P)[:, P - 1:P]
            whole = FULL // P
            for r in range(whole + 1):
                n = min(P, FULL - r * P)
                sp.dma_start(ENDI[0:n, r:r + 1], ends[r * P:r * P + n, :],
                             allow_slow_non_contiguous=True).then_inc(end_in, 16)
            for k in range(PARTS - 1):
                sp.dma_start(X[:, k * each:(k + 1) * each, :],
                             a.x[k * each * P:(k + 1) * each * P, :].rearrange("(b p) c -> p b c", p=P)).then_inc(x_in[k], 16)
            k = PARTS - 1
            sp.dma_start(X[:, k * each:NB - 1, :],
                         a.x[k * each * P:(NB - 1) * P, :].rearrange("(b p) c -> p b c", p=P)).then_inc(x_in[k], 16)
            sp.wait_ge(x_zeroed, 1)
            sp.dma_start(X[0:NLAST, NB - 1, :], a.x[(NB - 1) * P:N, :]).then_inc(x_in[k], 16)
            sp.wait_ge(table_known, 1)
            for r in range(SROWS):
                n = min(P, STEPS - r * P)
                sp.dma_start(m.step_block[r * P:r * P + n].rearrange("(p o) -> p o", o=1),
                             BI[0:n, r:r + 1]).then_inc(table_out, 16)
                sp.dma_start(m.rel_rows[r * P:r * P + n, :], DROW[0:n, r, :]).then_inc(table_out, 16)
                sp.dma_start(m.key_rows[r * P:r * P + n, :], KEY[0:n, r, :]).then_inc(table_out, 16)
            sp.wait_ge(table_out, 48 * SROWS)
            sp.dma_start(m.BT[:, :], m.step_block[:].rearrange("(o s) -> o s", o=1)).then_inc(table_out, 16)
            sp.wait_ge(table_out, 48 * SROWS + 16)

        @block.gpsimd
        def _(pool):
            nc.gpsimd.memset(PADI[0:2, :], 0).then_inc(pad_made, 1)
            pool.wait_ge(pad_made, 1)
            nc.gpsimd.memset(PADI[0:1, :], NB * P).then_inc(pad_made, 1)
            nc.gpsimd.iota(SID, pattern=[[P, SROWS]], base=0, channel_multiplier=1,
                           allow_small_or_imprecise_dtypes=True).then_inc(made, 1)
            nc.gpsimd.iota(BLK, pattern=[[1, NB]], base=0, channel_multiplier=0,
                           allow_small_or_imprecise_dtypes=True).then_inc(made, 1)
            nc.gpsimd.iota(START, pattern=[[P, NB]], base=0, channel_multiplier=0,
                           allow_small_or_imprecise_dtypes=True).then_inc(made, 1)
            nc.gpsimd.memset(m.ident[:, :], 0.0).then_inc(made, 1)
            nc.gpsimd.memset(m.ones[:, :], 1.0).then_inc(made, 1)
            nc.gpsimd.memset(m.upper[:, :], 1.0).then_inc(made, 1)
            nc.gpsimd.iota(m.iota_row[:, :], pattern=[[1, P]], base=0, channel_multiplier=0,
                           allow_small_or_imprecise_dtypes=True).then_inc(made, 1)
            nc.gpsimd.iota(m.iota_col[:, :], pattern=[[0, 1]], base=0, channel_multiplier=1,
                           allow_small_or_imprecise_dtypes=True).then_inc(made, 1)
            pool.wait_ge(made, 8)
            nc.gpsimd.affine_select(out=m.ident[:, :], in_=m.ident[:, :], compare_op=ALU.not_equal, fill=1.0,
                                    base=0, pattern=[[-1, P]], channel_multiplier=1).then_inc(made, 1)
            nc.gpsimd.affine_select(out=m.upper[:, :], in_=m.upper[:, :], compare_op=ALU.is_ge, fill=0.0,
                                    base=0, pattern=[[1, P]], channel_multiplier=-1).then_inc(made, 1)
            pool.wait_ge(e_in, 96)
            pool.wait_ge(tiles_known, 1)
            for r in range(SROWS):
                for k, (out, rows) in enumerate(((DINT, m.dst_rows), (SINT, m.src_rows))):
                    nc.gpsimd.indirect_dma_start(
                        out=out[:, r, :], out_offset=None, in_=rows[:, :],
                        in_offset=bass.IndirectOffsetOnAxis(ap=TI[:, r:r + 1], axis=0)).then_inc(rows_in, 16)

        @block.scalar
        def _(act):
            cut = FULL * P
            one = lambda v: v.rearrange("(o p) -> o p", o=1)
            act.dma_start(m.dst_rows[0:FULL, :], a.dst[0:cut].rearrange("(t p) -> t p", p=P)).then_inc(e_in, 16)
            act.dma_start(m.src_rows[0:FULL, :], a.src[0:cut].rearrange("(t p) -> t p", p=P)).then_inc(e_in, 16)
            act.dma_start(one(m.dst_rows[FULL, 0:ELAST]), one(a.dst[cut:E])).then_inc(e_in, 16)
            act.dma_start(one(m.src_rows[FULL, 0:ELAST]), one(a.src[cut:E])).then_inc(e_in, 16)
            act.wait_ge(pad_made, 2)
            act.dma_start(one(m.dst_rows[FULL, ELAST:P]), PADI[0:1, 0:P - ELAST]).then_inc(e_in, 16)
            act.dma_start(one(m.src_rows[FULL, ELAST:P]), PADI[1:2, 0:P - ELAST]).then_inc(e_in, 16)
            full = lambda v: v.rearrange("(o c) -> o c", o=1).broadcast_to([P, D])
            mix = a.L0_mix_Wqkv.rearrange("(k p) n -> p k n", p=P)
            for out, src in (
                (m.WP[:, :, 0:256], a.L0_gnn_Wq.rearrange("(k p) n -> p k n", p=P)),
                (m.WP[:, :, 256:512], a.L0_gnn_Wk.rearrange("(k p) n -> p k n", p=P)),
                (m.WP[:, :, 512:768], mix[:, :, D:2 * D]),
                (m.WP[:, :, 768:1024], a.L0_gnn_Wv.rearrange("(k p) n -> p k n", p=P)),
                (m.WP[:, :, 1024:1280], mix[:, :, 0:D]),
                (m.WP[:, :, 1280:1536], mix[:, :, 2 * D:3 * D]),
                (m.Wo[:, :, :], a.L0_gnn_Wo.rearrange("(k p) n -> p k n", p=P)),
                (m.Wout[:, :, :], a.L0_mix_Wout.rearrange("(k p) n -> p k n", p=P)),
                (m.rows[:, 0, :], full(a.L0_gnn_gamma)), (m.rows[:, 1, :], full(a.L0_gnn_beta)),
                (m.rows[:, 2, :], full(a.L0_mix_gamma)), (m.rows[:, 3, :], full(a.L0_ffn_b2)),
                (m.rows[:, 4, :], a.L0_ffn_wr.rearrange("c o -> o c").broadcast_to([P, D])),
                (m.brc[:, :], a.L0_ffn_br.rearrange("(o c) -> o c", o=1).broadcast_to([P, 1])),
                (m.b1c[:, :], a.L0_ffn_b1.rearrange("(k p) -> p k", p=P)),
            ):
                act.dma_start(out, src, allow_slow_non_contiguous=True).then_inc(w_in, 16)
            act.wait_ge(stat_var, NB + 1)
            nc.scalar.activation(m.rstd[:, :], m.stat[:, :, 1], ACT.Sqrt, bias=m.eps[:, :]).then_inc(stat_std, 1)
            act.wait_ge(w_in, 16 * 15)

        @block.tensor
        def _(pe):
            pe.wait_ge(counted, 1)
            pe.wait_ge(made, 10)
            nc.tensor.matmul(PC[:, 0:NB], m.ones[:, :], CUT, start=True, stop=True).then_inc(counted, 1)
            pe.wait_ge(table_known, 1)
            for q, rows in enumerate((DROW, SROW)):
                for r in range(SROWS):
                    n = min(P, STEPS - r * P)
                    nc.tensor.transpose(PT[:, 2 * q + r // 4, (r % 4) * P:(r % 4) * P + n], rows[0:n, r, :],
                                        m.ident[0:n, 0:n]).then_inc(turned, 1)

        @block.vector
        def _(dve):
            t = Tally(dve, chain)
            wide = [P, SROWS, NB]
            nc.vector.memset(m.eps[:, :], EPS).then_inc(stat_var, 1)
            nc.vector.memset(ENDI, 4 * NB * P).then_inc(end_set, 1)
            nc.vector.memset(X[:, NB - 1, :], 0.0).then_inc(x_zeroed, 1)
            dve.wait_ge(end_in, 16 * (FULL // P + 1))
            dve.wait_ge(made, 3)
            t.link(nc.vector.tensor_copy(ENDF, ENDI))
            block_row = lambda v: v.rearrange("p (o b) -> p o b", o=1).broadcast_to(wide)
            t.link(nc.vector.tensor_tensor(BELOW, last1(ENDF).broadcast_to(wide), block_row(START), ALU.is_lt))
            nc.vector.tensor_reduce(CUT, BELOW.rearrange("p r b -> p b r"), AX, ALU.add).then_inc(counted, 1)
            dve.wait_ge(counted, 2)
            t.link(nc.vector.tensor_tensor(CUT, PC[:, 0:NB], BLK, ALU.add))
            t.link(nc.vector.tensor_tensor(PASSED, last1(SID).broadcast_to(wide), block_row(CUT), ALU.is_ge))
            t.link(nc.vector.tensor_reduce(BF, PASSED[:, :, 1:NB], AX, ALU.add))
            t.link(nc.vector.tensor_tensor(TF, SID, BF, ALU.subtract))
            t.link(nc.vector.tensor_scalar(OFF, TF, float(TILES - 1), 4.0 * NB * P, ALU.is_gt, ALU.mult))
            t.link(nc.vector.tensor_scalar(TF, TF, float(TILES - 1), None, ALU.min))
            t.link(nc.vector.tensor_copy(BI, BF))
            t.link(nc.vector.scalar_tensor_tensor(out=OFF, in0=BF, scalar=float(-P), in1=OFF, op0=ALU.mult, op1=ALU.add))
            nc.vector.tensor_copy(TI, TF).then_inc(tiles_known, 1)
            for b in range(NB):
                if b % each == 0:
                    dve.wait_ge(x_in[b // each], 32 if b // each == PARTS - 1 else 16)
                t.inc(nc.vector.bn_stats(m.bnst[:, b, :], X[:, b, :]))
            t.wait()
            for b in range(NB):
                nc.vector.bn_aggr(m.stat[:, b, :], m.bnst[:, b, :]).then_inc(stat_var, 1)
            dve.wait_ge(rows_in, 32 * SROWS)
            t.inc(nc.vector.tensor_copy(SROW, SINT))
            t.link(nc.vector.tensor_copy(KEY, DINT))
            t.link(nc.vector.tensor_tensor(DROW, KEY, last1(OFF).broadcast_to([P, SROWS, P]), ALU.add))
            t.inc(nc.vector.tensor_scalar(MASK, DROW, 0.0, None, ALU.is_ge))
            t.link(nc.vector.tensor_scalar(MASK2, DROW, float(P), None, ALU.is_lt))
            t.link(nc.vector.tensor_tensor(MASK, MASK, MASK2, ALU.mult))
            t.link(nc.vector.scalar_tensor_tensor(out=KEY, in0=KEY, scalar=1.0, in1=MASK, op0=ALU.add, op1=ALU.mult))
            nc.vector.tensor_scalar(KEY, KEY, -1.0, None, ALU.add).then_inc(table_known, 1)
            dve.wait_ge(turned, 2 * SROWS)
            for q, out in enumerate((m.REL, m.SRC)):
                t.inc(nc.vector.tensor_copy(out[:, 0:512], PT[:, 2 * q, :]))
                t.inc(nc.vector.tensor_copy(out[:, 512:STEPS], PT[:, 2 * q + 1, 0:STEPS - 512]))
            dve.wait_ge(stat_std, 1)
            t.link(nc.vector.reciprocal(m.rstd[:, :], m.rstd[:, :]))


def projection_phase(nc, m, a):
    X = m.R1[:, 0:NB * D]
    QB = m.R2[:, 0:NB * D]
    XN = m.slots[:, 0:2 * D].rearrange("p (u c) -> p u c", u=2)
    XT = m.slots[:, 512:512 + 2 * D].rearrange("p (u k t) -> p u k t", u=2, k=2)
    KS = m.slots[:, 1024:1024 + 2 * D].rearrange("p (u c) -> p u c", u=2)
    MK = m.slots[:, 1536:1536 + 2 * D].rearrange("p (u c) -> p u c", u=2)
    TOP = m.slots[:, 2048:2048 + D]
    TOPT = m.slots[:, 2304:2306]
    DIAG = m.slots[:, 2560:2560 + D].rearrange("p (k c) -> p k c", k=2)
    last = NB // 2
    with ExitStack() as ctx:
        sem = lambda n: [m.sem(f"{n}{u}") for u in range(2)]
        PX = ctx.enter_context(nc.psum_tensor("PX", [P, 2, 512], F32))
        PP = ctx.enter_context(nc.psum_tensor("PP", [P, 2, 2, 512], F32))
        xn_made, turned, xt_made, done, copied, maxed = (sem(n) for n in (
            "p_xn", "p_turned", "p_xt", "p_done", "p_copied", "p_maxed"))
        x_stored, x_free, k_stored = (sem(n) for n in ("p_xst", "p_xfree", "p_kst"))
        chain, top_turned, diag_made, spread = (m.sem(n) for n in ("p_chain", "p_topt", "p_diag", "p_spread"))
        block = ctx.enter_context(nc.Block())
        rows = lambda i, u: ds((i * 2 + u) * P, P)
        turned_rows = lambda v: v.rearrange("p k t -> p (k t)")

        @block.sync
        def _(sp):
            def store(i, u):
                sp.wait_ge(xn_made[u], i + 1)
                sp.dma_start(m.xn_d[rows(i, u), :], XN[:, u, :]).then_inc(x_stored[u], 16)
                sp.wait_ge(xt_made[u], i + 1)
                sp.dma_start(m.xt_d[rows(i, u), :], turned_rows(XT[:, u, :, :])).then_inc(x_stored[u], 16)

            def free(i, u):
                sp.wait_ge(x_stored[u], (i + 1) * 32)
                sp.sem_inc(x_free[u], 1)
            for u in range(2):
                sp.sem_inc(x_free[u], 1)
            store(0, 0)
            store(0, 1)
            free(0, 0)
            with sp.Fori(1, last) as i:
                store(i, 0)
                free(i - 1, 1)
                store(i, 1)
                free(i, 0)
            store(last, 0)
            sp.wait_ge(x_stored[0], (last + 1) * 32)
            sp.wait_ge(x_stored[1], last * 32)

        @block.scalar
        def _(act):
            def copy_x(i, u):
                act.wait_ge(turned[u], i + 1)
                act.wait_ge(x_free[u], i + 1)
                nc.scalar.activation(XT[:, u, :, :], PX[:, u, 0:D].rearrange("p (k t) -> p k t", k=2), ACT.Copy).then_inc(xt_made[u], 1)

            def copies(i, u, first=False):
                act.wait_ge(done[u], i + 1)
                nc.scalar.activation(QB[:, ds((i * 2 + u) * D, D)], PP[:, u, 0, 0:D], ACT.Copy).then_inc(copied[u], 1)
                if not first:
                    act.wait_ge(k_stored[u], i * 32)
                nc.scalar.activation(KS[:, u, :], PP[:, u, 0, D:2 * D], ACT.Copy).then_inc(copied[u], 1)
                if not first:
                    act.wait_ge(maxed[u], i + 0)
                nc.scalar.activation(MK[:, u, :], PP[:, u, 1, 0:D], ACT.Copy).then_inc(copied[u], 1)

            def store(i, u):
                act.wait_ge(copied[u], i * 3 + 3)
                act.dma_start(m.k_d[rows(i, u), :], KS[:, u, :]).then_inc(k_stored[u], 16)
                act.dma_start(m.mk_d[rows(i, u), :], MK[:, u, :]).then_inc(k_stored[u], 16)
            copy_x(0, 0)
            copy_x(0, 1)
            copies(0, 0, True)
            copy_x(1, 0)
            store(0, 0)
            copies(0, 1, True)
            with act.Fori(1, last) as i:
                copy_x(i, 1)
                store(i - 1, 1)
                copies(i, 0)
                copy_x(i + 1, 0)
                store(i, 0)
                copies(i, 1)
            store(last - 1, 1)
            copies(last, 0)
            store(last, 0)
            act.wait_ge(k_stored[0], (last + 1) * 32)
            act.wait_ge(k_stored[1], last * 32)

        @block.tensor
        def _(pe):
            def turn(i, u):
                pe.wait_ge(xn_made[u], i + 1)
                for k in range(2):
                    ins = nc.tensor.transpose(PX[:, u, k * P:(k + 1) * P], XN[:, u, k * P:(k + 1) * P], m.ident[:, :])
                ins.then_inc(turned[u], 1)

            def project(i, u, first=False):
                pe.wait_ge(xt_made[u], i + 1)
                if not first:
                    pe.wait_ge(copied[u], i * 3)
                for c, n in ((0, 512), (1, 256)):
                    for k in range(2):
                        ins = nc.tensor.matmul(PP[:, u, c, 0:n], XT[:, u, k, :], m.WP[:, k, c * 512:c * 512 + n],
                                               start=(k == 0), stop=(k == 1))
                ins.then_inc(done[u], 1)

            turn(0, 0)
            turn(0, 1)
            project(0, 0, True)
            turn(1, 0)
            project(0, 1, True)
            with pe.Fori(1, last) as i:
                turn(i, 1)
                project(i, 0)
                turn(i + 1, 0)
                project(i, 1)
            project(last, 0)
            pe.wait_ge(maxed[0], last + 1)
            for k in range(2):
                ins = nc.tensor.transpose(PX[:, 0, k * P:(k + 1) * P], TOP[:, k * P:(k + 1) * P], m.ident[:, :])
            ins.then_inc(top_turned, 1)
            pe.wait_ge(diag_made, 2)
            for k in range(2):
                ins = nc.tensor.matmul(PX[:, 1, k * P:(k + 1) * P], m.ones[:, :], DIAG[:, k, :], start=True, stop=True)
            ins.then_inc(spread, 1)

        @block.vector
        def _(dve):
            t = Tally(dve, chain)

            def normalise(i, u, first=False):
                dve.wait_ge(x_free[u], i + 1)
                if not first:
                    dve.wait_ge(turned[u], i + 0)
                b = i * 2 + u
                nc.vector.tensor_scalar(XN[:, u, :], X[:, ds(b * D, D)], m.stat[:, ds(b, 1), 0], m.rstd[:, ds(b, 1)],
                                        ALU.subtract, ALU.mult).then_inc(xn_made[u], 1)

            def maximum(i, u, n=P):
                dve.wait_ge(copied[u], i * 3 + 3)
                t.wait()
                t.inc(nc.vector.tensor_tensor(TOP[0:n, :], TOP[0:n, :], MK[0:n, u, :], ALU.max))
                t.wait()
                dve.sem_inc(maxed[u], 1)
            t.link(nc.vector.memset(TOP, -BIG))
            normalise(0, 0, True)
            normalise(0, 1, True)
            with dve.Fori(0, last - 1) as i:
                t.enter(i, 2)
                for u in range(2):
                    normalise(i + 1, u)
                    maximum(i, u)
                t.leave(last - 1)
            normalise(last, 0)
            maximum(last - 1, 0)
            maximum(last - 1, 1)
            maximum(last, 0, NLAST)
            dve.wait_ge(top_turned, 1)
            t.link(nc.vector.tensor_reduce(TOPT, PX[:, 0, 0:D].rearrange("p (k t) -> p k t", k=2), AX, ALU.max))
            for k in range(2):
                nc.vector.tensor_scalar(DIAG[:, k, :], m.ident[:, :], TOPT[:, k:k + 1], None, ALU.mult).then_inc(diag_made, 1)
            dve.wait_ge(spread, 1)
            t.link(nc.vector.tensor_copy(m.TOPB[:, :], PX[:, 1, 0:D]))


def score_phase(nc, m, a):
    QB = m.R2[:, 0:NB * D]
    KG = m.slots.rearrange("p (j c) -> p j c", j=GROUP)
    at = [0]

    def take(n):
        at[0] += n
        return m.R1[:, at[0] - n:at[0]]
    OH = take(16 * P).rearrange("p (h j e) -> p h j e", h=2, j=8)
    PR = take(1024).rearrange("p (g c) -> p g c", g=2)
    SC = take(P).rearrange("p (h n) -> p h n", h=2)
    ST = take(2 * P)[0:P // 2].rearrange("p (h e) -> p h e", h=2)
    XT = take(D).rearrange("p (k t) -> p k t", k=2)
    MK = take(D)
    VQ = take(2 * D)
    MV = take(2 * P + 2).rearrange("p (k w) -> p k w", k=2)
    KX = take(D)
    QM = take(D)
    QR = take(2 * HEADS).rearrange("p (s h) -> p s h", s=2)
    SUM = take(2 * P + 2).rearrange("p (k w) -> p k w", k=2)
    SAME, RDEN = take(P), take(2)
    CTX, CTXT = (take(2 * P).rearrange("p (k c) -> p k c", k=2) for _ in range(2))
    MIX = NB
    with ExitStack() as ctx:
        sem = lambda n: m.sem(n)
        PQ = ctx.enter_context(nc.psum_tensor("PQ", [P, 4, 512], F32))
        PT = ctx.enter_context(nc.psum_tensor("PTS", [P, 512], F32))
        PM = ctx.enter_context(nc.psum_tensor("PMX", [P, 2, 512], F32))
        PC = ctx.enter_context(nc.psum_tensor("PCX", [P, 512], F32))
        turned = [sem(f"s_turned{h}") for h in range(2)]
        copied = [sem(f"s_copied{h}") for h in range(2)]
        stored = [sem(f"s_stored{h}") for h in range(2)]
        passed = sem("s_passed")
        mulled, scored = sem("s_mulled"), sem("s_scored")
        idx_made = [sem(f"s_idx{h}") for h in range(2)]
        k_in = [sem(f"s_k{j}") for j in range(GROUP)]
        rel_in = [sem(f"s_rel{h}") for h in range(2)]
        hot = [sem(f"s_hot{h}") for h in range(2)]
        q_out = [sem(f"s_q{b}") for b in range(4)]
        xt_in, mk_in, projected, vq_made, mv_made, v_stored, qs_stored = (sem(n) for n in (
            "s_xt", "s_mk", "s_proj", "s_vq", "s_mv", "s_vst", "s_qst"))
        k_sub, k_exp, q_sub, q_exp, q_made, ctx_out, ctx_added = (sem(n) for n in (
            "s_ksub", "s_kexp", "s_qsub", "s_qexp", "s_qmade", "s_ctx", "s_ctxadd"))
        same, chain, ctx_made, ctx_turned, ctxt_made, m_made = (sem(n) for n in (
            "s_same", "s_chain", "s_cm", "s_ct", "s_ctt", "s_m"))
        block = ctx.enter_context(nc.Block())
        rows = lambda i: ds(i * P, P)

        @block.sync
        def _(sp):
            def load(i, h):
                sp.dma_start(OH[:, h, :, :], m.rel_rows[ds((i * 2 + h) * 8, 8), :].rearrange("(o s) e -> o s e", o=1)
                             .broadcast_to([P, 8, P])).then_inc(rel_in[h], 16)

            def load_block(i):
                sp.dma_start(XT.rearrange("p k t -> p (k t)"), m.xt_d[rows(i), :]).then_inc(xt_in, 16)
                sp.dma_start(MK, m.mk_d[rows(i), :]).then_inc(mk_in, 16)

            def turn(i, store, then):
                sp.wait_ge(q_out[3], i * 2 + 1)
                load(i + 1, 0)
                if store:
                    sp.wait_ge(vq_made, i + 1)
                    sp.dma_start(m.v_d[rows(i), :], VQ[:, 0:D]).then_inc(v_stored, 16)
                if then:
                    sp.wait_ge(projected, i + 1)
                    sp.wait_ge(k_sub, i + 1)
                    load_block(i + 1)
                sp.wait_ge(q_out[3], i * 2 + 2)
                load(i + 1, 1)
                if store:
                    sp.wait_ge(q_made, i + 1)
                    sp.dma_start(m.qs_d[rows(i), :], QM).then_inc(qs_stored, 16)
            load(0, 0)
            load(0, 1)
            load_block(0)
            with sp.Fori(0, MIX - 1) as i:
                turn(i, True, True)
            turn(MIX - 1, True, False)
            for i in range(MIX, TURNS - 1):
                turn(i, False, False)
            sp.wait_ge(v_stored, 16 * MIX)
            sp.wait_ge(qs_stored, 16 * MIX)

        @block.gpsimd
        def _(pool):
            nc.gpsimd.memset(SAME, 0.0).then_inc(same, 1)
            for g in range(P // DH):
                pool.wait_ge(same, g + 1)
                nc.gpsimd.memset(SAME[g * DH:(g + 1) * DH, g * DH:(g + 1) * DH], 1.0).then_inc(same, 1)

            def gather(i, first):
                for h in range(2):
                    pool.wait_ge(idx_made[h], i + 1)
                    for j in range(8 * h, 8 * h + 8):
                        if j % 2 == 0 and not first:
                            pool.wait_ge(mulled, i * 8 + j // 2 - 7)
                        if j % 2 == 0:
                            pool.sem_inc(passed, 1)
                        nc.gpsimd.indirect_dma_start(
                            out=KG[:, j, :], out_offset=None, in_=m.k_d[:, :],
                            in_offset=bass.IndirectOffsetOnAxis(ap=m.IDX[:, j:j + 1], axis=0)).then_inc(k_in[j], 16)
            gather(0, True)
            with pool.Fori(1, TURNS) as i:
                gather(i, False)

        @block.scalar
        def _(act):
            def store(i, h, first):
                act.wait_ge(turned[h], i + 1)
                if not first:
                    act.wait_ge(stored[h], i * 16)
                nc.scalar.activation(ST[:, h, :], PT[0:P // 2, h * P:(h + 1) * P], ACT.Copy).then_inc(copied[h], 1)
                act.wait_ge(copied[h], i + 1)
                act.dma_start(half_rows(m.score_d, i, h), ST[:, h, :]).then_inc(stored[h], 16)

            def mix(i, n, first):
                act.wait_ge(k_sub, i + 1)
                nc.scalar.activation(KX[0:n, :], KX[0:n, :], ACT.Exp).then_inc(k_exp, 1)
                act.wait_ge(projected, i + 1)
                if not first:
                    act.wait_ge(v_stored, i * 16)
                    act.wait_ge(q_sub, i + 0)
                nc.scalar.activation(VQ, PM[:, 0, :], ACT.Copy).then_inc(vq_made, 1)
                if not first:
                    act.wait_ge(ctx_out, i + 0)
                nc.scalar.activation(MV[:, :, 0:P], PM[:, 1, 0:D].rearrange("p (k c) -> p k c", k=2), ACT.Copy).then_inc(mv_made, 1)
                act.wait_ge(q_sub, i + 1)
                nc.scalar.activation(QM, QM, ACT.Exp).then_inc(q_exp, 1)
            mix(0, P, True)
            store(0, 0, True)
            mix(1, P, False)
            store(0, 1, True)
            store(1, 0, False)
            with act.Fori(2, MIX - 1) as i:
                mix(i, P, False)
                store(i - 1, 1, False)
                store(i, 0, False)
            mix(MIX - 1, NLAST, False)
            with act.Fori(MIX - 1, TURNS) as i:
                store(i - 1, 1, False)
                store(i, 0, False)
            store(TURNS - 1, 1, False)
            for h in range(2):
                act.wait_ge(stored[h], 16 * TURNS)

        @block.tensor
        def _(pe):
            def turn(i, h, first):
                pe.wait_ge(scored, i * 8 + 4 * h + 4)
                if h == 1:
                    pe.wait_ge(copied[0], i + 1)
                elif not first:
                    pe.wait_ge(copied[1], i + 0)
                pe.sem_inc(passed, 1)
                nc.tensor.transpose(PT[0:P // 2, h * P:(h + 1) * P], SC[:, h, :], m.ident[:, :]).then_inc(turned[h], 1)

            def project(i, first):
                pe.wait_ge(xt_in, i * 16 + 16)
                if not first:
                    pe.wait_ge(vq_made, i + 0)
                    pe.wait_ge(mv_made, i + 0)
                for c, n in ((0, 512), (1, 256)):
                    for k in range(2):
                        ins = nc.tensor.matmul(PM[:, c, 0:n], XT[:, k, :], m.WP[:, k, 768 + c * 512:768 + c * 512 + n],
                                               start=(k == 0), stop=(k == 1))
                ins.then_inc(projected, 1)

            def context(i, n, first):
                pe.wait_ge(k_exp, i + 1)
                pe.wait_ge(mv_made, i + 1)
                if not first:
                    pe.wait_ge(ctx_added, i + 1)
                for k in range(2):
                    ins = nc.tensor.matmul(PC[:, k * (P + 1):(k + 1) * (P + 1)], KX[0:n, k * P:(k + 1) * P], MV[0:n, k, :],
                                           start=True, stop=True)
                ins.then_inc(ctx_out, 1)

            def expand(i, first, n):
                for j in range(GROUP):
                    g = j // 2
                    if j % 8 == 0:
                        block_of = blocks_of(nc, m, mybir.EngineType.PE, i, j // 8)
                        pe.wait_ge(hot[j // 8], i + 1)
                    if j == 8 and not first:
                        turn(i - 1, 1, isinstance(i, int) and i == 1)
                    if j % 2 == 0 and (g >= 4 or not first):
                        pe.wait_ge(mulled, i * 8 + g - 3)
                    ins = nc.tensor.matmul(PQ[:, g % 4, (j % 2) * D:(j % 2 + 1) * D], OH[:, j // 8, j % 8, :],
                                           QB[:, ds(block_of[j % 8] * D, D)], start=True, stop=True)
                    if j % 2:
                        ins.then_inc(q_out[g % 4], 1)
                    if j == 3 and n:
                        project(i, first)
                    if j == 11 and n:
                        context(i, n, first)
                turn(i, 0, first)
            expand(0, True, P)
            expand(1, False, P)
            with pe.Fori(2, MIX - 1) as i:
                expand(i, False, P)
            expand(MIX - 1, False, NLAST)
            with pe.Fori(MIX, TURNS) as i:
                expand(i, False, 0)
            turn(TURNS - 1, 1, False)
            pe.wait_ge(ctx_made, 2)
            for k in range(2):
                ins = nc.tensor.transpose(PM[:, 0, k * P:(k + 1) * P], CTX[:, k, :], m.ident[:, :])
            ins.then_inc(ctx_turned, 1)
            pe.wait_ge(ctxt_made, 1)
            for k in range(2):
                ins = nc.tensor.matmul(PM[:, 1, k * D:(k + 1) * D], CTXT[:, k, :], m.Wout[:, k, :], start=True, stop=True)
            ins.then_inc(m_made, 1)

        @block.vector
        def _(dve):
            t = Tally(dve, chain)
            head = lambda x: x.rearrange("p (h d) -> p h d", h=HEADS)
            over = lambda x: x.rearrange("p (h o) -> p h o", o=1).broadcast_to([P, HEADS, DH])

            def hots(i, h):
                dve.wait_ge(rel_in[h], (i + 1) * 16)
                nc.vector.tensor_scalar(OH[:, h, :, :], OH[:, h, :, :], m.iota_col[:, 0:1], None, ALU.is_equal).then_inc(hot[h], 1)

            def index(i, h):
                nc.vector.tensor_copy(m.IDX[:, 8 * h:8 * h + 8], m.SRC[:, ds(i * GROUP + 8 * h, 8)]).then_inc(idx_made[h], 1)

            def multiply(i, g, first):
                dve.wait_ge(q_out[g % 4], i * 2 + g // 4 + 1)
                dve.wait_ge(k_in[2 * g], (i + 1) * 16)
                dve.wait_ge(k_in[2 * g + 1], (i + 1) * 16)
                if g >= 2 or not first:
                    dve.wait_ge(scored, i * 8 + g - 1)
                nc.vector.tensor_tensor(PR[:, g % 2, :], PQ[:, g % 4, :], KG[:, 2 * g:2 * g + 2, :].rearrange("p j c -> p (j c)"),
                                        ALU.mult).then_inc(mulled, 1)

            def add_up(i, g, first):
                dve.wait_ge(mulled, i * 8 + g + 1)
                if g % 4 == 0 and not first:
                    dve.wait_ge(turned[g // 4], i + 0)
                nc.vector.tensor_reduce(SC[:, g // 4, (g % 4) * 2 * HEADS:(g % 4 + 1) * 2 * HEADS],
                                        PR[:, g % 2, :].rearrange("p (n d) -> p n d", d=DH), AX, ALU.add).then_inc(scored, 1)

            def mix(i, g, first):
                if g == 0:
                    dve.wait_ge(mk_in, i * 16 + 16)
                    if not first:
                        dve.wait_ge(ctx_out, i + 0)
                    nc.vector.tensor_tensor(KX, MK, m.TOPB[:, :], ALU.subtract).then_inc(k_sub, 1)
                if g == 3:
                    dve.wait_ge(vq_made, i + 1)
                    t.link(nc.vector.tensor_reduce(QR[:, 0, :], head(VQ[:, D:2 * D]), AX, ALU.max))
                    if not first:
                        dve.wait_ge(qs_stored, i * 16)
                    nc.vector.tensor_tensor(head(QM), head(VQ[:, D:2 * D]), over(QR[:, 0, :]), ALU.subtract).then_inc(q_sub, 1)
                if g == 5:
                    dve.wait_ge(q_exp, i + 1)
                    t.link(nc.vector.tensor_reduce(QR[:, 1, :], head(QM), AX, ALU.add))
                    t.link(nc.vector.reciprocal(QR[:, 1, :], QR[:, 1, :]))
                    nc.vector.scalar_tensor_tensor(out=head(QM), in0=head(QM), scalar=SCALE, in1=over(QR[:, 1, :]),
                                                   op0=ALU.mult, op1=ALU.mult).then_inc(q_made, 1)
                if g == 7:
                    dve.wait_ge(ctx_out, i + 1)
                    dve.wait_ge(ctx_added, i + 1)
                    nc.vector.tensor_tensor(SUM, SUM, PC[:, 0:2 * P + 2].rearrange("p (k w) -> p k w", k=2),
                                            ALU.add).then_inc(ctx_added, 1)

            def turn(i, first, last, block):
                for g in range(8):
                    multiply(i, g, first)
                    if g == 1:
                        hots(i, 1)
                    if g:
                        add_up(i, g - 1, first)
                    if g == 4 and not last:
                        index(i + 1, 0)
                    if g == 5 and not last:
                        hots(i + 1, 0)
                    if block:
                        mix(i, g, first)
                add_up(i, 7, first)
                if not last:
                    index(i + 1, 1)
            index(0, 0)
            index(0, 1)
            nc.vector.memset(SUM, 0.0).then_inc(ctx_added, 1)
            t.link(nc.vector.memset(MV[:, :, P], 1.0))
            hots(0, 0)
            turn(0, True, False, True)
            with dve.Fori(1, MIX) as i:
                t.enter(i - 1, 3)
                turn(i, False, False, True)
                t.leave(MIX - 1)
            for i in range(MIX, TURNS):
                turn(i, False, i == TURNS - 1, False)
            dve.wait_ge(ctx_added, MIX + 1)
            for k in range(2):
                t.inc(nc.vector.reciprocal(RDEN[:, k:k + 1], SUM[:, k, P:P + 1]))
            t.wait()
            dve.wait_ge(same, P // DH + 1)
            for k in range(2):
                nc.vector.scalar_tensor_tensor(out=CTX[:, k, :], in0=SUM[:, k, 0:P], scalar=RDEN[:, k:k + 1], in1=SAME,
                                               op0=ALU.mult, op1=ALU.mult).then_inc(ctx_made, 1)
            dve.wait_ge(ctx_turned, 1)
            nc.vector.tensor_copy(CTXT, PM[:, 0, 0:D].rearrange("p (k t) -> p k t", k=2)).then_inc(ctxt_made, 1)
            dve.wait_ge(m_made, 1)
            t.link(nc.vector.tensor_copy(m.Wmix[:, :, :], PM[:, 1, :].rearrange("p (k c) -> p k c", k=2)))


def softmax_phase(nc, m, a):
    S, KEY = m.R1[:, 0:CLEN], m.R1[:, CLEN:2 * CLEN]
    CUT, M = m.R2[:, 0:CLEN + 1], m.R2[:, CLEN + 1:2 * CLEN + 1]
    END = m.slots[:, 1024:1028]
    ENDS = m.slots[:, 1088:1088 + 4 * CHUNKS]
    MSK = m.slots[:, 1280:1280 + 2 * CHUNKS]
    TOP = m.slots[:, 1344:1346]
    with ExitStack() as ctx:
        sem = lambda n: m.sem(n)
        s_in, key_in, end_made, end_out, ends_in = (sem(n) for n in ("m_sin", "m_kin", "m_end", "m_eout", "m_ein"))
        chain, diff, exped, ex_out = (sem(n) for n in ("m_chain", "m_diff", "m_exp", "m_xout"))
        block = ctx.enter_context(nc.Block())

        @block.sync
        def _(sp):
            for h in range(HEADS):
                sp.dma_start(KEY[h * CHUNKS:(h + 1) * CHUNKS, :],
                             m.key_rows[:, :].rearrange("s e -> (s e)").rearrange("(c l) -> c l", c=CHUNKS)).then_inc(key_in, 16)
            sp.dma_start(S, m.score_d[:, :].rearrange("h (c l) -> (h c) l", c=CHUNKS)).then_inc(s_in, 16)
            sp.wait_ge(end_made, 2)
            sp.dma_start(m.end_d[:, :], END).then_inc(end_out, 16)
            sp.wait_ge(end_out, 16)
            for h in range(HEADS):
                sp.dma_start(ENDS[h * CHUNKS:(h + 1) * CHUNKS, :],
                             m.end_d[h * CHUNKS:(h + 1) * CHUNKS, :].rearrange("c k -> (c k)").rearrange("(o n) -> o n", o=1)
                             .broadcast_to([CHUNKS, 4 * CHUNKS])).then_inc(ends_in, 16)
            sp.wait_ge(exped, 1)
            sp.dma_start(m.ex_d[:, :].rearrange("h (c l) -> (h c) l", c=CHUNKS), S).then_inc(ex_out, 16)
            sp.wait_ge(ex_out, 16)

        @block.scalar
        def _(act):
            act.wait_ge(diff, 1)
            nc.scalar.activation(S, S, ACT.Exp, scale=SCALE).then_inc(exped, 1)

        @block.vector
        def _(dve):
            t = Tally(dve, chain)
            dve.wait_ge(key_in, 16 * HEADS)
            t.inc(nc.vector.memset(CUT[:, 0:1], -BIG))
            t.inc(nc.vector.memset(CUT[:, CLEN:CLEN + 1], -BIG))
            t.link(nc.vector.tensor_tensor(CUT[:, 1:CLEN], KEY[:, 1:CLEN], KEY[:, 0:CLEN - 1], ALU.not_equal))
            t.link(nc.vector.tensor_scalar(CUT[:, 1:CLEN], CUT[:, 1:CLEN], -BIG, None, ALU.mult))
            dve.wait_ge(s_in, 16)
            t.link(nc.vector.tensor_tensor_scan(M, CUT[:, 0:CLEN], S, -BIG, ALU.add, ALU.max))
            t.link(nc.vector.tensor_tensor_scan(M[:, ::-1], CUT[:, 1:CLEN + 1][:, ::-1], M[:, ::-1], -BIG, ALU.add, ALU.max))
            nc.vector.tensor_copy(END[:, 0:2], M[:, 0:CLEN:CLEN - 1]).then_inc(end_made, 1)
            nc.vector.tensor_copy(END[:, 2:4], KEY[:, 0:CLEN:CLEN - 1]).then_inc(end_made, 1)
            dve.wait_ge(ends_in, 16 * HEADS)
            ends = ENDS.rearrange("p (c v k) -> p c v k", v=2, k=2)
            msk = MSK.rearrange("p (c k) -> p c k", k=2)
            for e in range(2):
                t.link(nc.vector.tensor_scalar(msk, ends[:, :, 1, :], END[:, 2 + e:3 + e], -BIG, ALU.not_equal, ALU.mult))
                t.link(nc.vector.tensor_tensor(msk, msk, ends[:, :, 0, :], ALU.add))
                t.link(nc.vector.tensor_reduce(TOP[:, e:e + 1], MSK, AX, ALU.max))
            for e in range(2):
                t.link(nc.vector.tensor_scalar(CUT[:, 0:CLEN], KEY, END[:, 2 + e:3 + e], -BIG, ALU.not_equal, ALU.mult))
                t.link(nc.vector.scalar_tensor_tensor(out=M, in0=CUT[:, 0:CLEN], scalar=TOP[:, e:e + 1], in1=M,
                                                      op0=ALU.add, op1=ALU.max))
            nc.vector.tensor_tensor(S, S, M, ALU.subtract).then_inc(diff, 1)


def aggregate_phase(nc, m, a):
    ACC = m.R1
    VG = m.slots.rearrange("p (j c) -> p j c", j=GROUP)
    OH = m.R2[:, 0:16 * P].rearrange("p (h j e) -> p h j e", h=2, j=8)
    WV = m.R2[:, 2048:2048 + GROUP * AW].rearrange("p (j c) -> p j c", j=GROUP)
    XT = m.R2[0:P // 2, 6400:6400 + 2 * P].rearrange("p (h e) -> p h e", h=2)
    EX = m.R2[:, 6656:6656 + P].rearrange("p (h n) -> p h n", h=2)
    with ExitStack() as ctx:
        sem = lambda n: m.sem(n)
        PA = ctx.enter_context(nc.psum_tensor("PACC", [P, 4, 512], F32))
        PT = ctx.enter_context(nc.psum_tensor("PTG", [P, 2, 512], F32))
        passed = sem("g_passed")
        x_in = [sem(f"g_xin{h}") for h in range(2)]
        turned = [sem(f"g_turned{h}") for h in range(2)]
        zeroed, mulled, hot, summed, added = (sem(n) for n in ("g_zero", "g_mulled", "g_hot", "g_summed", "g_added"))
        idx_made = [sem(f"g_idx{h}") for h in range(2)]
        v_in = [sem(f"g_v{j}") for j in range(GROUP)]
        w_made = [sem(f"g_w{h}") for h in range(2)]
        block = ctx.enter_context(nc.Block())

        @block.gpsimd
        def _(pool):
            def gather(i, first):
                for h in range(2):
                    pool.wait_ge(idx_made[h], i + 1)
                    for j in range(8 * h, 8 * h + 8):
                        if j % 2 == 0 and not first:
                            pool.wait_ge(mulled, i * 8 + j // 2 - 7)
                        if j % 2 == 0:
                            pool.sem_inc(passed, 1)
                        nc.gpsimd.indirect_dma_start(
                            out=VG[:, j, :], out_offset=None, in_=m.v_d[:, :],
                            in_offset=bass.IndirectOffsetOnAxis(ap=m.IDX[:, j:j + 1], axis=0)).then_inc(v_in[j], 16)
            gather(0, True)
            with pool.Fori(1, TURNS) as i:
                gather(i, False)

        @block.sync
        def _(sp):
            def load(i, h):
                sp.dma_start(XT[:, h, :], half_rows(m.ex_d, i, h)).then_inc(x_in[h], 16)
            load(0, 0)
            load(0, 1)
            with sp.Fori(0, TURNS - 1) as i:
                for h in range(2):
                    sp.wait_ge(turned[h], i + 1)
                    load(i + 1, h)

        @block.scalar
        def _(act):
            def weights(i, h, first):
                act.wait_ge(turned[h], i + 1)
                if not first:
                    act.wait_ge(mulled, i * 8 + 4 * h - 4)
                    act.wait_ge(summed, i * GROUP + 8 * h - 8)
                nc.scalar.activation(EX[:, h, :], PT[:, h, 0:P // 2], ACT.Copy).then_inc(w_made[h], 1)
                nc.scalar.activation(WV[:, 8 * h:8 * h + 8, D:AW], PT[:, h, 0:P // 2].rearrange("p (j h) -> p j h", j=8),
                                     ACT.Copy).then_inc(w_made[h], 1)
            weights(0, 0, True)
            weights(0, 1, True)
            with act.Fori(1, TURNS) as i:
                weights(i, 0, False)
                weights(i, 1, False)

        @block.tensor
        def _(pe):
            def turn(i, h, first):
                pe.wait_ge(x_in[h], (i + 1) * 16)
                if not first:
                    pe.wait_ge(w_made[h], i * 2)
                pe.sem_inc(passed, 1)
                nc.tensor.transpose(PT[:, h, 0:P // 2], XT[:, h, :], m.ident[0:P // 2, 0:P // 2]).then_inc(turned[h], 1)

            def sums(i, first, last):
                for j in range(GROUP):
                    if j % 8 == 0:
                        pe.wait_ge(hot, i * 2 + j // 8 + 1)
                        pe.wait_ge(w_made[j // 8], i * 2 + 2)
                    if j == 8 and not last:
                        turn(i + 1, 0, False)
                    if j % 2 == 0:
                        pe.wait_ge(mulled, i * 8 + j // 2 + 1)
                    if j >= 4 or not first:
                        pe.wait_ge(added, i * GROUP + j - 3)
                    nc.tensor.matmul(PA[:, j % 4, 0:AW], OH[:, j // 8, j % 8, :], WV[:, j, :],
                                     start=True, stop=True).then_inc(summed, 1)
                if not last:
                    turn(i + 1, 1, False)
            turn(0, 0, True)
            turn(0, 1, True)
            sums(0, True, False)
            with pe.Fori(1, TURNS - 1) as i:
                sums(i, False, False)
            sums(TURNS - 1, False, True)

        @block.vector
        def _(dve):
            def index(i, h):
                nc.vector.tensor_copy(m.IDX[:, 8 * h:8 * h + 8], m.SRC[:, ds(i * GROUP + 8 * h, 8)]).then_inc(idx_made[h], 1)

            def hots(i, h):
                nc.vector.tensor_tensor(OH[:, h, :, :], m.iota_row[:, :].rearrange("p (o n) -> p o n", o=1).broadcast_to([P, 8, P]),
                                        m.REL[:, ds(i * GROUP + 8 * h, 8)].rearrange("p (j o) -> p j o", o=1).broadcast_to([P, 8, P]),
                                        ALU.is_equal).then_inc(hot, 1)

            def multiply(i, g):
                dve.wait_ge(v_in[2 * g], (i + 1) * 16)
                dve.wait_ge(v_in[2 * g + 1], (i + 1) * 16)
                if g % 4 == 0:
                    dve.wait_ge(w_made[g // 4], i * 2 + 2)
                nc.vector.tensor_tensor(
                    WV[:, 2 * g:2 * g + 2, 0:D].rearrange("p j (h d) -> p j h d", d=DH),
                    VG[:, 2 * g:2 * g + 2, :].rearrange("p j (h d) -> p j h d", d=DH),
                    EX[:, g // 4, (g % 4) * 2 * HEADS:(g % 4 + 1) * 2 * HEADS].rearrange("p (j h o) -> p j h o", j=2, o=1)
                    .broadcast_to([P, 2, HEADS, DH]), ALU.mult).then_inc(mulled, 1)

            def add(i, j, b, first):
                dve.wait_ge(summed, i * GROUP + j + 1)
                if j or not first:
                    dve.wait_ge(added, i * GROUP + j)
                nc.vector.tensor_tensor(ACC[:, ds(b * AW, AW)], ACC[:, ds(b * AW, AW)], PA[:, j % 4, 0:AW],
                                        ALU.add).then_inc(added, 1)

            def turn(i, first, last):
                for g in range(8):
                    if g == 0:
                        hots(i, 1)
                    multiply(i, g)
                    if g % 4 == 1:
                        block_of = blocks_of(nc, m, mybir.EngineType.DVE, i, g // 4)
                    if g:
                        add(i, 2 * g - 2, block_of[(2 * g - 2) % 8], first)
                        add(i, 2 * g - 1, block_of[(2 * g - 1) % 8], first)
                    if g == 4 and not last:
                        index(i + 1, 0)
                        hots(i + 1, 0)
                if not last:
                    index(i + 1, 1)
                add(i, GROUP - 2, block_of[6], False)
                add(i, GROUP - 1, block_of[7], False)
            nc.vector.memset(ACC[:, 0:NB * AW], 0.0).then_inc(zeroed, 1)
            dve.wait_ge(zeroed, 1)
            index(0, 0)
            index(0, 1)
            hots(0, 0)
            turn(0, True, False)
            with dve.Fori(1, TURNS - 1) as i:
                turn(i, False, False)
            turn(TURNS - 1, False, True)


def output_phase(nc, m, a):
    ACC = m.R1
    XT = m.R2[:, 0:2 * NB * P].rearrange("p (k t) -> p k t", k=2)
    SL = m.slots
    XI = SL[:, 0:2 * D].rearrange("p (u c) -> p u c", u=2)
    NI = SL[:, 512:512 + 2 * D].rearrange("p (u c) -> p u c", u=2)
    AI = SL[:, 1024:1024 + 4 * D].rearrange("p (u c) -> p u c", u=2)
    AT = SL[:, 2048:2048 + 4 * D].rearrange("p (u k t) -> p u k t", u=2, k=4)
    Y = m.EX[:, 0:2 * D].rearrange("p (u c) -> p u c", u=2)
    G = m.EX[:, 512:512 + 2 * D].rearrange("p (u c) -> p u c", u=2)
    H = m.EX[:, 1024:1024 + 2 * D].rearrange("p (u c) -> p u c", u=2)
    X1 = m.EX[:, 1536:1536 + 2 * D].rearrange("p (u c) -> p u c", u=2)
    X2 = m.EX[:, 2048:2048 + 2 * D].rearrange("p (u c) -> p u c", u=2)
    JUNK = m.EX[:, 2560:2560 + D]
    DEN = m.EX[:, 2816:2816 + 2 * HEADS].rearrange("p (u h) -> p u h", u=2)
    BST = m.EX[:, 2880:2880 + 36].rearrange("p (u k c) -> p u k c", u=2, k=3)
    ST = m.EX[:, 2944:2944 + 12].rearrange("p (u k c) -> p u k c", u=2, k=3)
    SD = m.EX[:, 2976:2976 + 8].rearrange("p (u k) -> p u k", u=2)
    with ExitStack() as ctx:
        sem = lambda n: [m.sem(f"{n}{u}") for u in range(2)]
        PT = ctx.enter_context(nc.psum_tensor("POT", [P, 2, 512], F32))
        PO = ctx.enter_context(nc.psum_tensor("POO", [P, 2, 512], F32))
        PX = ctx.enter_context(nc.psum_tensor("POX", [P, 2, 512], F32))
        x_in, at_made, turned, at_copied, o_made = (sem(n) for n in ("o_xin", "o_at", "o_turned", "o_copied", "o_made"))
        n_in, q_in = sem("o_nin"), sem("o_qin")
        var1, std1, var2, std2 = (sem(n) for n in ("o_var1", "o_std1", "o_var2", "o_std2"))
        x2_made, x2_turned, x2_copied = (sem(n) for n in ("o_x2", "o_x2t", "o_x2c"))
        chain, passed = m.sem("o_chain"), m.sem("o_passed")
        block = ctx.enter_context(nc.Block())
        last = NB // 2
        rows = lambda i, u: ds((i * 2 + u) * P, P)

        @block.sync
        def _(sp):
            def load(i, u, n):
                sp.dma_start(NI[:, u, :], m.xn_d[rows(i, u), :]).then_inc(n_in[u], 16)
                sp.dma_start(AI[:, u, D:2 * D], m.qs_d[rows(i, u), :]).then_inc(q_in[u], 16)
                sp.dma_start(XI[0:n, u, :], a.x[ds((i * 2 + u) * P, n), :]).then_inc(x_in[u], 16)
            load(0, 0, P)
            load(0, 1, P)
            with sp.Fori(0, last - 1) as i:
                for u in range(2):
                    sp.wait_ge(x2_made[u], i + 1)
                    load(i + 1, u, P)
            sp.wait_ge(x2_made[0], last)
            load(last, 0, NLAST)

        @block.scalar
        def _(act):
            def copy_a(i, u):
                act.wait_ge(turned[u], i + 1)
                nc.scalar.activation(AT[:, u, :, :], PT[:, u, :].rearrange("p (k t) -> p k t", k=4), ACT.Copy).then_inc(at_copied[u], 1)

            def root(i, u):
                act.wait_ge(var1[u], i + 1)
                nc.scalar.activation(SD[:, u, 0:2], ST[:, u, 0:2, 1], ACT.Sqrt, bias=m.eps[:, :]).then_inc(std1[u], 1)

            def root2(i, u):
                act.wait_ge(var2[u], i + 1)
                nc.scalar.activation(SD[:, u, 2:3], ST[:, u, 2, 1:2], ACT.Sqrt, bias=m.eps[:, :]).then_inc(std2[u], 1)

            def copy_x(i, u):
                act.wait_ge(x2_turned[u], i + 1)
                nc.scalar.activation(XT[:, :, ds((i * 2 + u) * P, P)], PX[:, u, 0:D].rearrange("p (k t) -> p k t", k=2),
                                     ACT.Copy).then_inc(x2_copied[u], 1)
            copy_a(0, 0)
            with act.Fori(0, last) as i:
                root(i, 0)
                copy_a(i, 1)
                root2(i, 0)
                copy_x(i, 0)
                root(i, 1)
                copy_a(i + 1, 0)
                root2(i, 1)
                copy_x(i, 1)
            root(last, 0)
            root2(last, 0)
            copy_x(last, 0)

        @block.tensor
        def _(pe):
            def attend(i, u, first):
                pe.wait_ge(at_made[u], i + 1)
                pe.wait_ge(q_in[u], (i + 1) * 16)
                for k in range(4):
                    ins = nc.tensor.transpose(PT[:, u, k * P:(k + 1) * P], AI[:, u, k * P:(k + 1) * P], m.ident[:, :])
                ins.then_inc(turned[u], 1)
                pe.wait_ge(at_copied[u], i + 1)
                for w, c in ((m.Wo, 0), (m.Wmix, 1)):
                    for k in range(2):
                        ins = nc.tensor.matmul(PO[:, u, c * D:(c + 1) * D], AT[:, u, 2 * c + k, :], w[:, k, :],
                                               start=(k == 0), stop=(k == 1))
                ins.then_inc(o_made[u], 1)

            def turn_x(i, u, first):
                pe.wait_ge(x2_made[u], i + 1)
                if not first:
                    pe.wait_ge(x2_copied[u], i + 0)
                for k in range(2):
                    ins = nc.tensor.transpose(PX[:, u, k * P:(k + 1) * P], X2[:, u, k * P:(k + 1) * P], m.ident[:, :])
                ins.then_inc(x2_turned[u], 1)
            attend(0, 0, True)
            attend(0, 1, True)
            turn_x(0, 0, True)
            attend(1, 0, False)
            turn_x(0, 1, True)
            with pe.Fori(1, last) as i:
                attend(i, 1, False)
                turn_x(i, 0, False)
                attend(i + 1, 0, False)
                turn_x(i, 1, False)
            turn_x(last, 0, False)

        @block.vector
        def _(dve):
            t = Tally(dve, chain)

            def attention(i, u):
                b = i * 2 + u
                if not isinstance(i, int) or i:
                    dve.wait_ge(turned[u], i + 0)
                t.link(nc.vector.tensor_scalar(DEN[:, u, :], ACC[:, ds(b * AW + D, HEADS)], 1e-9, None, ALU.add))
                t.link(nc.vector.reciprocal(DEN[:, u, :], DEN[:, u, :]))
                nc.vector.tensor_tensor(AI[:, u, 0:D].rearrange("p (h d) -> p h d", d=DH),
                                        ACC[:, ds(b * AW, D)].rearrange("p (h d) -> p h d", d=DH),
                                        DEN[:, u, :].rearrange("p (h o) -> p h o", o=1).broadcast_to([P, HEADS, DH]),
                                        ALU.mult).then_inc(at_made[u], 1)

            def norms(i, u):
                dve.wait_ge(o_made[u], i + 1)
                dve.wait_ge(n_in[u], (i + 1) * 16)
                dve.wait_ge(x_in[u], (i + 1) * 16)
                mix = PO[:, u, D:2 * D]
                t.inc(nc.vector.tensor_tensor(Y[:, u, :], PO[:, u, 0:D], NI[:, u, :], ALU.add))
                t.link(nc.vector.bn_stats(BST[:, u, 1, :], mix))
                t.link(nc.vector.bn_stats(BST[:, u, 0, :], Y[:, u, :]))
                t.inc(nc.vector.tensor_tensor(X1[:, u, :], XI[:, u, :], m.rows[:, 1, :], ALU.add))
                t.inc(nc.vector.bn_aggr(ST[:, u, 0, :], BST[:, u, 0, :]))
                nc.vector.bn_aggr(ST[:, u, 1, :], BST[:, u, 1, :]).then_inc(var1[u], 1)
                t.wait()
                dve.wait_ge(var1[u], i + 1)
                t.inc(nc.vector.scalar_tensor_tensor(out=G[:, u, :], in0=Y[:, u, :], scalar=ST[:, u, 0, 0:1], in1=m.rows[:, 0, :],
                                                     op0=ALU.subtract, op1=ALU.mult))
                t.inc(nc.vector.scalar_tensor_tensor(out=H[:, u, :], in0=mix, scalar=ST[:, u, 1, 0:1], in1=m.rows[:, 2, :],
                                                     op0=ALU.subtract, op1=ALU.mult))
                dve.wait_ge(std1[u], i + 1)
                t.link(nc.vector.reciprocal(SD[:, u, 0:2], SD[:, u, 0:2]))
                t.link(nc.vector.scalar_tensor_tensor(out=G[:, u, :], in0=G[:, u, :], scalar=SD[:, u, 0:1], in1=X1[:, u, :],
                                                      op0=ALU.mult, op1=ALU.add))
                t.link(nc.vector.scalar_tensor_tensor(out=X1[:, u, :], in0=H[:, u, :], scalar=SD[:, u, 1:2], in1=G[:, u, :],
                                                      op0=ALU.mult, op1=ALU.add))
                t.link(nc.vector.bn_stats(BST[:, u, 2, :], X1[:, u, :]))
                dve.sem_inc(passed, 1)
                nc.vector.bn_aggr(ST[:, u, 2, :], BST[:, u, 2, :]).then_inc(var2[u], 1)

            def router(i, u):
                b = i * 2 + u
                dve.wait_ge(std2[u], i + 1)
                dve.wait_ge(var2[u], i + 1)
                if not isinstance(i, int) or i:
                    dve.wait_ge(x2_turned[u], i + 0)
                t.link(nc.vector.reciprocal(SD[:, u, 2:3], SD[:, u, 2:3]))
                nc.vector.tensor_scalar(X2[:, u, :], X1[:, u, :], ST[:, u, 2, 0:1], SD[:, u, 2:3],
                                        ALU.subtract, ALU.mult).then_inc(x2_made[u], 1)
                dve.wait_ge(x2_made[u], i + 1)
                t.inc(nc.vector.tensor_tensor(ACC[:, ds(b * AW, D)], X1[:, u, :], X2[:, u, :], ALU.add))
                t.link(nc.vector.tensor_tensor_reduce(out=JUNK, in0=X2[:, u, :], in1=m.rows[:, 4, :], scale=1.0, scalar=0.0,
                                                      op0=ALU.mult, op1=ALU.add, accum_out=SD[:, u, 3:4]))
                t.link(nc.vector.tensor_copy(m.weight[:, ds(b, 1)], SD[:, u, 3:4]))
            each = 2 + 11 + 4
            attention(0, 0)
            attention(0, 1)
            norms(0, 0)
            router(0, 0)
            attention(1, 0)
            norms(0, 1)
            router(0, 1)
            with dve.Fori(1, last) as i:
                t.enter(i - 1, 2 * each)
                attention(i, 1)
                norms(i, 0)
                router(i, 0)
                attention(i + 1, 0)
                norms(i, 1)
                router(i, 1)
                t.leave(last - 1)
            norms(last, 0)
            router(last, 0)
            t.link(nc.vector.tensor_scalar(m.weight[:, :], m.weight[:, :], m.brc[:, 0:1], None, ALU.add))


def feed_forward_phase(nc, m, a):
    BASE = m.R1
    XT = m.R2[:, 0:2 * NB * P].rearrange("p (k t) -> p k t", k=2)
    W1 = m.slots[:, 0:2 * FF].rearrange("p (k n) -> p k n", k=2)
    W2 = m.slots[:, 2 * FF:4 * FF].rearrange("p (c n) -> p c n", c=8)
    HT = m.EX[:, 0:8 * 512].rearrange("p (c t) -> p c t", c=8)
    TMP = m.EX[:, 4096:4096 + 4 * D].rearrange("p (u c) -> p u c", u=4)
    S = [m.EX[:, 5120 + 64 * k:5120 + 64 * k + NB] for k in range(10)]
    HI, LO, NEG, SGN, KEY, T1, T2, SEL, TIE, COEF = S
    C = m.EX[:, 5824:5856]
    U32 = mybir.dt.uint32
    groups = NB // 4
    with ExitStack() as ctx:
        sem = lambda n: m.sem(n)
        PH = ctx.enter_context(nc.psum_tensor("PFH", [P, 3, 512], F32))
        PY = ctx.enter_context(nc.psum_tensor("PFY", [P, 4, 512], F32))
        PS = ctx.enter_context(nc.psum_tensor("PFS", [P, 512], F32))
        w_in, chain, counted, total, ties, ranked = (sem(n) for n in ("f_win", "f_chain", "f_cnt", "f_tot", "f_ties", "f_rank"))
        h_made, h_act, y_made, y_out, stored, tmp_made = (sem(n) for n in ("f_h", "f_act", "f_y", "f_yo", "f_st", "f_tmp"))
        block = ctx.enter_context(nc.Block())

        @block.sync
        def _(sp):
            sp.dma_start(W1, a.L0_ffn_w1.rearrange("(k p) n -> p k n", p=P)).then_inc(w_in, 16)
            sp.dma_start(W2, a.L0_ffn_w2.rearrange("(c p) n -> p c n", p=P)).then_inc(w_in, 16)
            with sp.Fori(0, NB - 1) as b:
                sp.wait_ge(y_out, b + 1)
                sp.dma_start(a.out[ds(b * P, P), :], BASE[:, ds(b * AW, D)]).then_inc(stored, 16)
            sp.wait_ge(y_out, NB)
            sp.dma_start(a.out[(NB - 1) * P:N, :], BASE[0:NLAST, (NB - 1) * AW:(NB - 1) * AW + D]).then_inc(stored, 16)
            sp.wait_ge(stored, 16 * NB)

        @block.scalar
        def _(act):
            def group(i):
                for c in range(8):
                    act.wait_ge(h_made, i * 8 + c + 1)
                    nc.scalar.activation(HT[:, c, :], PH[:, c % 3, :], ACT.Gelu_apprx_tanh, bias=m.b1c[:, c:c + 1]).then_inc(h_act, 1)
            with act.Fori(0, groups) as i:
                group(i)
            for c in range(8):
                act.wait_ge(h_made, groups * 8 + c + 1)
                nc.scalar.activation(HT[:, c, 0:P], PH[:, c % 3, 0:P], ACT.Gelu_apprx_tanh, bias=m.b1c[:, c:c + 1]).then_inc(h_act, 1)

        @block.tensor
        def _(pe):
            with pe.Fori(0, 32) as r:
                pe.wait_ge(counted, r + 1)
                nc.tensor.matmul(PS[:, 0:1], m.ones[:, :], C[:, 3:4], start=True, stop=True).then_inc(total, 1)
            pe.wait_ge(ties, 1)
            nc.tensor.matmul(PS[:, 64:64 + NB], m.ones[:, :], SEL, start=True, stop=True)
            nc.tensor.matmul(PS[:, 128:128 + NB], m.upper[:, :], TIE, start=True, stop=True)
            nc.tensor.matmul(PS[:, 192:192 + NB], m.ones[:, :], TIE, start=True, stop=True).then_inc(ranked, 1)
            pe.wait_ge(w_in, 32)

            def group(i, blocks, first):
                n = blocks * P
                for c in range(8):
                    if c >= 3 or not first:
                        pe.wait_ge(h_act, i * 8 + c - 2)
                    for k in range(2):
                        ins = nc.tensor.matmul(PH[:, c % 3, 0:n], W1[:, k, c * P:(c + 1) * P], XT[:, k, ds(i * 4 * P, n)],
                                               start=(k == 0), stop=(k == 1))
                    ins.then_inc(h_made, 1)
                pe.wait_ge(h_act, i * 8 + 8)
                for b in range(blocks):
                    if not first:
                        pe.wait_ge(tmp_made, i * 4 + b - 3)
                    for c in range(8):
                        ins = nc.tensor.matmul(PY[:, b, 0:D], HT[:, c, b * P:(b + 1) * P], W2[:, c, :],
                                               start=(c == 0), stop=(c == 7))
                    ins.then_inc(y_made, 1)
            group(0, 4, True)
            with pe.Fori(1, groups) as i:
                group(i, 4, False)
            group(groups, NB - 4 * groups, False)

        @block.vector
        def _(dve):
            t = Tally(dve, chain)
            bits = m.weight[:, :].bitcast(U32)
            t.link(nc.vector.tensor_scalar(m.weight[:, :], m.weight[:, :], 0.0, None, ALU.add))
            t.link(nc.vector.tensor_scalar(T1.bitcast(U32), bits, 16, None, ALU.logical_shift_right))
            t.link(nc.vector.tensor_copy(HI, T1.bitcast(U32)))
            t.link(nc.vector.tensor_scalar(T2.bitcast(U32), bits, 65535, None, ALU.bitwise_and))
            t.link(nc.vector.tensor_copy(LO, T2.bitcast(U32)))
            t.link(nc.vector.tensor_scalar(NEG, m.weight[:, :], 0.0, None, ALU.is_lt))
            t.link(nc.vector.tensor_scalar(SGN, NEG, -2.0, 1.0, ALU.mult, ALU.add))
            t.link(nc.vector.tensor_tensor(LO, LO, SGN, ALU.mult))
            t.link(nc.vector.scalar_tensor_tensor(out=LO, in0=NEG, scalar=65535.0, in1=LO, op0=ALU.mult, op1=ALU.add))
            t.link(nc.vector.tensor_tensor(HI, HI, SGN, ALU.mult))
            t.link(nc.vector.scalar_tensor_tensor(out=HI, in0=NEG, scalar=65535.0 - 32768.0, in1=HI, op0=ALU.mult, op1=ALU.add))
            t.link(nc.vector.tensor_scalar(HI, HI, 32768.0, None, ALU.add))
            t.link(nc.vector.tensor_scalar(T1[:, 0:1], m.iota_col[:, 0:1], float(NLAST), None, ALU.is_lt))
            t.link(nc.vector.scalar_tensor_tensor(out=HI[:, NB - 1:NB], in0=HI[:, NB - 1:NB], scalar=1.0, in1=T1[:, 0:1],
                                                  op0=ALU.add, op1=ALU.mult))
            t.link(nc.vector.tensor_scalar(HI[:, NB - 1:NB], HI[:, NB - 1:NB], -1.0, None, ALU.add))

            def search(key, base):
                t.link(nc.vector.memset(C[:, 0:1], 0.0))
                t.link(nc.vector.memset(C[:, 1:2], 32768.0))
                with dve.Fori(0, 16) as r:
                    t.enter(r, 4)
                    t.link(nc.vector.tensor_tensor(C[:, 2:3], C[:, 0:1], C[:, 1:2], ALU.add))
                    nc.vector.tensor_scalar(T2, key, C[:, 2:3], None, ALU.is_ge, ALU.add, accum_out=C[:, 3:4]).then_inc(counted, 1)
                    dve.wait_ge(total, r + (base + 1))
                    t.link(nc.vector.scalar_tensor_tensor(out=C[:, 4:5], in0=PS[:, 0:1], scalar=float(KEEP), in1=C[:, 1:2],
                                                          op0=ALU.is_ge, op1=ALU.mult))
                    t.link(nc.vector.tensor_tensor(C[:, 0:1], C[:, 0:1], C[:, 4:5], ALU.add))
                    t.link(nc.vector.tensor_scalar(C[:, 1:2], C[:, 1:2], 0.5, None, ALU.mult))
                    t.leave(16)
            search(HI, 0)
            t.link(nc.vector.tensor_scalar(T1, HI, C[:, 0:1], 65537.0, ALU.is_gt, ALU.mult))
            t.link(nc.vector.tensor_scalar(SEL, HI, C[:, 0:1], None, ALU.is_equal))
            t.link(nc.vector.scalar_tensor_tensor(out=KEY, in0=LO, scalar=1.0, in1=SEL, op0=ALU.add, op1=ALU.mult))
            t.link(nc.vector.tensor_tensor(KEY, KEY, T1, ALU.add))
            t.link(nc.vector.tensor_scalar(KEY, KEY, -1.0, None, ALU.add))
            search(KEY, 16)
            t.link(nc.vector.tensor_scalar(SEL, KEY, C[:, 0:1], None, ALU.is_gt))
            nc.vector.tensor_scalar(TIE, KEY, C[:, 0:1], None, ALU.is_equal).then_inc(ties, 1)
            dve.wait_ge(ranked, 1)
            t.link(nc.vector.tensor_reduce(C[:, 5:6], PS[:, 64:64 + NB], AX, ALU.add))
            t.link(nc.vector.tensor_scalar(C[:, 5:6], C[:, 5:6], -1.0, float(KEEP), ALU.mult, ALU.add))
            t.link(nc.vector.tensor_copy(T1, PS[:, 192:192 + NB]))
            t.link(nc.vector.memset(NEG, 0.0))
            t.link(nc.vector.tensor_tensor_scan(T2, NEG, T1, 0.0, ALU.add, ALU.add))
            t.link(nc.vector.tensor_tensor(T2, T2, T1, ALU.subtract))
            t.link(nc.vector.tensor_tensor(T2, T2, PS[:, 128:128 + NB], ALU.add))
            t.link(nc.vector.tensor_scalar(T2, T2, C[:, 5:6], None, ALU.is_le))
            t.link(nc.vector.tensor_tensor(T2, T2, TIE, ALU.mult))
            t.link(nc.vector.tensor_tensor(SEL, SEL, T2, ALU.add))
            t.link(nc.vector.tensor_tensor(COEF, SEL, m.weight[:, :], ALU.mult))

            def finish(i, b):
                k = i * 4 + b
                dve.wait_ge(y_made, k + 1)
                if not isinstance(i, int):
                    dve.wait_ge(y_out, k - 3)
                nc.vector.tensor_tensor(TMP[:, b, :], PY[:, b, 0:D], m.rows[:, 3, :], ALU.add).then_inc(tmp_made, 1)
                dve.wait_ge(tmp_made, k + 1)
                nc.vector.scalar_tensor_tensor(out=BASE[:, ds(k * AW, D)], in0=TMP[:, b, :], scalar=COEF[:, ds(k, 1)],
                                               in1=BASE[:, ds(k * AW, D)], op0=ALU.mult, op1=ALU.add).then_inc(y_out, 1)
            for b in range(4):
                finish(0, b)
            with dve.Fori(1, groups) as i:
                for b in range(4):
                    finish(i, b)
            for b in range(NB - 4 * groups):
                dve.wait_ge(y_out, 4 * groups + b - 3)
                finish(groups, b)


def build_program(nc, a):
    m = Mem()
    with ExitStack() as ctx:
        sb = lambda n, shape, dt=F32: ctx.enter_context(nc.sbuf_tensor(n, shape, dt))
        region = 2 * CLEN + 8
        m.R1 = sb("region1", [P, region])
        m.R2 = sb("region2", [P, region])
        m.EX = sb("edge_values", [P, STEPS * HEADS])
        m.slots = sb("slots", [P, GROUP * D])
        m.WP = sb("w_project", [P, 2, 6 * D])
        m.Wo, m.Wout, m.Wmix = sb("w_o", [P, 2, D]), sb("w_out", [P, 2, D]), sb("w_mix", [P, 2, D])
        m.rows = sb("row_vectors", [P, 5, D])
        m.REL, m.SRC = sb("relative", [P, STEPS]), sb("source", [P, STEPS], I32)
        m.IDX = sb("index", [P, GROUP], I32)
        m.BT = sb("block_table", [1, STEPS], I32)
        m.ident, m.ones, m.upper = sb("ident", [P, P]), sb("ones", [P, P]), sb("upper", [P, P])
        m.iota_row, m.iota_col = sb("iota_row", [P, P]), sb("iota_col", [P, 1])
        m.bnst, m.stat, m.rstd = sb("bn", [P, NB, 6]), sb("stat", [P, NB, 2]), sb("rstd", [P, NB])
        m.eps, m.brc, m.b1c = sb("eps", [P, 1]), sb("brc", [P, 1]), sb("b1c", [P, 8])
        m.weight = sb("weight", [P, NB])
        m.TOPB = sb("mix_k_top", [P, D])
        dram = lambda n, shape, dt=F32: nc.dram_tensor(n, shape, dt, kind="Internal").ap()
        m.dst_rows, m.src_rows = dram("dst_rows", [TILES, P], I32), dram("src_rows", [TILES, P], I32)
        m.rel_rows, m.key_rows = dram("rel_rows", [STEPS, P]), dram("key_rows", [STEPS, P])
        m.step_block = dram("step_block", [STEPS], I32)
        m.k_d, m.v_d, m.mk_d, m.xn_d, m.xt_d, m.qs_d, m.z_d = (dram(n, [NB * P, D]) for n in (
            "k_rows", "v_rows", "mix_k_rows", "xn_rows", "xn_turned", "mix_q_rows", "mix_out_rows"))
        m.score_d, m.ex_d = dram("scores", [HEADS, STEPS * P]), dram("weights", [HEADS, STEPS * P])
        m.end_d = dram("piece_ends", [P, 4])
        for phase in (setup_phase, projection_phase, score_phase, softmax_phase,
                      aggregate_phase, output_phase, feed_forward_phase)[:PHASES]:
            used = []
            m.sem = lambda name: used.append(nc.alloc_semaphore(name)) or used[-1]
            phase(nc, m, a)
            nc.clear_and_free_semaphores(used)
            nc.all_engine_barrier()


PHASES = 99
_INS = ["x", "src", "dst", "L0_gnn_Wq", "L0_gnn_Wk", "L0_gnn_Wv", "L0_gnn_Wo", "L0_gnn_gamma", "L0_gnn_beta",
        "L0_mix_Wqkv", "L0_mix_Wout", "L0_mix_gamma", "L0_ffn_attention_mask", "L0_ffn_wr", "L0_ffn_br",
        "L0_ffn_w1", "L0_ffn_b1", "L0_ffn_w2", "L0_ffn_b2"]


def kernel(**inputs):
    import concourse.bacc as bacc
    from concourse.bass_utils import run_bass_kernel_spmd

    nc = bacc.Bacc("TRN2", target_bir_lowering=False, num_devices=1)
    arrays, a = {}, Mem()
    for name in _INS:
        v = np.ascontiguousarray(inputs[name])
        arrays[f"in_{name}"] = v
        a.__dict__[name] = nc.dram_tensor(f"in_{name}", v.shape, mybir.dt.from_np(v.dtype), kind="ExternalInput").ap()
    a.out = nc.dram_tensor("out", (N, D), F32, kind="ExternalOutput").ap()
    build_program(nc, a)
    r = run_bass_kernel_spmd(nc, [arrays], core_ids=[0])
    return r.results[0]["out"]
```

```python
from contextlib import ExitStack

import numpy as np
import concourse.bass as bass
from concourse import mybir

F32 = mybir.dt.float32
I32 = mybir.dt.int32
ALU = mybir.AluOpType
ACT = mybir.ActivationFunctionType
AX = mybir.AxisListType.X

P = 128
N, D = 6250, 256
E = 100000
HEADS, DH = 8, 32
FF = 4 * D
NB = -(-N // P)
NLAST = N - (NB - 1) * P
TILES = -(-E // P)
ELAST = E - (TILES - 1) * P
GROUP = 16
STEPS = -(-(TILES + NB - 1) // GROUP) * GROUP
TURNS = STEPS // GROUP
SROWS = -(-STEPS // P)
CHUNKS = P // HEADS
CLEN = STEPS * P // CHUNKS
SCALE = float(DH) ** -0.5
KEEP = max(1, N // 2) - 1
EPS = 1e-5
BIG = 1e30
AW = D + HEADS


class Tally:

    def __init__(self, eng, sem):
        self.eng, self.sem, self.base, self.n, self.turn, self.per = eng, sem, 0, 0, None, 0

    def now(self):
        v = self.base + self.n
        return v if self.turn is None else self.turn * self.per + v

    def inc(self, ins):
        ins.then_inc(self.sem, 1)
        self.n += 1

    def wait(self):
        self.eng.wait_ge(self.sem, self.now())

    def link(self, ins):
        self.inc(ins)
        self.wait()

    def enter(self, turn, per):
        self.base, self.n, self.turn, self.per = self.base + self.n, 0, turn, per

    def leave(self, turns):
        assert self.n == self.per, (self.n, self.per)
        self.base, self.n, self.turn = self.base + turns * self.per, 0, None


class Mem:
    pass


def ds(start, size):
    return bass.ds(start, size)


def blocks_of(nc, m, engine, i, h):
    return nc.values_load_multi_w_load_instructions(
        m.BT[0:1, ds(i * GROUP + 8 * h, 8)], engines=bass.OrderedEngineSet([engine]), min_val=0, max_val=NB - 1,
        skip_runtime_bounds_check_because="a block is a sum of NB - 1 comparisons")[1]


def half_rows(d, i, h):
    return d[:, :].rearrange("h (s e) -> s h e", e=P)[ds((i * 2 + h) * (GROUP // 2), GROUP // 2), :, :]


def setup_phase(nc, m, a):
    X = m.R1[:, 0:NB * D].rearrange("p (b c) -> p b c", b=NB)
    at = [0]

    def take(n, dt=F32):
        at[0] += n
        v = m.R2[:, at[0] - n:at[0]]
        return v if dt is F32 else v.bitcast(dt)
    ENDI, ENDF = take(SROWS, I32), take(SROWS)
    BELOW = take(SROWS * NB).rearrange("p (r b) -> p r b", r=SROWS)
    CUT, BLK, START = take(NB), take(NB), take(NB)
    SID, BF, TF, OFF = (take(SROWS) for _ in range(4))
    TI, BI = take(SROWS, I32), take(SROWS, I32)
    PADI = take(P, I32)
    PASSED = take(SROWS * NB).rearrange("p (r b) -> p r b", r=SROWS)
    DROW, SROW, KEY, MASK, MASK2 = (take(SROWS * P).rearrange("p (r e) -> p r e", r=SROWS) for _ in range(5))
    DINT, SINT = (take(SROWS * P, I32).rearrange("p (r e) -> p r e", r=SROWS) for _ in range(2))
    last1 = lambda v: v.rearrange("p (r o) -> p r o", o=1)
    FULL = TILES - 1
    PARTS = 7
    each = NB // PARTS
    with ExitStack() as ctx:
        sem = lambda n: m.sem(n)
        PT = ctx.enter_context(nc.psum_tensor("PT", [P, 4, 512], F32))
        PC = ctx.enter_context(nc.psum_tensor("PC", [P, 512], F32))
        w_in, e_in, rows_in, end_set, end_in = (sem(n) for n in ("w_in", "e_in", "rows_in", "end_set", "end_in"))
        x_in = [sem(f"x_in{k}") for k in range(PARTS)]
        made, chain, counted, stat_var, stat_std = (sem(n) for n in (
            "const_made", "setup_chain", "counts_summed", "stat_var", "stat_std"))
        tiles_known, table_known, turned, table_out = (sem(n) for n in (
            "tiles_known", "table_known", "table_turned", "table_out"))
        pad_made, x_zeroed = sem("pad_made"), sem("x_zeroed")
        block = ctx.enter_context(nc.Block())

        @block.sync
        def _(sp):
            sp.wait_ge(end_set, 1)
            ends = a.dst[0:FULL * P].rearrange("(t e) -> t e", e=P)[:, P - 1:P]
            whole = FULL // P
            for r in range(whole + 1):
                n = min(P, FULL - r * P)
                sp.dma_start(ENDI[0:n, r:r + 1], ends[r * P:r * P + n, :],
                             allow_slow_non_contiguous=True).then_inc(end_in, 16)
            for k in range(PARTS - 1):
                sp.dma_start(X[:, k * each:(k + 1) * each, :],
                             a.x[k * each * P:(k + 1) * each * P, :].rearrange("(b p) c -> p b c", p=P)).then_inc(x_in[k], 16)
            k = PARTS - 1
            sp.dma_start(X[:, k * each:NB - 1, :],
                         a.x[k * each * P:(NB - 1) * P, :].rearrange("(b p) c -> p b c", p=P)).then_inc(x_in[k], 16)
            sp.wait_ge(x_zeroed, 1)
            sp.dma_start(X[0:NLAST, NB - 1, :], a.x[(NB - 1) * P:N, :]).then_inc(x_in[k], 16)
            sp.wait_ge(table_known, 1)
            for r in range(SROWS):
                n = min(P, STEPS - r * P)
                sp.dma_start(m.step_block[r * P:r * P + n].rearrange("(p o) -> p o", o=1),
                             BI[0:n, r:r + 1]).then_inc(table_out, 16)
                sp.dma_start(m.rel_rows[r * P:r * P + n, :], DROW[0:n, r, :]).then_inc(table_out, 16)
                sp.dma_start(m.key_rows[r * P:r * P + n, :], KEY[0:n, r, :]).then_inc(table_out, 16)
            sp.wait_ge(table_out, 48 * SROWS)
            sp.dma_start(m.BT[:, :], m.step_block[:].rearrange("(o s) -> o s", o=1)).then_inc(table_out, 16)
            sp.wait_ge(table_out, 48 * SROWS + 16)

        @block.gpsimd
        def _(pool):
            nc.gpsimd.memset(PADI[0:2, :], 0).then_inc(pad_made, 1)
            pool.wait_ge(pad_made, 1)
            nc.gpsimd.memset(PADI[0:1, :], NB * P).then_inc(pad_made, 1)
            nc.gpsimd.iota(SID, pattern=[[P, SROWS]], base=0, channel_multiplier=1,
                           allow_small_or_imprecise_dtypes=True).then_inc(made, 1)
            nc.gpsimd.iota(BLK, pattern=[[1, NB]], base=0, channel_multiplier=0,
                           allow_small_or_imprecise_dtypes=True).then_inc(made, 1)
            nc.gpsimd.iota(START, pattern=[[P, NB]], base=0, channel_multiplier=0,
                           allow_small_or_imprecise_dtypes=True).then_inc(made, 1)
            nc.gpsimd.memset(m.ident[:, :], 0.0).then_inc(made, 1)
            nc.gpsimd.memset(m.ones[:, :], 1.0).then_inc(made, 1)
            nc.gpsimd.memset(m.upper[:, :], 1.0).then_inc(made, 1)
            nc.gpsimd.iota(m.iota_row[:, :], pattern=[[1, P]], base=0, channel_multiplier=0,
                           allow_small_or_imprecise_dtypes=True).then_inc(made, 1)
            nc.gpsimd.iota(m.iota_col[:, :], pattern=[[0, 1]], base=0, channel_multiplier=1,
                           allow_small_or_imprecise_dtypes=True).then_inc(made, 1)
            pool.wait_ge(made, 8)
            nc.gpsimd.affine_select(out=m.ident[:, :], in_=m.ident[:, :], compare_op=ALU.not_equal, fill=1.0,
                                    base=0, pattern=[[-1, P]], channel_multiplier=1).then_inc(made, 1)
            nc.gpsimd.affine_select(out=m.upper[:, :], in_=m.upper[:, :], compare_op=ALU.is_ge, fill=0.0,
                                    base=0, pattern=[[1, P]], channel_multiplier=-1).then_inc(made, 1)
            pool.wait_ge(e_in, 96)
            pool.wait_ge(tiles_known, 1)
            for r in range(SROWS):
                for k, (out, rows) in enumerate(((DINT, m.dst_rows), (SINT, m.src_rows))):
                    nc.gpsimd.indirect_dma_start(
                        out=out[:, r, :], out_offset=None, in_=rows[:, :],
                        in_offset=bass.IndirectOffsetOnAxis(ap=TI[:, r:r + 1], axis=0)).then_inc(rows_in, 16)

        @block.scalar
        def _(act):
            cut = FULL * P
            one = lambda v: v.rearrange("(o p) -> o p", o=1)
            act.dma_start(m.dst_rows[0:FULL, :], a.dst[0:cut].rearrange("(t p) -> t p", p=P)).then_inc(e_in, 16)
            act.dma_start(m.src_rows[0:FULL, :], a.src[0:cut].rearrange("(t p) -> t p", p=P)).then_inc(e_in, 16)
            act.dma_start(one(m.dst_rows[FULL, 0:ELAST]), one(a.dst[cut:E])).then_inc(e_in, 16)
            act.dma_start(one(m.src_rows[FULL, 0:ELAST]), one(a.src[cut:E])).then_inc(e_in, 16)
            act.wait_ge(pad_made, 2)
            act.dma_start(one(m.dst_rows[FULL, ELAST:P]), PADI[0:1, 0:P - ELAST]).then_inc(e_in, 16)
            act.dma_start(one(m.src_rows[FULL, ELAST:P]), PADI[1:2, 0:P - ELAST]).then_inc(e_in, 16)
            full = lambda v: v.rearrange("(o c) -> o c", o=1).broadcast_to([P, D])
            mix = a.L0_mix_Wqkv.rearrange("(k p) n -> p k n", p=P)
            for out, src in (
                (m.WP[:, :, 0:256], a.L0_gnn_Wq.rearrange("(k p) n -> p k n", p=P)),
                (m.WP[:, :, 256:512], a.L0_gnn_Wk.rearrange("(k p) n -> p k n", p=P)),
                (m.WP[:, :, 512:768], mix[:, :, D:2 * D]),
                (m.WP[:, :, 768:1024], a.L0_gnn_Wv.rearrange("(k p) n -> p k n", p=P)),
                (m.WP[:, :, 1024:1280], mix[:, :, 0:D]),
                (m.WP[:, :, 1280:1536], mix[:, :, 2 * D:3 * D]),
                (m.Wo[:, :, :], a.L0_gnn_Wo.rearrange("(k p) n -> p k n", p=P)),
                (m.Wout[:, :, :], a.L0_mix_Wout.rearrange("(k p) n -> p k n", p=P)),
                (m.rows[:, 0, :], full(a.L0_gnn_gamma)), (m.rows[:, 1, :], full(a.L0_gnn_beta)),
                (m.rows[:, 2, :], full(a.L0_mix_gamma)), (m.rows[:, 3, :], full(a.L0_ffn_b2)),
                (m.rows[:, 4, :], a.L0_ffn_wr.rearrange("c o -> o c").broadcast_to([P, D])),
                (m.brc[:, :], a.L0_ffn_br.rearrange("(o c) -> o c", o=1).broadcast_to([P, 1])),
                (m.b1c[:, :], a.L0_ffn_b1.rearrange("(k p) -> p k", p=P)),
            ):
                act.dma_start(out, src, allow_slow_non_contiguous=True).then_inc(w_in, 16)
            act.wait_ge(stat_var, NB + 1)
            nc.scalar.activation(m.rstd[:, :], m.stat[:, :, 1], ACT.Sqrt, bias=m.eps[:, :]).then_inc(stat_std, 1)
            act.wait_ge(w_in, 16 * 15)

        @block.tensor
        def _(pe):
            pe.wait_ge(counted, 1)
            pe.wait_ge(made, 10)
            nc.tensor.matmul(PC[:, 0:NB], m.ones[:, :], CUT, start=True, stop=True).then_inc(counted, 1)
            pe.wait_ge(table_known, 1)
            for q, rows in enumerate((DROW, SROW)):
                for r in range(SROWS):
                    n = min(P, STEPS - r * P)
                    nc.tensor.transpose(PT[:, 2 * q + r // 4, (r % 4) * P:(r % 4) * P + n], rows[0:n, r, :],
                                        m.ident[0:n, 0:n]).then_inc(turned, 1)

        @block.vector
        def _(dve):
            t = Tally(dve, chain)
            wide = [P, SROWS, NB]
            nc.vector.memset(m.eps[:, :], EPS).then_inc(stat_var, 1)
            nc.vector.memset(ENDI, 4 * NB * P).then_inc(end_set, 1)
            nc.vector.memset(X[:, NB - 1, :], 0.0).then_inc(x_zeroed, 1)
            dve.wait_ge(end_in, 16 * (FULL // P + 1))
            dve.wait_ge(made, 3)
            t.link(nc.vector.tensor_copy(ENDF, ENDI))
            block_row = lambda v: v.rearrange("p (o b) -> p o b", o=1).broadcast_to(wide)
            t.link(nc.vector.tensor_tensor(BELOW, last1(ENDF).broadcast_to(wide), block_row(START), ALU.is_lt))
            nc.vector.tensor_reduce(CUT, BELOW.rearrange("p r b -> p b r"), AX, ALU.add).then_inc(counted, 1)
            dve.wait_ge(counted, 2)
            t.link(nc.vector.tensor_tensor(CUT, PC[:, 0:NB], BLK, ALU.add))
            t.link(nc.vector.tensor_tensor(PASSED, last1(SID).broadcast_to(wide), block_row(CUT), ALU.is_ge))
            t.link(nc.vector.tensor_reduce(BF, PASSED[:, :, 1:NB], AX, ALU.add))
            t.link(nc.vector.tensor_tensor(TF, SID, BF, ALU.subtract))
            t.link(nc.vector.tensor_scalar(OFF, TF, float(TILES - 1), 4.0 * NB * P, ALU.is_gt, ALU.mult))
            t.link(nc.vector.tensor_scalar(TF, TF, float(TILES - 1), None, ALU.min))
            t.link(nc.vector.tensor_copy(BI, BF))
            t.link(nc.vector.scalar_tensor_tensor(out=OFF, in0=BF, scalar=float(-P), in1=OFF, op0=ALU.mult, op1=ALU.add))
            nc.vector.tensor_copy(TI, TF).then_inc(tiles_known, 1)
            for b in range(NB):
                if b % each == 0:
                    dve.wait_ge(x_in[b // each], 32 if b // each == PARTS - 1 else 16)
                t.inc(nc.vector.bn_stats(m.bnst[:, b, :], X[:, b, :]))
            t.wait()
            for b in range(NB):
                nc.vector.bn_aggr(m.stat[:, b, :], m.bnst[:, b, :]).then_inc(stat_var, 1)
            dve.wait_ge(rows_in, 32 * SROWS)
            t.inc(nc.vector.tensor_copy(SROW, SINT))
            t.link(nc.vector.tensor_copy(KEY, DINT))
            t.link(nc.vector.tensor_tensor(DROW, KEY, last1(OFF).broadcast_to([P, SROWS, P]), ALU.add))
            t.inc(nc.vector.tensor_scalar(MASK, DROW, 0.0, None, ALU.is_ge))
            t.link(nc.vector.tensor_scalar(MASK2, DROW, float(P), None, ALU.is_lt))
            t.link(nc.vector.tensor_tensor(MASK, MASK, MASK2, ALU.mult))
            t.link(nc.vector.scalar_tensor_tensor(out=KEY, in0=KEY, scalar=1.0, in1=MASK, op0=ALU.add, op1=ALU.mult))
            nc.vector.tensor_scalar(KEY, KEY, -1.0, None, ALU.add).then_inc(table_known, 1)
            dve.wait_ge(turned, 2 * SROWS)
            for q, out in enumerate((m.REL, m.SRC)):
                t.inc(nc.vector.tensor_copy(out[:, 0:512], PT[:, 2 * q, :]))
                t.inc(nc.vector.tensor_copy(out[:, 512:STEPS], PT[:, 2 * q + 1, 0:STEPS - 512]))
            dve.wait_ge(stat_std, 1)
            t.link(nc.vector.reciprocal(m.rstd[:, :], m.rstd[:, :]))


def projection_phase(nc, m, a):
    X = m.R1[:, 0:NB * D]
    QB = m.R2[:, 0:NB * D]
    XN = m.slots[:, 0:2 * D].rearrange("p (u c) -> p u c", u=2)
    XT = m.slots[:, 512:512 + 2 * D].rearrange("p (u k t) -> p u k t", u=2, k=2)
    KS = m.slots[:, 1024:1024 + 2 * D].rearrange("p (u c) -> p u c", u=2)
    MK = m.slots[:, 1536:1536 + 2 * D].rearrange("p (u c) -> p u c", u=2)
    TOP = m.slots[:, 2048:2048 + D]
    TOPT = m.slots[:, 2304:2306]
    DIAG = m.slots[:, 2560:2560 + D].rearrange("p (k c) -> p k c", k=2)
    last = NB // 2
    with ExitStack() as ctx:
        sem = lambda n: [m.sem(f"{n}{u}") for u in range(2)]
        PX = ctx.enter_context(nc.psum_tensor("PX", [P, 2, 512], F32))
        PP = ctx.enter_context(nc.psum_tensor("PP", [P, 2, 2, 512], F32))
        xn_made, turned, xt_made, done, copied, maxed = (sem(n) for n in (
            "p_xn", "p_turned", "p_xt", "p_done", "p_copied", "p_maxed"))
        x_stored, x_free, k_stored = (sem(n) for n in ("p_xst", "p_xfree", "p_kst"))
        chain, top_turned, diag_made, spread = (m.sem(n) for n in ("p_chain", "p_topt", "p_diag", "p_spread"))
        block = ctx.enter_context(nc.Block())
        rows = lambda i, u: ds((i * 2 + u) * P, P)
        turned_rows = lambda v: v.rearrange("p k t -> p (k t)")

        @block.sync
        def _(sp):
            def store(i, u):
                sp.wait_ge(xn_made[u], i + 1)
                sp.dma_start(m.xn_d[rows(i, u), :], XN[:, u, :]).then_inc(x_stored[u], 16)
                sp.wait_ge(xt_made[u], i + 1)
                sp.dma_start(m.xt_d[rows(i, u), :], turned_rows(XT[:, u, :, :])).then_inc(x_stored[u], 16)

            def free(i, u):
                sp.wait_ge(x_stored[u], (i + 1) * 32)
                sp.sem_inc(x_free[u], 1)
            for u in range(2):
                sp.sem_inc(x_free[u], 1)
            store(0, 0)
            store(0, 1)
            free(0, 0)
            with sp.Fori(1, last) as i:
                store(i, 0)
                free(i - 1, 1)
                store(i, 1)
                free(i, 0)
            store(last, 0)
            sp.wait_ge(x_stored[0], (last + 1) * 32)
            sp.wait_ge(x_stored[1], last * 32)

        @block.scalar
        def _(act):
            def copy_x(i, u):
                act.wait_ge(turned[u], i + 1)
                act.wait_ge(x_free[u], i + 1)
                nc.scalar.activation(XT[:, u, :, :], PX[:, u, 0:D].rearrange("p (k t) -> p k t", k=2), ACT.Copy).then_inc(xt_made[u], 1)

            def copies(i, u, first=False):
                act.wait_ge(done[u], i + 1)
                nc.scalar.activation(QB[:, ds((i * 2 + u) * D, D)], PP[:, u, 0, 0:D], ACT.Copy).then_inc(copied[u], 1)
                if not first:
                    act.wait_ge(k_stored[u], i * 32)
                nc.scalar.activation(KS[:, u, :], PP[:, u, 0, D:2 * D], ACT.Copy).then_inc(copied[u], 1)
                if not first:
                    act.wait_ge(maxed[u], i + 0)
                nc.scalar.activation(MK[:, u, :], PP[:, u, 1, 0:D], ACT.Copy).then_inc(copied[u], 1)

            def store(i, u):
                act.wait_ge(copied[u], i * 3 + 3)
                act.dma_start(m.k_d[rows(i, u), :], KS[:, u, :]).then_inc(k_stored[u], 16)
                act.dma_start(m.mk_d[rows(i, u), :], MK[:, u, :]).then_inc(k_stored[u], 16)
            copy_x(0, 0)
            copy_x(0, 1)
            copies(0, 0, True)
            copy_x(1, 0)
            store(0, 0)
            copies(0, 1, True)
            with act.Fori(1, last) as i:
                copy_x(i, 1)
                store(i - 1, 1)
                copies(i, 0)
                copy_x(i + 1, 0)
                store(i, 0)
                copies(i, 1)
            store(last - 1, 1)
            copies(last, 0)
            store(last, 0)
            act.wait_ge(k_stored[0], (last + 1) * 32)
            act.wait_ge(k_stored[1], last * 32)

        @block.tensor
        def _(pe):
            def turn(i, u):
                pe.wait_ge(xn_made[u], i + 1)
                for k in range(2):
                    ins = nc.tensor.transpose(PX[:, u, k * P:(k + 1) * P], XN[:, u, k * P:(k + 1) * P], m.ident[:, :])
                ins.then_inc(turned[u], 1)

            def project(i, u, first=False):
                pe.wait_ge(xt_made[u], i + 1)
                if not first:
                    pe.wait_ge(copied[u], i * 3)
                for c, n in ((0, 512), (1, 256)):
                    for k in range(2):
                        ins = nc.tensor.matmul(PP[:, u, c, 0:n], XT[:, u, k, :], m.WP[:, k, c * 512:c * 512 + n],
                                               start=(k == 0), stop=(k == 1))
                ins.then_inc(done[u], 1)

            turn(0, 0)
            turn(0, 1)
            project(0, 0, True)
            turn(1, 0)
            project(0, 1, True)
            with pe.Fori(1, last) as i:
                turn(i, 1)
                project(i, 0)
                turn(i + 1, 0)
                project(i, 1)
            project(last, 0)
            pe.wait_ge(maxed[0], last + 1)
            for k in range(2):
                ins = nc.tensor.transpose(PX[:, 0, k * P:(k + 1) * P], TOP[:, k * P:(k + 1) * P], m.ident[:, :])
            ins.then_inc(top_turned, 1)
            pe.wait_ge(diag_made, 2)
            for k in range(2):
                ins = nc.tensor.matmul(PX[:, 1, k * P:(k + 1) * P], m.ones[:, :], DIAG[:, k, :], start=True, stop=True)
            ins.then_inc(spread, 1)

        @block.vector
        def _(dve):
            t = Tally(dve, chain)

            def normalise(i, u, first=False):
                dve.wait_ge(x_free[u], i + 1)
                if not first:
                    dve.wait_ge(turned[u], i + 0)
                b = i * 2 + u
                nc.vector.tensor_scalar(XN[:, u, :], X[:, ds(b * D, D)], m.stat[:, ds(b, 1), 0], m.rstd[:, ds(b, 1)],
                                        ALU.subtract, ALU.mult).then_inc(xn_made[u], 1)

            def maximum(i, u, n=P):
                dve.wait_ge(copied[u], i * 3 + 3)
                t.wait()
                t.inc(nc.vector.tensor_tensor(TOP[0:n, :], TOP[0:n, :], MK[0:n, u, :], ALU.max))
                t.wait()
                dve.sem_inc(maxed[u], 1)
            t.link(nc.vector.memset(TOP, -BIG))
            normalise(0, 0, True)
            normalise(0, 1, True)
            with dve.Fori(0, last - 1) as i:
                t.enter(i, 2)
                for u in range(2):
                    normalise(i + 1, u)
                    maximum(i, u)
                t.leave(last - 1)
            normalise(last, 0)
            maximum(last - 1, 0)
            maximum(last - 1, 1)
            maximum(last, 0, NLAST)
            dve.wait_ge(top_turned, 1)
            t.link(nc.vector.tensor_reduce(TOPT, PX[:, 0, 0:D].rearrange("p (k t) -> p k t", k=2), AX, ALU.max))
            for k in range(2):
                nc.vector.tensor_scalar(DIAG[:, k, :], m.ident[:, :], TOPT[:, k:k + 1], None, ALU.mult).then_inc(diag_made, 1)
            dve.wait_ge(spread, 1)
            t.link(nc.vector.tensor_copy(m.TOPB[:, :], PX[:, 1, 0:D]))


def score_phase(nc, m, a):
    QB = m.R2[:, 0:NB * D]
    KG = m.slots.rearrange("p (j c) -> p j c", j=GROUP)
    at = [0]

    def take(n):
        at[0] += n
        return m.R1[:, at[0] - n:at[0]]
    OH = take(16 * P).rearrange("p (h j e) -> p h j e", h=2, j=8)
    PR = take(1024).rearrange("p (g c) -> p g c", g=2)
    SC = take(P).rearrange("p (h n) -> p h n", h=2)
    ST = take(2 * P)[0:P // 2].rearrange("p (h e) -> p h e", h=2)
    XT = take(D).rearrange("p (k t) -> p k t", k=2)
    MK = take(D)
    VQ = take(2 * D)
    MV = take(2 * P + 2).rearrange("p (k w) -> p k w", k=2)
    KX = take(D)
    QM = take(D)
    QR = take(2 * HEADS).rearrange("p (s h) -> p s h", s=2)
    SUM = take(2 * P + 2).rearrange("p (k w) -> p k w", k=2)
    SAME, RDEN = take(P), take(2)
    CTX, CTXT = (take(2 * P).rearrange("p (k c) -> p k c", k=2) for _ in range(2))
    MIX = NB
    with ExitStack() as ctx:
        sem = lambda n: m.sem(n)
        PQ = ctx.enter_context(nc.psum_tensor("PQ", [P, 4, 512], F32))
        PT = ctx.enter_context(nc.psum_tensor("PTS", [P, 512], F32))
        PM = ctx.enter_context(nc.psum_tensor("PMX", [P, 2, 512], F32))
        PC = ctx.enter_context(nc.psum_tensor("PCX", [P, 512], F32))
        turned = [sem(f"s_turned{h}") for h in range(2)]
        copied = [sem(f"s_copied{h}") for h in range(2)]
        stored = [sem(f"s_stored{h}") for h in range(2)]
        passed = sem("s_passed")
        mulled, scored = sem("s_mulled"), sem("s_scored")
        idx_made = [sem(f"s_idx{h}") for h in range(2)]
        k_in = [sem(f"s_k{j}") for j in range(GROUP)]
        rel_in = [sem(f"s_rel{h}") for h in range(2)]
        hot = [sem(f"s_hot{h}") for h in range(2)]
        q_out = [sem(f"s_q{b}") for b in range(4)]
        xt_in, mk_in, projected, vq_made, mv_made, v_stored, qs_stored = (sem(n) for n in (
            "s_xt", "s_mk", "s_proj", "s_vq", "s_mv", "s_vst", "s_qst"))
        k_sub, k_exp, q_sub, q_exp, q_made, ctx_out, ctx_added = (sem(n) for n in (
            "s_ksub", "s_kexp", "s_qsub", "s_qexp", "s_qmade", "s_ctx", "s_ctxadd"))
        same, chain, ctx_made, ctx_turned, ctxt_made, m_made = (sem(n) for n in (
            "s_same", "s_chain", "s_cm", "s_ct", "s_ctt", "s_m"))
        block = ctx.enter_context(nc.Block())
        rows = lambda i: ds(i * P, P)

        @block.sync
        def _(sp):
            def load(i, h):
                sp.dma_start(OH[:, h, :, :], m.rel_rows[ds((i * 2 + h) * 8, 8), :].rearrange("(o s) e -> o s e", o=1)
                             .broadcast_to([P, 8, P])).then_inc(rel_in[h], 16)

            def load_block(i):
                sp.dma_start(XT.rearrange("p k t -> p (k t)"), m.xt_d[rows(i), :]).then_inc(xt_in, 16)
                sp.dma_start(MK, m.mk_d[rows(i), :]).then_inc(mk_in, 16)

            def turn(i, store, then):
                sp.wait_ge(q_out[3], i * 2 + 1)
                load(i + 1, 0)
                if store:
                    sp.wait_ge(vq_made, i + 1)
                    sp.dma_start(m.v_d[rows(i), :], VQ[:, 0:D]).then_inc(v_stored, 16)
                if then:
                    sp.wait_ge(projected, i + 1)
                    sp.wait_ge(k_sub, i + 1)
                    load_block(i + 1)
                sp.wait_ge(q_out[3], i * 2 + 2)
                load(i + 1, 1)
                if store:
                    sp.wait_ge(q_made, i + 1)
                    sp.dma_start(m.qs_d[rows(i), :], QM).then_inc(qs_stored, 16)
            load(0, 0)
            load(0, 1)
            load_block(0)
            with sp.Fori(0, MIX - 1) as i:
                turn(i, True, True)
            turn(MIX - 1, True, False)
            for i in range(MIX, TURNS - 1):
                turn(i, False, False)
            sp.wait_ge(v_stored, 16 * MIX)
            sp.wait_ge(qs_stored, 16 * MIX)

        @block.gpsimd
        def _(pool):
            nc.gpsimd.memset(SAME, 0.0).then_inc(same, 1)
            for g in range(P // DH):
                pool.wait_ge(same, g + 1)
                nc.gpsimd.memset(SAME[g * DH:(g + 1) * DH, g * DH:(g + 1) * DH], 1.0).then_inc(same, 1)

            def gather(i, first):
                for h in range(2):
                    pool.wait_ge(idx_made[h], i + 1)
                    for j in range(8 * h, 8 * h + 8):
                        if j % 2 == 0 and not first:
                            pool.wait_ge(mulled, i * 8 + j // 2 - 7)
                        if j % 2 == 0:
                            pool.sem_inc(passed, 1)
                        nc.gpsimd.indirect_dma_start(
                            out=KG[:, j, :], out_offset=None, in_=m.k_d[:, :],
                            in_offset=bass.IndirectOffsetOnAxis(ap=m.IDX[:, j:j + 1], axis=0)).then_inc(k_in[j], 16)
            gather(0, True)
            with pool.Fori(1, TURNS) as i:
                gather(i, False)

        @block.scalar
        def _(act):
            def store(i, h, first):
                act.wait_ge(turned[h], i + 1)
                if not first:
                    act.wait_ge(stored[h], i * 16)
                nc.scalar.activation(ST[:, h, :], PT[0:P // 2, h * P:(h + 1) * P], ACT.Copy).then_inc(copied[h], 1)
                act.wait_ge(copied[h], i + 1)
                act.dma_start(half_rows(m.score_d, i, h), ST[:, h, :]).then_inc(stored[h], 16)

            def mix(i, n, first):
                act.wait_ge(k_sub, i + 1)
                nc.scalar.activation(KX[0:n, :], KX[0:n, :], ACT.Exp).then_inc(k_exp, 1)
                act.wait_ge(projected, i + 1)
                if not first:
                    act.wait_ge(v_stored, i * 16)
                    act.wait_ge(q_sub, i + 0)
                nc.scalar.activation(VQ, PM[:, 0, :], ACT.Copy).then_inc(vq_made, 1)
                if not first:
                    act.wait_ge(ctx_out, i + 0)
                nc.scalar.activation(MV[:, :, 0:P], PM[:, 1, 0:D].rearrange("p (k c) -> p k c", k=2), ACT.Copy).then_inc(mv_made, 1)
                act.wait_ge(q_sub, i + 1)
                nc.scalar.activation(QM, QM, ACT.Exp).then_inc(q_exp, 1)
            mix(0, P, True)
            store(0, 0, True)
            mix(1, P, False)
            store(0, 1, True)
            store(1, 0, False)
            with act.Fori(2, MIX - 1) as i:
                mix(i, P, False)
                store(i - 1, 1, False)
                store(i, 0, False)
            mix(MIX - 1, NLAST, False)
            with act.Fori(MIX - 1, TURNS) as i:
                store(i - 1, 1, False)
                store(i, 0, False)
            store(TURNS - 1, 1, False)
            for h in range(2):
                act.wait_ge(stored[h], 16 * TURNS)

        @block.tensor
        def _(pe):
            def turn(i, h, first):
                pe.wait_ge(scored, i * 8 + 4 * h + 4)
                if h == 1:
                    pe.wait_ge(copied[0], i + 1)
                elif not first:
                    pe.wait_ge(copied[1], i + 0)
                pe.sem_inc(passed, 1)
                nc.tensor.transpose(PT[0:P // 2, h * P:(h + 1) * P], SC[:, h, :], m.ident[:, :]).then_inc(turned[h], 1)

            def project(i, first):
                pe.wait_ge(xt_in, i * 16 + 16)
                if not first:
                    pe.wait_ge(vq_made, i + 0)
                    pe.wait_ge(mv_made, i + 0)
                for c, n in ((0, 512), (1, 256)):
                    for k in range(2):
                        ins = nc.tensor.matmul(PM[:, c, 0:n], XT[:, k, :], m.WP[:, k, 768 + c * 512:768 + c * 512 + n],
                                               start=(k == 0), stop=(k == 1))
                ins.then_inc(projected, 1)

            def context(i, n, first):
                pe.wait_ge(k_exp, i + 1)
                pe.wait_ge(mv_made, i + 1)
                if not first:
                    pe.wait_ge(ctx_added, i + 1)
                for k in range(2):
                    ins = nc.tensor.matmul(PC[:, k * (P + 1):(k + 1) * (P + 1)], KX[0:n, k * P:(k + 1) * P], MV[0:n, k, :],
                                           start=True, stop=True)
                ins.then_inc(ctx_out, 1)

            def expand(i, first, n):
                for j in range(GROUP):
                    g = j // 2
                    if j % 8 == 0:
                        block_of = blocks_of(nc, m, mybir.EngineType.PE, i, j // 8)
                        pe.wait_ge(hot[j // 8], i + 1)
                    if j == 8 and not first:
                        turn(i - 1, 1, isinstance(i, int) and i == 1)
                    if j % 2 == 0 and (g >= 4 or not first):
                        pe.wait_ge(mulled, i * 8 + g - 3)
                    ins = nc.tensor.matmul(PQ[:, g % 4, (j % 2) * D:(j % 2 + 1) * D], OH[:, j // 8, j % 8, :],
                                           QB[:, ds(block_of[j % 8] * D, D)], start=True, stop=True)
                    if j % 2:
                        ins.then_inc(q_out[g % 4], 1)
                    if j == 3 and n:
                        project(i, first)
                    if j == 11 and n:
                        context(i, n, first)
                turn(i, 0, first)
            expand(0, True, P)
            expand(1, False, P)
            with pe.Fori(2, MIX - 1) as i:
                expand(i, False, P)
            expand(MIX - 1, False, NLAST)
            with pe.Fori(MIX, TURNS) as i:
                expand(i, False, 0)
            turn(TURNS - 1, 1, False)
            pe.wait_ge(ctx_made, 2)
            for k in range(2):
                ins = nc.tensor.transpose(PM[:, 0, k * P:(k + 1) * P], CTX[:, k, :], m.ident[:, :])
            ins.then_inc(ctx_turned, 1)
            pe.wait_ge(ctxt_made, 1)
            for k in range(2):
                ins = nc.tensor.matmul(PM[:, 1, k * D:(k + 1) * D], CTXT[:, k, :], m.Wout[:, k, :], start=True, stop=True)
            ins.then_inc(m_made, 1)

        @block.vector
        def _(dve):
            t = Tally(dve, chain)
            head = lambda x: x.rearrange("p (h d) -> p h d", h=HEADS)
            over = lambda x: x.rearrange("p (h o) -> p h o", o=1).broadcast_to([P, HEADS, DH])

            def hots(i, h):
                dve.wait_ge(rel_in[h], (i + 1) * 16)
                nc.vector.tensor_scalar(OH[:, h, :, :], OH[:, h, :, :], m.iota_col[:, 0:1], None, ALU.is_equal).then_inc(hot[h], 1)

            def index(i, h):
                nc.vector.tensor_copy(m.IDX[:, 8 * h:8 * h + 8], m.SRC[:, ds(i * GROUP + 8 * h, 8)]).then_inc(idx_made[h], 1)

            def multiply(i, g, first):
                dve.wait_ge(q_out[g % 4], i * 2 + g // 4 + 1)
                dve.wait_ge(k_in[2 * g], (i + 1) * 16)
                dve.wait_ge(k_in[2 * g + 1], (i + 1) * 16)
                if g >= 2 or not first:
                    dve.wait_ge(scored, i * 8 + g - 1)
                nc.vector.tensor_tensor(PR[:, g % 2, :], PQ[:, g % 4, :], KG[:, 2 * g:2 * g + 2, :].rearrange("p j c -> p (j c)"),
                                        ALU.mult).then_inc(mulled, 1)

            def add_up(i, g, first):
                dve.wait_ge(mulled, i * 8 + g + 1)
                if g % 4 == 0 and not first:
                    dve.wait_ge(turned[g // 4], i + 0)
                nc.vector.tensor_reduce(SC[:, g // 4, (g % 4) * 2 * HEADS:(g % 4 + 1) * 2 * HEADS],
                                        PR[:, g % 2, :].rearrange("p (n d) -> p n d", d=DH), AX, ALU.add).then_inc(scored, 1)

            def mix(i, g, first):
                if g == 0:
                    dve.wait_ge(mk_in, i * 16 + 16)
                    if not first:
                        dve.wait_ge(ctx_out, i + 0)
                    nc.vector.tensor_tensor(KX, MK, m.TOPB[:, :], ALU.subtract).then_inc(k_sub, 1)
                if g == 3:
                    dve.wait_ge(vq_made, i + 1)
                    t.link(nc.vector.tensor_reduce(QR[:, 0, :], head(VQ[:, D:2 * D]), AX, ALU.max))
                    if not first:
                        dve.wait_ge(qs_stored, i * 16)
                    nc.vector.tensor_tensor(head(QM), head(VQ[:, D:2 * D]), over(QR[:, 0, :]), ALU.subtract).then_inc(q_sub, 1)
                if g == 5:
                    dve.wait_ge(q_exp, i + 1)
                    t.link(nc.vector.tensor_reduce(QR[:, 1, :], head(QM), AX, ALU.add))
                    t.link(nc.vector.reciprocal(QR[:, 1, :], QR[:, 1, :]))
                    nc.vector.scalar_tensor_tensor(out=head(QM), in0=head(QM), scalar=SCALE, in1=over(QR[:, 1, :]),
                                                   op0=ALU.mult, op1=ALU.mult).then_inc(q_made, 1)
                if g == 7:
                    dve.wait_ge(ctx_out, i + 1)
                    dve.wait_ge(ctx_added, i + 1)
                    nc.vector.tensor_tensor(SUM, SUM, PC[:, 0:2 * P + 2].rearrange("p (k w) -> p k w", k=2),
                                            ALU.add).then_inc(ctx_added, 1)

            def turn(i, first, last, block):
                for g in range(8):
                    multiply(i, g, first)
                    if g == 1:
                        hots(i, 1)
                    if g:
                        add_up(i, g - 1, first)
                    if g == 4 and not last:
                        index(i + 1, 0)
                    if g == 5 and not last:
                        hots(i + 1, 0)
                    if block:
                        mix(i, g, first)
                add_up(i, 7, first)
                if not last:
                    index(i + 1, 1)
            index(0, 0)
            index(0, 1)
            nc.vector.memset(SUM, 0.0).then_inc(ctx_added, 1)
            t.link(nc.vector.memset(MV[:, :, P], 1.0))
            hots(0, 0)
            turn(0, True, False, True)
            with dve.Fori(1, MIX) as i:
                t.enter(i - 1, 3)
                turn(i, False, False, True)
                t.leave(MIX - 1)
            for i in range(MIX, TURNS):
                turn(i, False, i == TURNS - 1, False)
            dve.wait_ge(ctx_added, MIX + 1)
            for k in range(2):
                t.inc(nc.vector.reciprocal(RDEN[:, k:k + 1], SUM[:, k, P:P + 1]))
            t.wait()
            dve.wait_ge(same, P // DH + 1)
            for k in range(2):
                nc.vector.scalar_tensor_tensor(out=CTX[:, k, :], in0=SUM[:, k, 0:P], scalar=RDEN[:, k:k + 1], in1=SAME,
                                               op0=ALU.mult, op1=ALU.mult).then_inc(ctx_made, 1)
            dve.wait_ge(ctx_turned, 1)
            nc.vector.tensor_copy(CTXT, PM[:, 0, 0:D].rearrange("p (k t) -> p k t", k=2)).then_inc(ctxt_made, 1)
            dve.wait_ge(m_made, 1)
            t.link(nc.vector.tensor_copy(m.Wmix[:, :, :], PM[:, 1, :].rearrange("p (k c) -> p k c", k=2)))


def softmax_phase(nc, m, a):
    S, KEY = m.R1[:, 0:CLEN], m.R1[:, CLEN:2 * CLEN]
    CUT, M = m.R2[:, 0:CLEN + 1], m.R2[:, CLEN + 1:2 * CLEN + 1]
    END = m.slots[:, 1024:1028]
    ENDS = m.slots[:, 1088:1088 + 4 * CHUNKS]
    MSK = m.slots[:, 1280:1280 + 2 * CHUNKS]
    TOP = m.slots[:, 1344:1346]
    with ExitStack() as ctx:
        sem = lambda n: m.sem(n)
        s_in, key_in, end_made, end_out, ends_in = (sem(n) for n in ("m_sin", "m_kin", "m_end", "m_eout", "m_ein"))
        chain, diff, exped, ex_out = (sem(n) for n in ("m_chain", "m_diff", "m_exp", "m_xout"))
        block = ctx.enter_context(nc.Block())

        @block.sync
        def _(sp):
            for h in range(HEADS):
                sp.dma_start(KEY[h * CHUNKS:(h + 1) * CHUNKS, :],
                             m.key_rows[:, :].rearrange("s e -> (s e)").rearrange("(c l) -> c l", c=CHUNKS)).then_inc(key_in, 16)
            sp.dma_start(S, m.score_d[:, :].rearrange("h (c l) -> (h c) l", c=CHUNKS)).then_inc(s_in, 16)
            sp.wait_ge(end_made, 2)
            sp.dma_start(m.end_d[:, :], END).then_inc(end_out, 16)
            sp.wait_ge(end_out, 16)
            for h in range(HEADS):
                sp.dma_start(ENDS[h * CHUNKS:(h + 1) * CHUNKS, :],
                             m.end_d[h * CHUNKS:(h + 1) * CHUNKS, :].rearrange("c k -> (c k)").rearrange("(o n) -> o n", o=1)
                             .broadcast_to([CHUNKS, 4 * CHUNKS])).then_inc(ends_in, 16)
            sp.wait_ge(exped, 1)
            sp.dma_start(m.ex_d[:, :].rearrange("h (c l) -> (h c) l", c=CHUNKS), S).then_inc(ex_out, 16)
            sp.wait_ge(ex_out, 16)

        @block.scalar
        def _(act):
            act.wait_ge(diff, 1)
            nc.scalar.activation(S, S, ACT.Exp, scale=SCALE).then_inc(exped, 1)

        @block.vector
        def _(dve):
            t = Tally(dve, chain)
            dve.wait_ge(key_in, 16 * HEADS)
            t.inc(nc.vector.memset(CUT[:, 0:1], -BIG))
            t.inc(nc.vector.memset(CUT[:, CLEN:CLEN + 1], -BIG))
            t.link(nc.vector.tensor_tensor(CUT[:, 1:CLEN], KEY[:, 1:CLEN], KEY[:, 0:CLEN - 1], ALU.not_equal))
            t.link(nc.vector.tensor_scalar(CUT[:, 1:CLEN], CUT[:, 1:CLEN], -BIG, None, ALU.mult))
            dve.wait_ge(s_in, 16)
            t.link(nc.vector.tensor_tensor_scan(M, CUT[:, 0:CLEN], S, -BIG, ALU.add, ALU.max))
            t.link(nc.vector.tensor_tensor_scan(M[:, ::-1], CUT[:, 1:CLEN + 1][:, ::-1], M[:, ::-1], -BIG, ALU.add, ALU.max))
            nc.vector.tensor_copy(END[:, 0:2], M[:, 0:CLEN:CLEN - 1]).then_inc(end_made, 1)
            nc.vector.tensor_copy(END[:, 2:4], KEY[:, 0:CLEN:CLEN - 1]).then_inc(end_made, 1)
            dve.wait_ge(ends_in, 16 * HEADS)
            ends = ENDS.rearrange("p (c v k) -> p c v k", v=2, k=2)
            msk = MSK.rearrange("p (c k) -> p c k", k=2)
            for e in range(2):
                t.link(nc.vector.tensor_scalar(msk, ends[:, :, 1, :], END[:, 2 + e:3 + e], -BIG, ALU.not_equal, ALU.mult))
                t.link(nc.vector.tensor_tensor(msk, msk, ends[:, :, 0, :], ALU.add))
                t.link(nc.vector.tensor_reduce(TOP[:, e:e + 1], MSK, AX, ALU.max))
            for e in range(2):
                t.link(nc.vector.tensor_scalar(CUT[:, 0:CLEN], KEY, END[:, 2 + e:3 + e], -BIG, ALU.not_equal, ALU.mult))
                t.link(nc.vector.scalar_tensor_tensor(out=M, in0=CUT[:, 0:CLEN], scalar=TOP[:, e:e + 1], in1=M,
                                                      op0=ALU.add, op1=ALU.max))
            nc.vector.tensor_tensor(S, S, M, ALU.subtract).then_inc(diff, 1)


def aggregate_phase(nc, m, a):
    ACC = m.R1
    VG = m.slots.rearrange("p (j c) -> p j c", j=GROUP)
    OH = m.R2[:, 0:16 * P].rearrange("p (h j e) -> p h j e", h=2, j=8)
    WV = m.R2[:, 2048:2048 + GROUP * AW].rearrange("p (j c) -> p j c", j=GROUP)
    XT = m.R2[0:P // 2, 6400:6400 + 2 * P].rearrange("p (h e) -> p h e", h=2)
    EX = m.R2[:, 6656:6656 + P].rearrange("p (h n) -> p h n", h=2)
    at = [6784]

    def take(n):
        at[0] += n
        return m.R2[:, at[0] - n:at[0]]
    QI, XI, Z, H, XB = (take(D) for _ in range(5))
    QT = take(D).rearrange("p (k t) -> p k t", k=2)
    BST, ST, SD = take(8)[:, 0:6], take(2), take(2)[:, 0:1]
    assert NB + 2 < TURNS
    with ExitStack() as ctx:
        sem = lambda n: m.sem(n)
        PA = ctx.enter_context(nc.psum_tensor("PACC", [P, 4, 512], F32))
        PT = ctx.enter_context(nc.psum_tensor("PTG", [P, 2, 512], F32))
        passed, passed_v = sem("g_passed"), sem("g_passed_v")
        x_in = [sem(f"g_xin{h}") for h in range(2)]
        turned = [sem(f"g_turned{h}") for h in range(2)]
        zeroed, mulled, hot, summed, added = (sem(n) for n in ("g_zero", "g_mulled", "g_hot", "g_summed", "g_added"))
        idx_made = [sem(f"g_idx{h}") for h in range(2)]
        v_in = [sem(f"g_v{j}") for j in range(GROUP)]
        w_made = [sem(f"g_w{h}") for h in range(2)]
        PZT = ctx.enter_context(nc.psum_tensor("PZT", [P, 512], F32))
        PZM = ctx.enter_context(nc.psum_tensor("PZM", [P, 512], F32))
        q_in, zx_in, z_turned, z_copied, z_mixed, z_taken = (sem(n) for n in (
            "z_qin", "z_xin", "z_turned", "z_copied", "z_mixed", "z_taken"))
        z_var, z_std, z_made, z_out, chain = (sem(n) for n in ("z_var", "z_std", "z_made", "z_out", "z_chain"))
        mulled_act = sem("g_mulled_act")
        block = ctx.enter_context(nc.Block())

        def wait_mulled(eng, i, j):
            if j % 8 == 7:
                eng.wait_ge(mulled_act, i * 2 + (j // 8 + 1))
            else:
                eng.wait_ge(mulled, i * 14 + (j // 8 * 7 + j % 8 + 1))

        @block.gpsimd
        def _(pool):
            def gather(i, first):
                for h in range(2):
                    pool.wait_ge(idx_made[h], i + 1)
                    for j in range(8 * h, 8 * h + 8):
                        if j % 2 == 0 and not first:
                            wait_mulled(pool, i - 1, j)
                            wait_mulled(pool, i - 1, j + 1)
                        if j % 2 == 0:
                            pool.sem_inc(passed, 1)
                        nc.gpsimd.indirect_dma_start(
                            out=VG[:, j, :], out_offset=None, in_=m.v_d[:, :],
                            in_offset=bass.IndirectOffsetOnAxis(ap=m.IDX[:, j:j + 1], axis=0)).then_inc(v_in[j], 16)
            gather(0, True)
            with pool.Fori(1, TURNS) as i:
                gather(i, False)

        @block.sync
        def _(sp):
            def load(i, h):
                sp.dma_start(XT[:, h, :], half_rows(m.ex_d, i, h)).then_inc(x_in[h], 16)

            def loads(i):
                for h in range(2):
                    sp.wait_ge(turned[h], i + 1)
                    load(i + 1, h)

            def load_q(b):
                sp.dma_start(QI, m.qs_d[ds(b * P, P), :]).then_inc(q_in, 16)

            def store_z(b):
                sp.wait_ge(z_made, b + 1)
                sp.dma_start(m.z_d[ds(b * P, P), :], Z).then_inc(z_out, 16)
            load(0, 0)
            load(0, 1)
            load_q(0)
            sp.dma_start(XI, a.x[0:P, :]).then_inc(zx_in, 16)
            loads(0)
            sp.wait_ge(z_turned, 1)
            load_q(1)
            with sp.Fori(1, NB - 1) as i:
                loads(i)
                sp.wait_ge(z_turned, i + 1)
                load_q(i + 1)
                store_z(i - 1)
                sp.dma_start(XI, a.x[ds(i * P, P), :]).then_inc(zx_in, 16)
            loads(NB - 1)
            store_z(NB - 2)
            sp.dma_start(XI[0:NLAST, :], a.x[(NB - 1) * P:N, :]).then_inc(zx_in, 16)
            loads(NB)
            store_z(NB - 1)
            with sp.Fori(NB + 1, TURNS - 1) as i:
                loads(i)
            sp.wait_ge(z_out, 16 * NB)

        @block.scalar
        def _(act):
            def weights(i, h, first):
                act.wait_ge(turned[h], i + 1)
                if not first:
                    wait_mulled(act, i - 1, 8 * h + 6)
                    act.wait_ge(summed, i * GROUP + 8 * h - 8)
                nc.scalar.activation(EX[:, h, :], PT[:, h, 0:P // 2], ACT.Copy).then_inc(w_made[h], 1)
                nc.scalar.activation(WV[:, 8 * h:8 * h + 8, D:AW], PT[:, h, 0:P // 2].rearrange("p (j h) -> p j h", j=8),
                                     ACT.Copy).then_inc(w_made[h], 1)

            def multiply(i, h):
                j = 8 * h + 7
                act.wait_ge(v_in[j], (i + 1) * 16)
                act.wait_ge(w_made[h], i * 2 + 2)
                for head in range(HEADS):
                    part = slice(head * DH, (head + 1) * DH)
                    ins = nc.scalar.activation(WV[:, j, part], VG[:, j, part], ACT.Copy,
                                               scale=EX[:, h, 7 * HEADS + head:7 * HEADS + head + 1])
                ins.then_inc(mulled_act, 1)

            def root(b):
                act.wait_ge(z_var, b + 1)
                nc.scalar.activation(SD, ST[:, 1:2], ACT.Sqrt, bias=m.eps[:, :]).then_inc(z_std, 1)

            def copy_q(b):
                act.wait_ge(z_turned, b + 1)
                nc.scalar.activation(QT, PZT[:, 0:D].rearrange("p (k t) -> p k t", k=2), ACT.Copy).then_inc(z_copied, 1)
            weights(0, 0, True)
            weights(0, 1, True)
            copy_q(0)
            for h in range(2):
                multiply(0, h)
                weights(1, h, False)
            with act.Fori(1, NB) as i:
                root(i - 1)
                copy_q(i)
                for h in range(2):
                    multiply(i, h)
                    weights(i + 1, h, False)
            root(NB - 1)
            with act.Fori(NB, TURNS - 1) as i:
                for h in range(2):
                    multiply(i, h)
                    weights(i + 1, h, False)
            multiply(TURNS - 1, 0)
            multiply(TURNS - 1, 1)

        @block.tensor
        def _(pe):
            def turn(i, h, first):
                pe.wait_ge(x_in[h], (i + 1) * 16)
                if not first:
                    pe.wait_ge(w_made[h], i * 2)
                pe.sem_inc(passed, 1)
                nc.tensor.transpose(PT[:, h, 0:P // 2], XT[:, h, :], m.ident[0:P // 2, 0:P // 2]).then_inc(turned[h], 1)

            def turn_q(b, first):
                pe.wait_ge(q_in, (b + 1) * 16)
                if not first:
                    pe.wait_ge(z_copied, b + 0)
                for k in range(2):
                    ins = nc.tensor.transpose(PZT[:, k * P:(k + 1) * P], QI[:, k * P:(k + 1) * P], m.ident[:, :])
                ins.then_inc(z_turned, 1)

            def mix(b, first):
                pe.wait_ge(z_copied, b + 1)
                if not first:
                    pe.wait_ge(z_taken, b + 0)
                for k in range(2):
                    ins = nc.tensor.matmul(PZM[:, 0:D], QT[:, k, :], m.Wmix[:, k, :], start=(k == 0), stop=(k == 1))
                ins.then_inc(z_mixed, 1)

            def sums(i, first, last, z):
                for j in range(GROUP):
                    if z and j == 3:
                        turn_q(i, first)
                    if z and j == 12:
                        mix(i, first)
                    if j % 8 == 0:
                        pe.wait_ge(hot, i * 2 + j // 8 + 1)
                        pe.wait_ge(w_made[j // 8], i * 2 + 2)
                    if j == 8 and not last:
                        turn(i + 1, 0, False)
                    wait_mulled(pe, i, j)
                    if j >= 4 or not first:
                        pe.wait_ge(added, i * GROUP + j - 3)
                    nc.tensor.matmul(PA[:, j % 4, 0:AW], OH[:, j // 8, j % 8, :], WV[:, j, :],
                                     start=True, stop=True).then_inc(summed, 1)
                if not last:
                    turn(i + 1, 1, False)
            turn(0, 0, True)
            turn(0, 1, True)
            sums(0, True, False, True)
            with pe.Fori(1, NB) as i:
                sums(i, False, False, True)
            with pe.Fori(NB, TURNS - 1) as i:
                sums(i, False, False, False)
            sums(TURNS - 1, False, True, False)

        @block.vector
        def _(dve):
            t = Tally(dve, chain)

            def z_stats(b):
                dve.wait_ge(z_mixed, b + 1)
                t.link(nc.vector.bn_stats(BST, PZM[:, 0:D]))
                dve.sem_inc(passed_v, 1)
                nc.vector.bn_aggr(ST, BST).then_inc(z_var, 1)

            def z_start(b):
                dve.wait_ge(z_std, b + 1)
                dve.wait_ge(z_var, b + 1)
                t.inc(nc.vector.reciprocal(SD, SD))

            def z_terms(b, k):
                if k == 0:
                    nc.vector.scalar_tensor_tensor(out=H, in0=PZM[:, 0:D], scalar=ST[:, 0:1], in1=m.rows[:, 2, :],
                                                   op0=ALU.subtract, op1=ALU.mult).then_inc(z_taken, 1)
                else:
                    dve.wait_ge(zx_in, (b + 1) * 16)
                    t.inc(nc.vector.tensor_tensor(XB, XI, m.rows[:, 1, :], ALU.add))

            def z_finish(b, first):
                t.wait()
                dve.wait_ge(z_taken, b + 1)
                if not first:
                    dve.wait_ge(z_out, b * 16)
                nc.vector.scalar_tensor_tensor(out=Z, in0=H, scalar=SD, in1=XB,
                                               op0=ALU.mult, op1=ALU.add).then_inc(z_made, 1)

            def index(i, h, first=False):
                if not first:
                    dve.wait_ge(v_in[8 * h + 7], i * 16)
                    dve.sem_inc(passed_v, 1)
                nc.vector.tensor_copy(m.IDX[:, 8 * h:8 * h + 8], m.SRC[:, ds(i * GROUP + 8 * h, 8)]).then_inc(idx_made[h], 1)

            def hots(i, h):
                nc.vector.tensor_tensor(OH[:, h, :, :], m.iota_row[:, :].rearrange("p (o n) -> p o n", o=1).broadcast_to([P, 8, P]),
                                        m.REL[:, ds(i * GROUP + 8 * h, 8)].rearrange("p (j o) -> p j o", o=1).broadcast_to([P, 8, P]),
                                        ALU.is_equal).then_inc(hot, 1)

            def multiply(i, j):
                dve.wait_ge(v_in[j], (i + 1) * 16)
                if j % 8 == 0:
                    dve.wait_ge(w_made[j // 8], i * 2 + 2)
                nc.vector.tensor_tensor(
                    WV[:, j, 0:D].rearrange("p (h d) -> p h d", d=DH), VG[:, j, :].rearrange("p (h d) -> p h d", d=DH),
                    EX[:, j // 8, (j % 8) * HEADS:(j % 8 + 1) * HEADS].rearrange("p (h o) -> p h o", o=1)
                    .broadcast_to([P, HEADS, DH]), ALU.mult).then_inc(mulled, 1)

            def add(i, j, b, first):
                dve.wait_ge(summed, i * GROUP + j + 1)
                if j or not first:
                    dve.wait_ge(added, i * GROUP + j)
                nc.vector.tensor_tensor(ACC[:, ds(b * AW, AW)], ACC[:, ds(b * AW, AW)], PA[:, j % 4, 0:AW],
                                        ALU.add).then_inc(added, 1)

            def turn(i, first, last, z):
                for g in range(8):
                    if g == 0:
                        hots(i, 1)
                    if g % 4 == 1:
                        block_of = blocks_of(nc, m, mybir.EngineType.DVE, i, g // 4)
                    if z and g == 3:
                        z_start(i - 1)
                    if g == 4 and not last:
                        index(i + 1, 0)
                    for k in range(2):
                        if (2 * g + k) % 8 < 7:
                            multiply(i, 2 * g + k)
                        if g:
                            j = 2 * g - 2 + k
                            add(i, j, block_of[j % 8], first)
                        if z and g == 3:
                            z_terms(i - 1, k)
                    if z and g == 1:
                        z_stats(i - 1)
                    if z and g == 4:
                        z_finish(i - 1, z == 1)
                    if g == 4 and not last:
                        hots(i + 1, 0)
                if not last:
                    index(i + 1, 1)
                add(i, GROUP - 2, block_of[6], False)
                add(i, GROUP - 1, block_of[7], False)
            nc.vector.memset(ACC[:, 0:NB * AW], 0.0).then_inc(zeroed, 1)
            dve.wait_ge(zeroed, 1)
            index(0, 0, True)
            index(0, 1, True)
            hots(0, 0)
            turn(0, True, False, 0)
            turn(1, False, False, 1)
            with dve.Fori(2, NB + 1) as i:
                t.enter(i - 2, 3)
                turn(i, False, False, 2)
                t.leave(NB - 1)
            with dve.Fori(NB + 1, TURNS - 1) as i:
                turn(i, False, False, 0)
            turn(TURNS - 1, False, True, 0)


def output_phase(nc, m, a):
    ACC = m.R1
    at = [0]

    def take(n, k=0):
        at[0] += 2 * n
        v = m.R2[:, at[0] - 2 * n:at[0]].rearrange("p (u c) -> p u c", u=2)
        return v.rearrange("p u (k c) -> p u k c", k=k) if k else v
    NI, ZI, AI, Y, G, X1, X2, BASE = (take(D) for _ in range(8))
    AT = take(D, 2)
    JUNK = take(D)[:, 0, :]
    DEN, BST, ST, SD, W = take(HEADS), take(16, 2), take(4, 2), take(2), take(2)
    with ExitStack() as ctx:
        sem = lambda n: m.sem(n)
        pair = lambda n: [m.sem(f"{n}{u}") for u in range(2)]
        PT = ctx.enter_context(nc.psum_tensor("POT", [P, 2, 512], F32))
        PO = ctx.enter_context(nc.psum_tensor("POO", [P, 2, 512], F32))
        n_in, z_in, x2_out, base_out = (pair(n) for n in ("o_nin", "o_zin", "o_x2out", "o_baseout"))
        at_made, turned, at_copied, o_made, y_made = (sem(n) for n in ("o_at", "o_turned", "o_copied", "o_made", "o_y"))
        var1, std1, var2, std2, x2_made, x1_made, base_made = (sem(n) for n in (
            "o_var1", "o_std1", "o_var2", "o_std2", "o_x2", "o_x1", "o_base"))
        chain, passed, g_made = sem("o_chain"), sem("o_passed"), sem("o_g")
        block = ctx.enter_context(nc.Block())

        class At:

            def __init__(self, i, u, stage=0):
                self.u = (u - stage) % 2
                self.k = i + (u - stage - self.u) // 2
                self.b = self.k * 2 + self.u
                self.first = isinstance(i, int) and self.k < 1
                self.real = not isinstance(i, int) or 0 <= self.b < NB

        @block.sync
        def _(sp):
            def load(c, n=P):
                if not c.first:
                    sp.wait_ge(y_made, c.b - 1)
                sp.dma_start(NI[:, c.u, :], m.xn_d[ds(c.b * P, P), :]).then_inc(n_in[c.u], 16)
                if not c.first:
                    sp.wait_ge(x1_made, c.b - 1)
                sp.dma_start(ZI[:, c.u, :], m.z_d[ds(c.b * P, P), :]).then_inc(z_in[c.u], 16)

            def store(c, n=P):
                sp.wait_ge(x2_made, c.b + 1)
                sp.dma_start(m.xn2_d[ds(c.b * P, P), :], X2[:, c.u, :]).then_inc(x2_out[c.u], 16)
                sp.wait_ge(base_made, c.b + 1)
                sp.dma_start(a.out[ds(c.b * P, n), :], BASE[0:n, c.u, :]).then_inc(base_out[c.u], 16)
            load(At(0, 0))
            load(At(0, 1))
            with sp.Fori(1, NB // 2) as i:
                for u in range(2):
                    load(At(i, u))
                    store(At(i - 1, u))
            for b in range(NB // 2 * 2, NB):
                load(At(b // 2, b % 2))
            for b in range(NB // 2 * 2 - 2, NB):
                store(At(b // 2, b % 2), P if b < NB - 1 else NLAST)
            for u in range(2):
                sp.wait_ge(x2_out[u], 16 * ((NB + 1 - u) // 2))
                sp.wait_ge(base_out[u], 16 * ((NB + 1 - u) // 2))

        @block.gpsimd
        def _(pool):
            def base(c):
                pool.wait_ge(x2_made, c.b + 1)
                pool.wait_ge(x1_made, c.b + 1)
                if not c.first:
                    pool.wait_ge(base_out[c.u], c.k * 16)
                nc.gpsimd.tensor_tensor(BASE[:, c.u, :], X1[:, c.u, :], X2[:, c.u, :], ALU.add).then_inc(base_made, 1)
            base(At(0, 0))
            base(At(0, 1))
            with pool.Fori(1, NB // 2) as i:
                for u in range(2):
                    base(At(i, u))
            for b in range(NB // 2 * 2, NB):
                base(At(b // 2, b % 2))

        def staged(eng, step):
            for t in range(4):
                step(t // 2, t % 2)
            with eng.Fori(2, NB // 2) as i:
                for u in range(2):
                    step(i, u)
            for t in range(NB // 2 * 2, NB + 3):
                step(t // 2, t % 2)

        @block.scalar
        def _(act):
            def step(i, u):
                c = At(i, u)
                if c.real:
                    act.wait_ge(turned, c.b + 1)
                    nc.scalar.activation(AT[:, c.u, :, :], PT[:, c.u, 0:D].rearrange("p (k t) -> p k t", k=2),
                                         ACT.Copy).then_inc(at_copied, 1)
                for stage, var, std in ((1, var1, std1), (2, var2, std2)):
                    c = At(i, u, stage)
                    if c.real:
                        act.wait_ge(var, c.b + 1)
                        nc.scalar.activation(SD[:, c.u, stage - 1:stage], ST[:, c.u, stage - 1, 1:2], ACT.Sqrt,
                                             bias=m.eps[:, :]).then_inc(std, 1)
            staged(act, step)

        @block.tensor
        def _(pe):
            def attend(c):
                pe.wait_ge(at_made, c.b + 1)
                for k in range(2):
                    ins = nc.tensor.transpose(PT[:, c.u, k * P:(k + 1) * P], AI[:, c.u, k * P:(k + 1) * P], m.ident[:, :])
                ins.then_inc(turned, 1)
                pe.wait_ge(at_copied, c.b + 1)
                if not c.first:
                    pe.wait_ge(y_made, c.b - 1)
                for k in range(2):
                    ins = nc.tensor.matmul(PO[:, c.u, 0:D], AT[:, c.u, k, :], m.Wo[:, k, :], start=(k == 0), stop=(k == 1))
                ins.then_inc(o_made, 1)
            attend(At(0, 0))
            attend(At(0, 1))
            with pe.Fori(1, NB // 2) as i:
                for u in range(2):
                    attend(At(i, u))
            for b in range(NB // 2 * 2, NB):
                attend(At(b // 2, b % 2))

        @block.vector
        def _(dve):
            t = Tally(dve, chain)

            def step(i, u):
                c0, c1, c2, c3 = (At(i, u, stage) for stage in range(4))
                if c0.real:
                    den = DEN[:, c0.u, :]
                    t.link(nc.vector.tensor_scalar(den, ACC[:, ds(c0.b * AW + D, HEADS)], 1e-9, None, ALU.add))
                    t.inc(nc.vector.reciprocal(den, den))
                if c3.real:
                    dve.wait_ge(std2, c3.b + 1)
                    t.link(nc.vector.reciprocal(SD[:, c3.u, 1:2], SD[:, c3.u, 1:2]))
                    if not c3.first:
                        dve.wait_ge(x2_out[c3.u], c3.k * 16)
                        dve.wait_ge(base_made, c3.b - 1)
                    nc.vector.tensor_scalar(X2[:, c3.u, :], X1[:, c3.u, :], ST[:, c3.u, 1, 0:1], SD[:, c3.u, 1:2],
                                            ALU.subtract, ALU.mult).then_inc(x2_made, 1)
                elif c0.real:
                    t.wait()
                if c0.real:
                    nc.vector.tensor_tensor(AI[:, c0.u, :].rearrange("p (h d) -> p h d", d=DH),
                                            ACC[:, ds(c0.b * AW, D)].rearrange("p (h d) -> p h d", d=DH),
                                            den.rearrange("p (h o) -> p h o", o=1).broadcast_to([P, HEADS, DH]),
                                            ALU.mult).then_inc(at_made, 1)
                if c2.real:
                    dve.wait_ge(std1, c2.b + 1)
                    t.inc(nc.vector.reciprocal(SD[:, c2.u, 0:1], SD[:, c2.u, 0:1]))
                if c3.real:
                    dve.wait_ge(x2_made, c3.b + 1)
                    t.inc(nc.vector.tensor_tensor_reduce(out=JUNK, in0=X2[:, c3.u, :], in1=m.rows[:, 4, :], scale=1.0, scalar=0.0,
                                                         op0=ALU.mult, op1=ALU.add, accum_out=W[:, c3.u, 0:1]))
                if c1.real:
                    dve.wait_ge(o_made, c1.b + 1)
                    dve.wait_ge(n_in[c1.u], (c1.k + 1) * 16)
                    nc.vector.tensor_tensor(Y[:, c1.u, :], PO[:, c1.u, 0:D], NI[:, c1.u, :], ALU.add).then_inc(y_made, 1)
                if c2.real:
                    t.wait()
                    dve.wait_ge(z_in[c2.u], (c2.k + 1) * 16)
                    dve.wait_ge(g_made, c2.b + 1)
                    if not c2.first:
                        dve.wait_ge(base_made, c2.b - 1)
                    nc.vector.scalar_tensor_tensor(out=X1[:, c2.u, :], in0=G[:, c2.u, :], scalar=SD[:, c2.u, 0:1],
                                                   in1=ZI[:, c2.u, :], op0=ALU.mult, op1=ALU.add).then_inc(x1_made, 1)
                if c1.real:
                    dve.wait_ge(y_made, c1.b + 1)
                    t.inc(nc.vector.bn_stats(BST[:, c1.u, 0, 0:6], Y[:, c1.u, :]))
                if c2.real:
                    dve.wait_ge(x1_made, c2.b + 1)
                    t.inc(nc.vector.bn_stats(BST[:, c2.u, 1, 0:6], X1[:, c2.u, :]))
                if c1.real or c2.real:
                    t.wait()
                    dve.sem_inc(passed, 1)
                if c1.real:
                    nc.vector.bn_aggr(ST[:, c1.u, 0, 0:2], BST[:, c1.u, 0, 0:6]).then_inc(var1, 1)
                if c2.real:
                    nc.vector.bn_aggr(ST[:, c2.u, 1, 0:2], BST[:, c2.u, 1, 0:6]).then_inc(var2, 1)
                if c3.real:
                    t.wait()
                    t.inc(nc.vector.tensor_copy(m.weight[:, ds(c3.b, 1)], W[:, c3.u, 0:1]))
                if c1.real:
                    dve.wait_ge(var1, c1.b + 1)
                    nc.vector.scalar_tensor_tensor(out=G[:, c1.u, :], in0=Y[:, c1.u, :], scalar=ST[:, c1.u, 0, 0:1],
                                                   in1=m.rows[:, 0, :], op0=ALU.subtract, op1=ALU.mult).then_inc(g_made, 1)
            for b in range(4):
                step(b // 2, b % 2)
            with dve.Fori(2, NB // 2) as i:
                t.enter(i - 2, 16)
                step(i, 0)
                step(i, 1)
                t.leave(NB // 2 - 2)
            for b in range(NB // 2 * 2, NB + 3):
                step(b // 2, b % 2)
            t.wait()
            t.link(nc.vector.tensor_scalar(m.weight[:, :], m.weight[:, :], m.brc[:, 0:1], None, ALU.add))


def feed_forward_phase(nc, m, a):
    KT = -(-KEEP // P)
    groups, rest = KT // 4, KT % 4
    KLAST = KEEP - (KT - 1) * P
    DIGIT = 16
    assert rest == 1 and KT + 1 < P and NB < P
    at = [0]

    def take(n, dt=F32):
        at[0] += n
        v = m.R2[:, at[0] - n:at[0]]
        return v if dt is F32 else v.bitcast(dt)
    HOT = take(NB * P).rearrange("p (b q) -> p b q", b=NB)
    LIST = take(NB * 2 * KT).rearrange("p (b k t) -> p b k t", b=NB, k=2)
    XG, BG, TMP, RES = (take(4 * D).rearrange("p (b c) -> p b c", b=4) for _ in range(4))
    W1 = m.slots[:, 0:2 * FF].rearrange("p (k n) -> p k n", k=2)
    W2 = m.slots[:, 2 * FF:4 * FF].rearrange("p (c n) -> p c n", c=8)
    HT = m.EX[:, 0:8 * 512].rearrange("p (c t) -> p c t", c=8)
    XT = m.EX[:, 4096:4096 + 1024].rearrange("p (k t) -> p k t", k=2)
    S = [m.EX[:, 5120 + 64 * k:5120 + 64 * k + NB] for k in range(9)]
    HI, LO, NEG, SGN, KEY, T1, T2, SEL, TIE = S
    C = m.EX[:, 5700:5716]
    TRIAL, HITS, COUNT, ABOVE = (m.EX[:, 5720 + 16 * k:5720 + 16 * k + DIGIT - 1] for k in range(4))
    FOUND = m.EX[:, 5800:5800 + 2 * KT].rearrange("p (k t) -> p k t", k=2)
    TOKEN = m.EX[:, 5860:5860 + KT].bitcast(I32)
    IX, IB, IS = (m.EX[:, 5900 + 4 * k:5904 + 4 * k].bitcast(I32) for k in range(3))
    CMP = m.EX[:, 5920:5920 + (DIGIT - 1) * NB].rearrange("p (k b) -> p k b", b=NB)
    U32 = mybir.dt.uint32
    with ExitStack() as ctx:
        sem = lambda n: m.sem(n)
        PH = ctx.enter_context(nc.psum_tensor("PFH", [P, 4, 512], F32))
        PY = ctx.enter_context(nc.psum_tensor("PFY", [P, 2, 512], F32))
        PX = ctx.enter_context(nc.psum_tensor("PFX", [P, 2, 512], F32))
        PS, PL = PX[:, 0, :], PX[:, 1, :]
        w_in, chain, counted, total, ties, tied, kept, ranked = (sem(n) for n in (
            "f_win", "f_chain", "f_cnt", "f_tot", "f_ties", "f_tied", "f_kept", "f_rank"))
        listed_out = sem("f_listed_out")
        hot, listed, x_turned, x_copied = (sem(n) for n in ("f_hot", "f_listed", "f_xturned", "f_xcopied"))
        h_made, h_act, y_made, y_taken, done, passed = (sem(n) for n in (
            "f_h", "f_act", "f_y", "f_ytaken", "f_done", "f_passed"))
        passed_v = sem("f_passed_v")
        ix, ib, iz = sem("f_ix"), sem("f_ib"), sem("f_is")
        x_in, b_in, out_done = ([sem(f"{n}{b}") for b in range(4)] for n in ("f_x", "f_b", "f_out"))
        block = ctx.enter_context(nc.Block())

        @block.sync
        def _(sp):
            sp.dma_start(W1, a.L0_ffn_w1.rearrange("(k p) n -> p k n", p=P)).then_inc(w_in, 16)
            sp.dma_start(W2, a.L0_ffn_w2.rearrange("(c p) n -> p c n", p=P)).then_inc(w_in, 16)

        @block.gpsimd
        def _(pool):
            def gather(out, source, index, signal):
                nc.gpsimd.indirect_dma_start(out=out, out_offset=None, in_=source,
                                             in_offset=bass.IndirectOffsetOnAxis(ap=index, axis=0)).then_inc(signal, 16)

            def gather_x(i, n, first):
                pool.wait_ge(ix, i + 1)
                if not first:
                    pool.wait_ge(x_turned, i + 0)
                pool.sem_inc(passed, 1)
                for b in range(n):
                    gather(XG[:, b, :], m.xn2_d[:, :], IX[:, b:b + 1], x_in[b])

            def gather_base(i, b, first):
                if b == 0:
                    pool.wait_ge(ib, i + 1)
                if not first:
                    pool.wait_ge(done, i * 4 + b - 3)
                pool.sem_inc(passed, 1)
                gather(BG[:, b, :], a.out[:, :], IB[:, b:b + 1], b_in[b])

            def scatter(i, b, n):
                if b == 0:
                    pool.wait_ge(iz, i + 1)
                pool.wait_ge(done, i * 4 + b + 1)
                pool.sem_inc(passed, 1)
                nc.gpsimd.indirect_dma_start(
                    out=a.out[:, :], out_offset=bass.IndirectOffsetOnAxis(ap=IS[0:n, b:b + 1], axis=0),
                    in_=RES[0:n, b, :], in_offset=None).then_inc(out_done[b], 16)
            gather_x(0, 4, True)
            for b in range(4):
                gather_base(0, b, True)
            with pool.Fori(0, groups - 1) as i:
                gather_x(i + 1, 4, False)
                for b in range(4):
                    scatter(i, b, P)
                    gather_base(i + 1, b, False)
            gather_x(groups, rest, False)
            for b in range(4):
                scatter(groups - 1, b, P)
                if b < rest:
                    gather_base(groups, b, False)
            scatter(groups, 0, KLAST)
            for b in range(4):
                pool.wait_ge(out_done[b], 16 * (groups + (b < rest)))

        @block.scalar
        def _(act):
            def copy_x(i, n):
                act.wait_ge(x_turned, i + 1)
                for k in range(2):
                    nc.scalar.activation(XT[:, k, 0:n], PX[:, k, 0:n], ACT.Copy).then_inc(x_copied, 1)

            def gelu(i, n, first):
                for c in range(8):
                    act.wait_ge(h_made, i * 8 + c + 1)
                    if not first and c == 0:
                        act.wait_ge(y_made, i * 4 + 0)
                    nc.scalar.activation(HT[:, c, 0:n], PH[:, c % 4, 0:n], ACT.Gelu_apprx_tanh,
                                         bias=m.b1c[:, c:c + 1]).then_inc(h_act, 1)
            copy_x(0, 512)
            gelu(0, 512, True)
            copy_x(1, 512)
            with act.Fori(1, groups - 1) as i:
                gelu(i, 512, False)
                copy_x(i + 1, 512)
            gelu(groups - 1, 512, False)
            copy_x(groups, rest * P)
            gelu(groups, rest * P, False)

        @block.tensor
        def _(pe):
            with pe.Fori(0, 8) as r:
                pe.wait_ge(counted, r + 1)
                nc.tensor.matmul(PS[:, 0:DIGIT - 1], m.ones[:, :], COUNT, start=True, stop=True).then_inc(total, 1)
            pe.wait_ge(ties, 1)
            nc.tensor.matmul(PS[:, 64:64 + NB], m.ones[:, :], SEL, start=True, stop=True)
            nc.tensor.matmul(PS[:, 128:128 + NB], m.upper[:, :], TIE, start=True, stop=True)
            nc.tensor.matmul(PS[:, 192:192 + NB], m.ones[:, :], TIE, start=True, stop=True).then_inc(tied, 1)
            pe.wait_ge(kept, 1)
            nc.tensor.matmul(PS[:, 256:256 + NB], m.upper[:, :], SEL, start=True, stop=True)
            nc.tensor.matmul(PS[:, 320:320 + NB], m.ones[:, :], SEL, start=True, stop=True).then_inc(ranked, 1)
            for b in range(NB):
                if b % 7 == 0:
                    pe.wait_ge(hot, b // 7 + 1)
                ins = nc.tensor.matmul(PL[:, 0:2 * KT], HOT[:, b, :], LIST[:, b, :, :].rearrange("p k t -> p (k t)"),
                                       start=(b == 0), stop=(b == NB - 1))
            ins.then_inc(listed, 1)

            def turn(i, n):
                for b in range(n):
                    pe.wait_ge(x_in[b], (i + 1) * 16)
                    for k in range(2):
                        ins = nc.tensor.transpose(PX[:, k, b * P:(b + 1) * P], XG[:, b, k * P:(k + 1) * P], m.ident[:, :])
                ins.then_inc(x_turned, 1)

            def hidden(i, n, first):
                pe.wait_ge(x_copied, i * 2 + 2)
                for c in range(8):
                    if c >= 4 or not first:
                        pe.wait_ge(h_act, i * 8 + c - 3)
                    for k in range(2):
                        ins = nc.tensor.matmul(PH[:, c % 4, 0:n], W1[:, k, c * P:(c + 1) * P], XT[:, k, 0:n],
                                               start=(k == 0), stop=(k == 1))
                    ins.then_inc(h_made, 1)

            def out(i, n, first):
                pe.wait_ge(h_act, i * 8 + 8)
                for b in range(n):
                    if b >= 2 or not first:
                        pe.wait_ge(y_taken, i * 4 + b - 1)
                    for c in range(8):
                        ins = nc.tensor.matmul(PY[:, b % 2, 0:D], HT[:, c, b * P:(b + 1) * P], W2[:, c, :],
                                               start=(c == 0), stop=(c == 7))
                    ins.then_inc(y_made, 1)
            pe.wait_ge(listed_out, 1)
            turn(0, 4)
            pe.wait_ge(w_in, 32)
            hidden(0, 512, True)
            turn(1, 4)
            out(0, 4, True)
            with pe.Fori(1, groups - 1) as i:
                hidden(i, 512, False)
                turn(i + 1, 4)
                out(i, 4, False)
            hidden(groups - 1, 512, False)
            turn(groups, rest)
            out(groups - 1, 4, False)
            hidden(groups, rest * P, False)
            out(groups, rest, False)

        @block.vector
        def _(dve):
            t = Tally(dve, chain)
            bits = m.weight[:, :].bitcast(U32)
            t.link(nc.vector.tensor_scalar(m.weight[:, :], m.weight[:, :], 0.0, None, ALU.add))
            t.inc(nc.vector.tensor_scalar(T1.bitcast(U32), bits, 16, None, ALU.logical_shift_right))
            t.inc(nc.vector.tensor_scalar(T2.bitcast(U32), bits, 65535, None, ALU.bitwise_and))
            t.link(nc.vector.tensor_scalar(NEG, m.weight[:, :], 0.0, None, ALU.is_lt))
            t.inc(nc.vector.tensor_copy(HI, T1.bitcast(U32)))
            t.inc(nc.vector.tensor_copy(LO, T2.bitcast(U32)))
            t.link(nc.vector.tensor_scalar(SGN, NEG, -2.0, 1.0, ALU.mult, ALU.add))
            t.inc(nc.vector.tensor_tensor(LO, LO, SGN, ALU.mult))
            t.link(nc.vector.tensor_tensor(HI, HI, SGN, ALU.mult))
            t.inc(nc.vector.scalar_tensor_tensor(out=LO, in0=NEG, scalar=65535.0, in1=LO, op0=ALU.mult, op1=ALU.add))
            t.link(nc.vector.scalar_tensor_tensor(out=HI, in0=NEG, scalar=65535.0 - 32768.0, in1=HI, op0=ALU.mult, op1=ALU.add))
            t.inc(nc.vector.tensor_scalar(T1[:, 0:1], m.iota_col[:, 0:1], float(NLAST), None, ALU.is_lt))
            t.link(nc.vector.tensor_scalar(HI, HI, 32768.0, None, ALU.add))
            t.link(nc.vector.scalar_tensor_tensor(out=HI[:, NB - 1:NB], in0=HI[:, NB - 1:NB], scalar=1.0, in1=T1[:, 0:1],
                                                  op0=ALU.add, op1=ALU.mult))
            t.link(nc.vector.tensor_scalar(HI[:, NB - 1:NB], HI[:, NB - 1:NB], -1.0, None, ALU.add))

            def search(key, base):
                t.inc(nc.vector.memset(C[:, 0:1], 0.0))
                t.inc(nc.vector.memset(C[:, 1:2], 4096.0))
                t.link(nc.vector.tensor_scalar(HITS, m.iota_row[:, 1:DIGIT], 4096.0, None, ALU.mult))
                with dve.Fori(0, 4) as r:
                    t.enter(r, 6)
                    t.link(nc.vector.tensor_scalar(TRIAL, HITS, C[:, 0:1], None, ALU.add))
                    t.link(nc.vector.tensor_tensor(CMP, key.rearrange("p (o b) -> p o b", o=1).broadcast_to([P, DIGIT - 1, NB]),
                                                   TRIAL.rearrange("p (k o) -> p k o", o=1).broadcast_to([P, DIGIT - 1, NB]),
                                                   ALU.is_ge))
                    nc.vector.tensor_reduce(COUNT, CMP, AX, ALU.add).then_inc(counted, 1)
                    t.inc(nc.vector.tensor_scalar(HITS, HITS, 0.0625, None, ALU.mult))
                    dve.wait_ge(total, r + (base + 1))
                    t.link(nc.vector.tensor_scalar(ABOVE, PS[:, 0:DIGIT - 1], float(KEEP), None, ALU.is_ge, ALU.add,
                                                   accum_out=C[:, 4:5]))
                    t.link(nc.vector.scalar_tensor_tensor(out=C[:, 0:1], in0=C[:, 4:5], scalar=C[:, 1:2], in1=C[:, 0:1],
                                                          op0=ALU.mult, op1=ALU.add))
                    t.link(nc.vector.tensor_scalar(C[:, 1:2], C[:, 1:2], 0.0625, None, ALU.mult))
                    t.leave(4)
            search(HI, 0)
            t.inc(nc.vector.tensor_scalar(T1, HI, C[:, 0:1], 65537.0, ALU.is_gt, ALU.mult))
            t.link(nc.vector.tensor_scalar(SEL, HI, C[:, 0:1], None, ALU.is_equal))
            t.link(nc.vector.scalar_tensor_tensor(out=KEY, in0=LO, scalar=1.0, in1=SEL, op0=ALU.add, op1=ALU.mult))
            t.link(nc.vector.tensor_tensor(KEY, KEY, T1, ALU.add))
            t.link(nc.vector.tensor_scalar(KEY, KEY, -1.0, None, ALU.add))
            search(KEY, 4)
            t.link(nc.vector.tensor_scalar(SEL, KEY, C[:, 0:1], None, ALU.is_gt))
            nc.vector.tensor_scalar(TIE, KEY, C[:, 0:1], None, ALU.is_equal).then_inc(ties, 1)
            dve.wait_ge(tied, 1)
            t.inc(nc.vector.tensor_reduce(C[:, 5:6], PS[:, 64:64 + NB], AX, ALU.add))
            t.inc(nc.vector.tensor_copy(T1, PS[:, 192:192 + NB]))
            t.link(nc.vector.memset(NEG, 0.0))
            t.inc(nc.vector.tensor_scalar(C[:, 5:6], C[:, 5:6], -1.0, float(KEEP), ALU.mult, ALU.add))
            t.link(nc.vector.tensor_tensor_scan(T2, NEG, T1, 0.0, ALU.add, ALU.add))
            t.link(nc.vector.tensor_tensor(T2, T2, T1, ALU.subtract))
            t.link(nc.vector.tensor_tensor(T2, T2, PS[:, 128:128 + NB], ALU.add))
            t.link(nc.vector.tensor_scalar(T2, T2, C[:, 5:6], None, ALU.is_le))
            t.link(nc.vector.tensor_tensor(T2, T2, TIE, ALU.mult))
            nc.vector.tensor_tensor(SEL, SEL, T2, ALU.add).then_inc(kept, 1)
            dve.wait_ge(ranked, 1)
            t.link(nc.vector.tensor_copy(T1, PS[:, 320:320 + NB]))
            t.link(nc.vector.tensor_tensor_scan(T2, NEG, T1, -1.0, ALU.add, ALU.add))
            t.link(nc.vector.tensor_tensor(T2, T2, T1, ALU.subtract))
            t.link(nc.vector.tensor_tensor(T2, T2, PS[:, 256:256 + NB], ALU.add))
            t.link(nc.vector.tensor_scalar(T2, T2, 0.0, None, ALU.max))
            t.link(nc.vector.tensor_copy(T1.bitcast(I32), T2))
            t.inc(nc.vector.tensor_scalar(HI.bitcast(I32), T1.bitcast(I32), 7, None, ALU.arith_shift_right))
            t.link(nc.vector.tensor_scalar(LO.bitcast(I32), T1.bitcast(I32), P - 1, None, ALU.bitwise_and))
            t.inc(nc.vector.tensor_copy(KEY, HI.bitcast(I32)))
            t.inc(nc.vector.tensor_scalar(TIE, m.iota_row[:, 0:NB], float(P), m.iota_col[:, 0:1], ALU.mult, ALU.add))
            t.link(nc.vector.tensor_copy(T2, LO.bitcast(I32)))
            dve.wait_ge(kept, 1)
            t.link(nc.vector.scalar_tensor_tensor(out=KEY, in0=KEY, scalar=1.0, in1=SEL, op0=ALU.add, op1=ALU.mult))
            t.link(nc.vector.tensor_scalar(KEY, KEY, -1.0, None, ALU.add))
            wide = lambda v: v.rearrange("p (b o) -> p b o", o=1).broadcast_to([P, NB, KT])
            t.link(nc.vector.tensor_tensor(LIST[:, :, 1, :], m.iota_row[:, 0:KT].rearrange("p (o t) -> p o t", o=1)
                                           .broadcast_to([P, NB, KT]), wide(KEY), ALU.is_equal))
            t.link(nc.vector.tensor_tensor(LIST[:, :, 0, :], LIST[:, :, 1, :], wide(TIE), ALU.mult))
            t.link(nc.vector.tensor_tensor(LIST[:, :, 1, :], LIST[:, :, 1, :], wide(m.weight[:, :]), ALU.mult))
            for b in range(0, NB, 7):
                nc.vector.tensor_tensor(HOT[:, b:b + 7, :], m.iota_row[:, :].rearrange("p (o n) -> p o n", o=1).broadcast_to([P, 7, P]),
                                        T2[:, b:b + 7].rearrange("p (b o) -> p b o", o=1).broadcast_to([P, 7, P]),
                                        ALU.is_equal).then_inc(hot, 1)
            dve.wait_ge(listed, 1)
            nc.vector.tensor_copy(FOUND.rearrange("p k t -> p (k t)"), PL[:, 0:2 * KT]).then_inc(listed_out, 1)
            dve.wait_ge(listed_out, 1)
            t.link(nc.vector.tensor_copy(TOKEN, FOUND[:, 0, :]))

            def index(to, i, n, signal, used):
                for b in range(4 if used is not None else 0):
                    dve.wait_ge(used[b], i * 16)
                dve.sem_inc(passed_v, 1)
                nc.vector.tensor_copy(to[:, 0:n], TOKEN[:, ds(i * 4, n)]).then_inc(signal, 1)

            def finish(i, b, first):
                k = i * 4 + b
                dve.wait_ge(y_made, k + 1)
                if not first:
                    dve.wait_ge(done, k - 3)
                nc.vector.tensor_tensor(TMP[:, b, :], PY[:, b % 2, 0:D], m.rows[:, 3, :], ALU.add).then_inc(y_taken, 1)
                dve.wait_ge(y_taken, k + 1)
                dve.wait_ge(b_in[b], (i + 1) * 16)
                if not first:
                    dve.wait_ge(out_done[b], i * 16)
                nc.vector.scalar_tensor_tensor(out=RES[:, b, :], in0=TMP[:, b, :], scalar=FOUND[:, 1, ds(k, 1)],
                                               in1=BG[:, b, :], op0=ALU.mult, op1=ALU.add).then_inc(done, 1)

            def group(i, n, following, first):
                if following:
                    index(IX, i + 1, following, ix, x_in)
                    index(IB, i + 1, following, ib, b_in)
                index(IS, i, n, iz, None if first else out_done)
                for b in range(n):
                    finish(i, b, first)
            index(IX, 0, 4, ix, None)
            index(IB, 0, 4, ib, None)
            group(0, 4, 4, True)
            with dve.Fori(1, groups - 1) as i:
                group(i, 4, 4, False)
            group(groups - 1, 4, rest, False)
            group(groups, rest, 0, False)


def build_program(nc, a):
    m = Mem()
    with ExitStack() as ctx:
        sb = lambda n, shape, dt=F32: ctx.enter_context(nc.sbuf_tensor(n, shape, dt))
        region = 2 * CLEN + 8
        m.R1 = sb("region1", [P, region])
        m.R2 = sb("region2", [P, region])
        m.EX = sb("edge_values", [P, STEPS * HEADS])
        m.slots = sb("slots", [P, GROUP * D])
        m.WP = sb("w_project", [P, 2, 6 * D])
        m.Wo, m.Wout, m.Wmix = sb("w_o", [P, 2, D]), sb("w_out", [P, 2, D]), sb("w_mix", [P, 2, D])
        m.rows = sb("row_vectors", [P, 5, D])
        m.REL, m.SRC = sb("relative", [P, STEPS]), sb("source", [P, STEPS], I32)
        m.IDX = sb("index", [P, GROUP], I32)
        m.BT = sb("block_table", [1, STEPS], I32)
        m.ident, m.ones, m.upper = sb("ident", [P, P]), sb("ones", [P, P]), sb("upper", [P, P])
        m.iota_row, m.iota_col = sb("iota_row", [P, P]), sb("iota_col", [P, 1])
        m.bnst, m.stat, m.rstd = sb("bn", [P, NB, 6]), sb("stat", [P, NB, 2]), sb("rstd", [P, NB])
        m.eps, m.brc, m.b1c = sb("eps", [P, 1]), sb("brc", [P, 1]), sb("b1c", [P, 8])
        m.weight = sb("weight", [P, NB])
        m.TOPB = sb("mix_k_top", [P, D])
        dram = lambda n, shape, dt=F32: nc.dram_tensor(n, shape, dt, kind="Internal").ap()
        m.dst_rows, m.src_rows = dram("dst_rows", [TILES, P], I32), dram("src_rows", [TILES, P], I32)
        m.rel_rows, m.key_rows = dram("rel_rows", [STEPS, P]), dram("key_rows", [STEPS, P])
        m.step_block = dram("step_block", [STEPS], I32)
        m.k_d, m.v_d, m.mk_d, m.xn_d, m.xt_d, m.qs_d, m.z_d, m.xn2_d = (dram(n, [NB * P, D]) for n in (
            "k_rows", "v_rows", "mix_k_rows", "xn_rows", "xn_turned", "mix_q_rows", "mix_out_rows", "xn2_rows"))
        m.score_d, m.ex_d = dram("scores", [HEADS, STEPS * P]), dram("weights", [HEADS, STEPS * P])
        m.end_d = dram("piece_ends", [P, 4])
        for phase in (setup_phase, projection_phase, score_phase, softmax_phase,
                      aggregate_phase, output_phase, feed_forward_phase):
            used = []
            m.sem = lambda name: used.append(nc.alloc_semaphore(name)) or used[-1]
            phase(nc, m, a)
            nc.clear_and_free_semaphores(used)
            nc.all_engine_barrier()


_INS = ["x", "src", "dst", "L0_gnn_Wq", "L0_gnn_Wk", "L0_gnn_Wv", "L0_gnn_Wo", "L0_gnn_gamma", "L0_gnn_beta",
        "L0_mix_Wqkv", "L0_mix_Wout", "L0_mix_gamma", "L0_ffn_attention_mask", "L0_ffn_wr", "L0_ffn_br",
        "L0_ffn_w1", "L0_ffn_b1", "L0_ffn_w2", "L0_ffn_b2"]


def kernel(**inputs):
    import concourse.bacc as bacc
    from concourse.bass_utils import run_bass_kernel_spmd

    nc = bacc.Bacc("TRN2", target_bir_lowering=False, num_devices=1)
    arrays, a = {}, Mem()
    for name in _INS:
        v = np.ascontiguousarray(inputs[name])
        arrays[f"in_{name}"] = v
        a.__dict__[name] = nc.dram_tensor(f"in_{name}", v.shape, mybir.dt.from_np(v.dtype), kind="ExternalInput").ap()
    a.out = nc.dram_tensor("out", (N, D), F32, kind="ExternalOutput").ap()
    build_program(nc, a)
    r = run_bass_kernel_spmd(nc, [arrays], core_ids=[0])
    return r.results[0]["out"]
```
